# Optimizing a Trainium2 kernel written in Bass

```python
import numpy as np
import jax
import jax.numpy as jnp

def _softmax(x, axis=-1):
    return jax.nn.softmax(x, axis=axis)
def _gelu(x):
    return jax.nn.gelu(x, approximate=True)
def _silu(x):
    return jax.nn.silu(x)
def _sigmoid(x):
    return jax.nn.sigmoid(x)
def _layernorm(x, axis=-1, eps=1e-5):
    m = jnp.mean(x, axis=axis, keepdims=True)
    v = jnp.var(x, axis=axis, keepdims=True)
    return (x - m) / jnp.sqrt(v + eps)
def _scatter_add(tgt, idx, src, axis=0):
    return tgt.at[idx].add(src)
def _segment_sum(src, seg, n):
    return jax.ops.segment_sum(src, seg, n)

kernel_name = 'mk_conv_preact_d4_conv_nhwc384_ff8dcc'

def setup_inputs(seed: int = 0):
    np.random.seed(seed)
    _w = jnp.asarray
    def _rec_inputs():
        import jax
        import jax.numpy as jnp
        _gk = jax.random.key(seed)
        x = -0.0008768 + 1.001 * jax.random.normal(jax.random.fold_in(_gk, 1), (2, 48, 48, 384), jnp.float32)
        return x
    x = _rec_inputs()
    def _L0_conv_setup():
        import jax, jax.numpy as jnp
        import numpy as np
        from jax import lax
        B_SZ, H_SZ, W_SZ = (2, 48, 48)
        D_MODEL = 192
        SSM_RATIO = 2.0
        D_PROJ = int(SSM_RATIO * D_MODEL)
        C_INNER = 2 * D_PROJ
        K_GRP = 4
        D_IN = C_INNER // K_GRP
        N_STATE = 16
        R_RANK = 12

        def _ss2d(x, in_proj_w, conv_w, conv_b, x_proj_weight, dt_projs_weight, dt_projs_bias, A_logs, Ds, out_norm_w, out_norm_b, out_proj_w):
            B, H, W, _ = x.shape
            C = in_proj_w.shape[0]
            K = x_proj_weight.shape[0]
            d = C // K
            N = A_logs.shape[1]
            R = dt_projs_weight.shape[2]
            L = H * W
            xz = jnp.einsum('bhwc,oc->bhwo', x, in_proj_w)
            xc = xz.transpose(0, 3, 1, 2)
            xc = lax.conv_general_dilated(xc, conv_w, (1, 1), 'SAME', feature_group_count=C)
            xc = xc + conv_b[None, :, None, None]
            xc = xc * jax.nn.sigmoid(xc)
            ch = xc.reshape(B, K, d, H, W)
            f0 = ch[:, 0].reshape(B, d, L)
            f1 = ch[:, 1].transpose(0, 1, 3, 2).reshape(B, d, L)
            f2 = jnp.flip(ch[:, 2].reshape(B, d, L), -1)
            f3 = jnp.flip(ch[:, 3].transpose(0, 1, 3, 2).reshape(B, d, L), -1)
            xs = jnp.stack([f0, f1, f2, f3], axis=1)
            x_dbl = jnp.einsum('bkdl,kcd->bkcl', xs, x_proj_weight)
            dts, Bs, Cs = jnp.split(x_dbl, [R, R + N], axis=2)
            dts = jnp.einsum('bkrl,kdr->bkdl', dts, dt_projs_weight) + dt_projs_bias[None, :, :, None]
            u = xs.astype(jnp.float32)
            dts = jax.nn.softplus(dts.astype(jnp.float32))
            Bs = Bs.astype(jnp.float32)
            Cs = Cs.astype(jnp.float32)
            A = -jnp.exp(A_logs.astype(jnp.float32)).reshape(K, d, N)

            def step(h, inp):
                u_t, dt_t, B_t, C_t = inp
                h = h * jnp.exp(dt_t[..., None] * A) + (dt_t * u_t)[..., None] * B_t[:, :, None, :]
                y_t = jnp.einsum('bkdn,bkn->bkd', h, C_t)
                return (h, y_t)
            inps = (u.transpose(3, 0, 1, 2), dts.transpose(3, 0, 1, 2), Bs.transpose(3, 0, 1, 2), Cs.transpose(3, 0, 1, 2))
            h0 = jnp.zeros((B, K, d, N), jnp.float32)
            _, ys = lax.scan(step, h0, inps)
            ys = ys.transpose(1, 2, 3, 0)
            ys = ys + Ds.astype(jnp.float32).reshape(K, d)[None, :, :, None] * u
            y0 = ys[:, 0]
            y1 = ys[:, 1].reshape(B, d, W, H).transpose(0, 1, 3, 2).reshape(B, d, L)
            y2 = jnp.flip(ys[:, 2], -1)
            y3 = jnp.flip(ys[:, 3], -1).reshape(B, d, W, H).transpose(0, 1, 3, 2).reshape(B, d, L)
            y = jnp.concatenate([y0, y1, y2, y3], axis=1).reshape(B, C, H, W).transpose(0, 2, 3, 1)
            mu = jnp.mean(y, -1, keepdims=True)
            var = jnp.mean(jnp.square(y - mu), -1, keepdims=True)
            y = (y - mu) * lax.rsqrt(var + 1e-05) * out_norm_w + out_norm_b
            out = jnp.einsum('bhwc,oc->bhwo', y.astype(x.dtype), out_proj_w)
            return out
        key = jax.random.key(seed)
        ks = jax.random.split(key, 12)
        x = jax.random.normal(ks[0], (B_SZ, H_SZ, W_SZ, 2 * D_MODEL), jnp.float32)
        in_proj_w = jax.random.normal(ks[1], (C_INNER, 2 * D_MODEL), jnp.float32) * 0.02
        conv_w = jax.random.normal(ks[2], (C_INNER, 1, 3, 3), jnp.float32) * 0.1
        conv_b = jnp.zeros((C_INNER,), jnp.float32)
        x_proj_weight = jax.random.normal(ks[3], (K_GRP, R_RANK + 2 * N_STATE, D_IN), jnp.float32) * 0.05
        dt_projs_weight = jax.random.normal(ks[4], (K_GRP, D_IN, R_RANK), jnp.float32) * R_RANK ** (-0.5)
        dt = jnp.exp(jax.random.uniform(ks[5], (K_GRP, D_IN)) * (np.log(0.1) - np.log(0.001)) + np.log(0.001))
        dt = jnp.clip(dt, 0.0001, None)
        dt_projs_bias = dt + jnp.log(-jnp.expm1(-dt))
        A_logs = jnp.log(jnp.tile(jnp.arange(1, N_STATE + 1, dtype=jnp.float32)[None, :], (K_GRP * D_IN, 1)))
        Ds = jnp.ones((K_GRP * D_IN,), jnp.float32)
        out_norm_w = jnp.ones((C_INNER,), jnp.float32)
        out_norm_b = jnp.zeros((C_INNER,), jnp.float32)
        out_proj_w = jax.random.normal(ks[6], (2 * D_MODEL, C_INNER), jnp.float32) * 0.02
        return dict(x=x, in_proj_w=in_proj_w, conv_w=conv_w, conv_b=conv_b, x_proj_weight=x_proj_weight, dt_projs_weight=dt_projs_weight, dt_projs_bias=dt_projs_bias, A_logs=A_logs, Ds=Ds, out_norm_w=out_norm_w, out_norm_b=out_norm_b, out_proj_w=out_proj_w)
    _L0_conv_all = _L0_conv_setup()
    _L0_conv_in = {k: v for k, v in _L0_conv_all.items() if k in ('in_proj_w', 'conv_w', 'conv_b', 'x_proj_weight', 'dt_projs_weight', 'dt_projs_bias', 'A_logs', 'Ds', 'out_norm_w', 'out_norm_b', 'out_proj_w', )}
    del _L0_conv_all

    def _L1_conv_setup():
        import jax, jax.numpy as jnp
        import numpy as np
        B, H, W, DIM = (8, 32, 32, 384)
        HEAD_DIM = 32
        NUM_HEADS = DIM // HEAD_DIM
        ATTN_DIM = NUM_HEADS * HEAD_DIM
        GP_NUM = 20
        key = jax.random.key(seed)
        k1, k2, k3, k4 = jax.random.split(key, 4)
        x = jax.random.normal(k1, (B, H, W, DIM), dtype=jnp.float32)
        W_qkv = jax.random.normal(k2, (DIM, 3 * ATTN_DIM), dtype=jnp.float32) * DIM ** (-0.5)
        gp_w = jax.random.normal(k3, (GP_NUM, DIM), dtype=jnp.float32) * DIM ** (-0.5)
        t_param = jnp.ones((1,), dtype=jnp.float32)
        W_proj = jax.random.normal(k4, (ATTN_DIM, DIM), dtype=jnp.float32) * ATTN_DIM ** (-0.5)
        return {'x': x, 'W_qkv': W_qkv, 'gp_w': gp_w, 't_param': t_param, 'W_proj': W_proj}
    _L1_conv_all = _L1_conv_setup()
    _L1_conv_in = {k: v for k, v in _L1_conv_all.items() if k in ('W_qkv', 'gp_w', 't_param', 'W_proj', )}
    del _L1_conv_all

    def _L2_conv_setup():
        import jax, jax.numpy as jnp
        import numpy as np
        WINDOW = (1, 5, 20)
        FILL = 1.0

        def box_sum(x, axis, w):
            if w == 1:
                return x
            lo = w // 2
            hi = w - lo - 1
            xm = jnp.moveaxis(x, axis, -1)
            shp = xm.shape
            xr = xm.reshape(-1, 1, shp[-1])
            k = jnp.ones((1, 1, w), x.dtype)
            y = jax.lax.conv_general_dilated(xr, k, window_strides=(1,), padding=[(lo, hi)])
            return jnp.moveaxis(y.reshape(shp), -1, axis)
        key = jax.random.key(seed)
        x = jax.random.normal(key, (2, 256, 256, 384), dtype=jnp.float32)
        return {'x': x}
    _L2_conv_all = _L2_conv_setup()
    _L2_conv_in = {k: v for k, v in _L2_conv_all.items() if k in ()}
    del _L2_conv_all

    def _L3_conv_setup():
        import jax, jax.numpy as jnp
        import numpy as np
        B, H, W, C = (8, 32, 32, 384)
        NH, HD = (6, 64)
        SCALE = HD ** (-0.5)

        def _get_rel_pos(rel_pos, q_size, k_size):
            coords = jnp.arange(q_size)[:, None] - jnp.arange(k_size)[None, :] + (k_size - 1)
            return rel_pos[coords]
        key = jax.random.key(seed)
        ks = jax.random.split(key, 7)
        return {'x': jax.random.normal(ks[0], (B, H, W, C), jnp.float32), 'qkv_w': jax.random.normal(ks[1], (C, 3 * C), jnp.float32) * 0.02, 'qkv_b': jax.random.normal(ks[2], (3 * C,), jnp.float32) * 0.02, 'proj_w': jax.random.normal(ks[3], (C, C), jnp.float32) * 0.02, 'proj_b': jax.random.normal(ks[4], (C,), jnp.float32) * 0.02, 'rel_pos_h': jax.random.normal(ks[5], (2 * H - 1, HD), jnp.float32) * 0.02, 'rel_pos_w': jax.random.normal(ks[6], (2 * W - 1, HD), jnp.float32) * 0.02}
    _L3_conv_all = _L3_conv_setup()
    _L3_conv_in = {k: v for k, v in _L3_conv_all.items() if k in ('qkv_w', 'qkv_b', 'proj_w', 'proj_b', 'rel_pos_h', 'rel_pos_w', )}
    del _L3_conv_all

    return {
        "x": x,
        "L0_conv_in_proj_w": _L0_conv_in["in_proj_w"],
        "L0_conv_conv_w": _L0_conv_in["conv_w"],
        "L0_conv_conv_b": _L0_conv_in["conv_b"],
        "L0_conv_x_proj_weight": _L0_conv_in["x_proj_weight"],
        "L0_conv_dt_projs_weight": _L0_conv_in["dt_projs_weight"],
        "L0_conv_dt_projs_bias": _L0_conv_in["dt_projs_bias"],
        "L0_conv_A_logs": _L0_conv_in["A_logs"],
        "L0_conv_Ds": _L0_conv_in["Ds"],
        "L0_conv_out_norm_w": _L0_conv_in["out_norm_w"],
        "L0_conv_out_norm_b": _L0_conv_in["out_norm_b"],
        "L0_conv_out_proj_w": _L0_conv_in["out_proj_w"],
        "L1_conv_W_qkv": _L1_conv_in["W_qkv"],
        "L1_conv_gp_w": _L1_conv_in["gp_w"],
        "L1_conv_t_param": _L1_conv_in["t_param"],
        "L1_conv_W_proj": _L1_conv_in["W_proj"],
        "L3_conv_qkv_w": _L3_conv_in["qkv_w"],
        "L3_conv_qkv_b": _L3_conv_in["qkv_b"],
        "L3_conv_proj_w": _L3_conv_in["proj_w"],
        "L3_conv_proj_b": _L3_conv_in["proj_b"],
        "L3_conv_rel_pos_h": _L3_conv_in["rel_pos_h"],
        "L3_conv_rel_pos_w": _L3_conv_in["rel_pos_w"],
    }

def reference(x, L0_conv_in_proj_w, L0_conv_conv_w, L0_conv_conv_b, L0_conv_x_proj_weight, L0_conv_dt_projs_weight, L0_conv_dt_projs_bias, L0_conv_A_logs, L0_conv_Ds, L0_conv_out_norm_w, L0_conv_out_norm_b, L0_conv_out_proj_w, L1_conv_W_qkv, L1_conv_gp_w, L1_conv_t_param, L1_conv_W_proj, L3_conv_qkv_w, L3_conv_qkv_b, L3_conv_proj_w, L3_conv_proj_b, L3_conv_rel_pos_h, L3_conv_rel_pos_w):
    import jax
    import jax.numpy as jnp
    def _L0_conv_ref(x, in_proj_w, conv_w, conv_b, x_proj_weight, dt_projs_weight, dt_projs_bias, A_logs, Ds, out_norm_w, out_norm_b, out_proj_w):
        import jax, jax.numpy as jnp
        import numpy as np
        from jax import lax
        B_SZ, H_SZ, W_SZ = (2, 48, 48)
        D_MODEL = 192
        SSM_RATIO = 2.0
        D_PROJ = int(SSM_RATIO * D_MODEL)
        C_INNER = 2 * D_PROJ
        K_GRP = 4
        D_IN = C_INNER // K_GRP
        N_STATE = 16
        R_RANK = 12

        def _ss2d(x, in_proj_w, conv_w, conv_b, x_proj_weight, dt_projs_weight, dt_projs_bias, A_logs, Ds, out_norm_w, out_norm_b, out_proj_w):
            B, H, W, _ = x.shape
            C = in_proj_w.shape[0]
            K = x_proj_weight.shape[0]
            d = C // K
            N = A_logs.shape[1]
            R = dt_projs_weight.shape[2]
            L = H * W
            xz = jnp.einsum('bhwc,oc->bhwo', x, in_proj_w)
            xc = xz.transpose(0, 3, 1, 2)
            xc = lax.conv_general_dilated(xc, conv_w, (1, 1), 'SAME', feature_group_count=C)
            xc = xc + conv_b[None, :, None, None]
            xc = xc * jax.nn.sigmoid(xc)
            ch = xc.reshape(B, K, d, H, W)
            f0 = ch[:, 0].reshape(B, d, L)
            f1 = ch[:, 1].transpose(0, 1, 3, 2).reshape(B, d, L)
            f2 = jnp.flip(ch[:, 2].reshape(B, d, L), -1)
            f3 = jnp.flip(ch[:, 3].transpose(0, 1, 3, 2).reshape(B, d, L), -1)
            xs = jnp.stack([f0, f1, f2, f3], axis=1)
            x_dbl = jnp.einsum('bkdl,kcd->bkcl', xs, x_proj_weight)
            dts, Bs, Cs = jnp.split(x_dbl, [R, R + N], axis=2)
            dts = jnp.einsum('bkrl,kdr->bkdl', dts, dt_projs_weight) + dt_projs_bias[None, :, :, None]
            u = xs.astype(jnp.float32)
            dts = jax.nn.softplus(dts.astype(jnp.float32))
            Bs = Bs.astype(jnp.float32)
            Cs = Cs.astype(jnp.float32)
            A = -jnp.exp(A_logs.astype(jnp.float32)).reshape(K, d, N)

            def step(h, inp):
                u_t, dt_t, B_t, C_t = inp
                h = h * jnp.exp(dt_t[..., None] * A) + (dt_t * u_t)[..., None] * B_t[:, :, None, :]
                y_t = jnp.einsum('bkdn,bkn->bkd', h, C_t)
                return (h, y_t)
            inps = (u.transpose(3, 0, 1, 2), dts.transpose(3, 0, 1, 2), Bs.transpose(3, 0, 1, 2), Cs.transpose(3, 0, 1, 2))
            h0 = jnp.zeros((B, K, d, N), jnp.float32)
            _, ys = lax.scan(step, h0, inps)
            ys = ys.transpose(1, 2, 3, 0)
            ys = ys + Ds.astype(jnp.float32).reshape(K, d)[None, :, :, None] * u
            y0 = ys[:, 0]
            y1 = ys[:, 1].reshape(B, d, W, H).transpose(0, 1, 3, 2).reshape(B, d, L)
            y2 = jnp.flip(ys[:, 2], -1)
            y3 = jnp.flip(ys[:, 3], -1).reshape(B, d, W, H).transpose(0, 1, 3, 2).reshape(B, d, L)
            y = jnp.concatenate([y0, y1, y2, y3], axis=1).reshape(B, C, H, W).transpose(0, 2, 3, 1)
            mu = jnp.mean(y, -1, keepdims=True)
            var = jnp.mean(jnp.square(y - mu), -1, keepdims=True)
            y = (y - mu) * lax.rsqrt(var + 1e-05) * out_norm_w + out_norm_b
            out = jnp.einsum('bhwc,oc->bhwo', y.astype(x.dtype), out_proj_w)
            return out
        return _ss2d(x, in_proj_w, conv_w, conv_b, x_proj_weight, dt_projs_weight, dt_projs_bias, A_logs, Ds, out_norm_w, out_norm_b, out_proj_w)

    def _L1_conv_ref(x, W_qkv, gp_w, t_param, W_proj):
        import jax, jax.numpy as jnp
        import numpy as np
        B, H, W, DIM = (8, 32, 32, 384)
        HEAD_DIM = 32
        NUM_HEADS = DIM // HEAD_DIM
        ATTN_DIM = NUM_HEADS * HEAD_DIM
        GP_NUM = 20
        b, h, w, c = x.shape
        n = h * w
        scale = HEAD_DIM ** (-0.5)
        qkv = x.reshape(b, n, c) @ W_qkv
        q, k, v = jnp.split(qkv, 3, axis=-1)
        q = q.reshape(b, n, NUM_HEADS, HEAD_DIM).transpose(0, 2, 1, 3)
        k = k.reshape(b, n, NUM_HEADS, HEAD_DIM).transpose(0, 2, 1, 3)
        v = v.reshape(b, n, NUM_HEADS, HEAD_DIM).transpose(0, 2, 1, 3)
        attn = jax.nn.softmax(jnp.einsum('bhnd,bhmd->bhnm', q, k) * scale, axis=-1)
        gp = gp_w.reshape(NUM_HEADS, GP_NUM, HEAD_DIM)
        t = jax.nn.softplus(t_param)[0]
        gw = jax.nn.softmax(jnp.einsum('bhnd,hmd->bhnm', q, gp) / t, axis=-1)
        group_weight = jnp.einsum('bhnm,bhkm->bhnk', gw, gw)
        attn = attn * group_weight
        attn = attn / (attn.sum(axis=2, keepdims=True) + 1e-08)
        out = jnp.einsum('bhnm,bhmd->bhnd', attn, v)
        out = out.transpose(0, 2, 1, 3).reshape(b, h, w, ATTN_DIM)
        return out @ W_proj

    def _L2_conv_ref(x):
        import jax, jax.numpy as jnp
        import numpy as np
        WINDOW = (1, 5, 20)
        FILL = 1.0

        def box_sum(x, axis, w):
            if w == 1:
                return x
            lo = w // 2
            hi = w - lo - 1
            xm = jnp.moveaxis(x, axis, -1)
            shp = xm.shape
            xr = xm.reshape(-1, 1, shp[-1])
            k = jnp.ones((1, 1, w), x.dtype)
            y = jax.lax.conv_general_dilated(xr, k, window_strides=(1,), padding=[(lo, hi)])
            return jnp.moveaxis(y.reshape(shp), -1, axis)
        w0, w1, w2 = WINDOW
        s = box_sum(box_sum(x, 1, w0), 2, w1)
        num = box_sum(s * s, 3, w2)
        d = box_sum(box_sum(box_sum(x * x, 1, w0), 2, w1), 3, w2)
        c0 = box_sum(jnp.ones((x.shape[1],), x.dtype), 0, w0)
        c1 = box_sum(jnp.ones((x.shape[2],), x.dtype), 0, w1)
        norm = c0[:, None] * c1[None, :]
        denum = d * norm[None, :, :, None]
        return jnp.nan_to_num(num / denum, nan=FILL)

    def _L3_conv_ref(x, qkv_w, qkv_b, proj_w, proj_b, rel_pos_h, rel_pos_w):
        import jax, jax.numpy as jnp
        import numpy as np
        B, H, W, C = (8, 32, 32, 384)
        NH, HD = (6, 64)
        SCALE = HD ** (-0.5)

        def _get_rel_pos(rel_pos, q_size, k_size):
            coords = jnp.arange(q_size)[:, None] - jnp.arange(k_size)[None, :] + (k_size - 1)
            return rel_pos[coords]
        b, h, w, c = x.shape
        hw = h * w
        qkv = x.reshape(b, hw, c) @ qkv_w + qkv_b
        qkv = qkv.reshape(b, hw, 3, NH, HD).transpose(2, 0, 3, 1, 4)
        qkv = qkv.reshape(3, b * NH, hw, HD)
        q, k, v = (qkv[0], qkv[1], qkv[2])
        attn = jnp.einsum('bqd,bkd->bqk', q * SCALE, k)
        Rh = _get_rel_pos(rel_pos_h, h, h)
        Rw = _get_rel_pos(rel_pos_w, w, w)
        r_q = q.reshape(b * NH, h, w, HD)
        rel_h = jnp.einsum('bhwc,hkc->bhwk', r_q, Rh)
        rel_w = jnp.einsum('bhwc,wkc->bhwk', r_q, Rw)
        attn = attn.reshape(b * NH, h, w, h, w) + rel_h[:, :, :, :, None] + rel_w[:, :, :, None, :]
        attn = attn.reshape(b * NH, hw, hw)
        attn = jax.nn.softmax(attn, axis=-1)
        out = jnp.einsum('bqk,bkd->bqd', attn, v)
        out = out.reshape(b, NH, h, w, HD).transpose(0, 2, 3, 1, 4).reshape(b, h, w, c)
        return out @ proj_w + proj_b

    def _gn(v, G=32, eps=1e-5):
        B_, H_, W_, C_ = v.shape
        g = v.reshape(B_, H_, W_, G, C_ // G)
        m = jnp.mean(g, axis=(1, 2, 4), keepdims=True)
        s = jnp.var(g, axis=(1, 2, 4), keepdims=True)
        return ((g - m) / jnp.sqrt(s + eps)).reshape(v.shape)

    def _ln_c(v, eps=1e-6):
        m = jnp.mean(v, axis=-1, keepdims=True)
        s = jnp.var(v, axis=-1, keepdims=True)
        return (v - m) / jnp.sqrt(s + eps)

    def _ln_t(v, eps=1e-5):
        m = jnp.mean(v, axis=-1, keepdims=True)
        s = jnp.var(v, axis=-1, keepdims=True)
        return (v - m) / jnp.sqrt(s + eps)

    def _to_tokens(v):
        B_, H_, W_, C_ = v.shape
        return v.reshape(B_, H_ * W_, C_)
    def _from_tokens(t, like):
        return t.reshape(like.shape)

    x = x + _L0_conv_ref(_gn(x), L0_conv_in_proj_w, L0_conv_conv_w, L0_conv_conv_b, L0_conv_x_proj_weight, L0_conv_dt_projs_weight, L0_conv_dt_projs_bias, L0_conv_A_logs, L0_conv_Ds, L0_conv_out_norm_w, L0_conv_out_norm_b, L0_conv_out_proj_w)
    x = x + _L1_conv_ref(_gn(x), L1_conv_W_qkv, L1_conv_gp_w, L1_conv_t_param, L1_conv_W_proj)
    x = x + _L2_conv_ref(_gn(x))
    x = x + _L3_conv_ref(_gn(x), L3_conv_qkv_w, L3_conv_qkv_b, L3_conv_proj_w, L3_conv_proj_b, L3_conv_rel_pos_h, L3_conv_rel_pos_w)
    return x


_drawn_inputs = setup_inputs


def setup_inputs(seed=0):
    import zlib

    import numpy as np

    out = dict(_drawn_inputs(seed))
    spreads = {'L0_conv_conv_b': (0.0, 0.1),
     'L0_conv_Ds': (1.0, 0.2),
     'L0_conv_out_norm_w': (1.0, 0.2),
     'L0_conv_out_norm_b': (0.0, 0.1)}
    factors = {'L0_conv_x_proj_weight': 8.0,
     'L0_conv_dt_projs_weight': 8.0,
     'L0_conv_dt_projs_bias': 8.0,
     'L0_conv_A_logs': 8.0,
     'L1_conv_gp_w': 8.0,
     'L3_conv_qkv_b': 8.0,
     'L3_conv_proj_b': 3.535,
     'L3_conv_rel_pos_h': 64.0,
     'L3_conv_rel_pos_w': 64.0}
    for name, (base, spread) in spreads.items():
        noise = np.random.default_rng([zlib.crc32(name.encode()), seed]).standard_normal(out[name].shape)
        drawn = base * np.exp(spread * noise) if base else spread * noise
        out[name] = jnp.asarray(drawn.astype(out[name].dtype))
    for name, factor in factors.items():
        out[name] = (out[name] * factor).astype(out[name].dtype)
    return out
```

```python
import concourse.bass as bass
from concourse import mybir
from contextlib import ExitStack

F32 = mybir.dt.float32
BF16 = mybir.dt.bfloat16
ALU = mybir.AluOpType
ACT = mybir.ActivationFunctionType
AX = mybir.AxisListType

B, H, W, C = 2, 48, 48, 384
L = H * W
T = B * L
CT = C // 128
GN_GROUP = C // 32
CI = 2 * C
K = 4
D_IN = CI // K
NS = 16
R = 12
KINDS = 3
LEFT = D_IN - 128
NH1, D1, GP = 12, 32, 20
NH3, D3 = 6, 64
QT = L // 128


class Phase:

    def __init__(self, nc, name):
        self.nc, self.name, self.stack, self.sems = nc, name, ExitStack(), []

    def __enter__(self):
        self.stack.__enter__()
        return self

    def sb(self, name, shape, dt=F32):
        return self.stack.enter_context(self.nc.sbuf_tensor(f"{self.name}_{name}", shape, dt))

    def psum(self, name, shape, dt=F32):
        return self.stack.enter_context(self.nc.psum_tensor(f"{self.name}_{name}", shape, dt))

    def sem(self, name):
        s = self.nc.alloc_semaphore(f"{self.name}_{name}")
        self.sems.append(s)
        return s

    def __exit__(self, *a):
        self.stack.__exit__(*a)
        if a[0] is None:
            self.nc.clear_and_free_semaphores(self.sems)
            self.nc.all_engine_barrier()


def cols(ap, width):
    return ap.rearrange("p (n w) -> p n w", w=width)


def spans(total, width):
    return [(s, min(width, total - s)) for s in range(0, total, width)]


def to_channels(nc, x, xc, ident):
    with Phase(nc, "tc") as ph:
        tok = ph.sb("tok", [128, 2, C])
        idn = ph.sb("idn", [128, 128])
        xcm = ph.sb("xcm", [128, CT, T])
        ps = [ph.psum(f"ps{r}", [128, CT, 128]) for r in range(2)]
        s_idn, s_turned, s_copied, s_stored = (ph.sem(n) for n in ("idn", "turned", "copied", "stored"))
        s_tok = [ph.sem(f"tok{r}") for r in range(2)]
        x_v = x.rearrange("(n p) c -> n p c", p=128)
        xcm_v = xcm[:, :, :].rearrange("p t (n w) -> p t n w", w=128)
        with nc.Block() as block:

            @block.sync
            def _(sp):
                sp.dma_start(idn[:, :], ident).then_inc(s_idn, 16)
                for r in range(2):
                    sp.dma_start(tok[:, r, :], x_v[r]).then_inc(s_tok[r], 16)
                with sp.Fori(1, T // 256) as i:
                    for r in range(2):
                        sp.wait_ge(s_turned, 2 * i + r - 1)
                        sp.dma_start(tok[:, r, :], x_v[2 * i + r]).then_inc(s_tok[r], 16)
                sp.wait_ge(s_copied, T // 128)
                sp.dma_start(xc.rearrange("(t p) n -> p t n", p=128), xcm[:, :, :]).then_inc(s_stored, 16)
                sp.wait_ge(s_stored, 16)

            @block.tensor
            def _(pe):
                pe.wait_ge(s_idn, 16)

                def turn(i, r, peeled):
                    pe.wait_ge(s_tok[r], 16 * i + 16)
                    if not peeled:
                        pe.wait_ge(s_copied, 2 * i + r - 1)
                    for t in range(CT):
                        last = pe.transpose(ps[r][:, t, :], tok[:, r, t * 128:(t + 1) * 128], idn[:, :])
                    last.then_inc(s_turned, 1)

                for r in range(2):
                    turn(0, r, True)
                with pe.Fori(1, T // 256) as i:
                    for r in range(2):
                        turn(i, r, False)

            @block.vector
            def _(dve):
                with dve.Fori(0, T // 256) as i:
                    for r in range(2):
                        dve.wait_ge(s_turned, 2 * i + r + 1)
                        dve.tensor_copy(xcm_v[:, :, 2 * i + r, :], ps[r][:, :, :]).then_inc(s_copied, 1)


def to_tokens(nc, xc, out, ident):
    with Phase(nc, "tt") as ph:
        chn = ph.sb("chn", [128, 2, CT, 128])
        tok = ph.sb("tok", [128, 2, C])
        idn = ph.sb("idn", [128, 128])
        ps = [ph.psum(f"ps{r}", [128, CT, 128]) for r in range(2)]
        s_idn, s_turned, s_copied = (ph.sem(n) for n in ("idn", "turned", "copied"))
        s_chn = [ph.sem(f"chn{r}") for r in range(2)]
        s_out = [ph.sem(f"out{r}") for r in range(2)]
        xc_v = xc.rearrange("(t p) (n w) -> n p t w", p=128, w=128)
        out_v = out.rearrange("(n p) c -> n p c", p=128)
        with nc.Block() as block:

            @block.sync
            def _(sp):
                sp.dma_start(idn[:, :], ident).then_inc(s_idn, 16)
                for r in range(2):
                    sp.dma_start(chn[:, r, :, :], xc_v[r]).then_inc(s_chn[r], 16)
                with sp.Fori(1, T // 256) as i:
                    for r in range(2):
                        sp.wait_ge(s_turned, 2 * i + r - 1)
                        sp.dma_start(chn[:, r, :, :], xc_v[2 * i + r]).then_inc(s_chn[r], 16)

            @block.tensor
            def _(pe):
                pe.wait_ge(s_idn, 16)

                def turn(i, r, peeled):
                    pe.wait_ge(s_chn[r], 16 * i + 16)
                    if not peeled:
                        pe.wait_ge(s_copied, 2 * i + r - 1)
                    for t in range(CT):
                        last = pe.transpose(ps[r][:, t, :], chn[:, r, t, :], idn[:, :])
                    last.then_inc(s_turned, 1)

                for r in range(2):
                    turn(0, r, True)
                with pe.Fori(1, T // 256) as i:
                    for r in range(2):
                        turn(i, r, False)

            @block.vector
            def _(dve):
                def copy(i, r, peeled):
                    dve.wait_ge(s_turned, 2 * i + r + 1)
                    if not peeled:
                        dve.wait_ge(s_out[r], 16 * i)
                    dve.tensor_copy(tok[:, r, :], ps[r][:, :, :].rearrange("p t w -> p (t w)")).then_inc(s_copied, 1)

                for r in range(2):
                    copy(0, r, True)
                with dve.Fori(1, T // 256) as i:
                    for r in range(2):
                        copy(i, r, False)

            @block.scalar
            def _(act):
                with act.Fori(0, T // 256) as i:
                    for r in range(2):
                        act.wait_ge(s_copied, 2 * i + r + 1)
                        act.dma_start(out_v[2 * i + r], tok[:, r, :]).then_inc(s_out[r], 16)
                for r in range(2):
                    act.wait_ge(s_out[r], 16 * (T // 256))


def group_norm(nc, tag, xc, xn, gmat, eps=1e-5):
    NCH = 6
    with Phase(nc, f"gn{tag}") as ph:
        x = ph.sb("x", [128, CT, B, L])
        gm = ph.sb("gm", [128, CT, C])
        stats = ph.sb("stats", [128, CT, B, NCH, 6])
        mv = ph.sb("mv", [128, CT, B, 2])
        mean = ph.sb("mean", [128, CT, B])
        dev = ph.sb("dev", [128, CT, B])
        spread = ph.sb("spread", [128, CT, B])
        std = ph.sb("std", [128, CT, B])
        rstd = ph.sb("rstd", [128, CT, B])
        epsc = ph.sb("epsc", [128, 1])
        ps = ph.psum("ps", [128, 2, CT, B])
        s_gm, s_mv, s_mean, s_spread, s_var, s_std, s_xn, s_out, s_link = (
            ph.sem(n) for n in ("gm", "mv", "mean", "spread", "var", "std", "xn", "out", "link"))
        s_x = [ph.sem(f"x{t}") for t in range(CT)]
        xc_v = xc.rearrange("(t p) (b n) -> t p b n", p=128, b=B)
        xn_v = xn.rearrange("(t p) (b n) -> t p b n", p=128, b=B)
        with nc.Block() as block:

            @block.sync
            def _(sp):
                for t in range(CT):
                    sp.dma_start(x[:, t, :, :], xc_v[t]).then_inc(s_x[t], 16)
                sp.dma_start(gm[:, :, :], gmat.rearrange("(t p) c -> p t c", p=128)).then_inc(s_gm, 16)
                for t in range(CT):
                    sp.wait_ge(s_xn, B * (t + 1))
                    sp.dma_start(xn_v[t], x[:, t, :, :]).then_inc(s_out, 16)
                sp.wait_ge(s_out, 16 * CT)

            @block.vector
            def _(dve):
                chain = [0]

                def link(ins):
                    chain[0] += 1
                    ins.then_inc(s_link, 1)
                    dve.wait_ge(s_link, chain[0])

                dve.memset(epsc[:, :], eps)
                for t in range(CT):
                    dve.wait_ge(s_x[t], 16)
                    for b in range(B):
                        for c, (s, w) in enumerate(spans(L, L // NCH)):
                            last = dve.bn_stats(stats[:, t, b, c, :], x[:, t, b, s:s + w])
                link(last)
                for t in range(CT):
                    for b in range(B):
                        dve.bn_aggr(mv[:, t, b, :], stats[:, t, b, :, :].rearrange("p n s -> p (n s)")).then_inc(s_mv, 1)
                dve.wait_ge(s_mean, 1)
                dve.wait_ge(s_mv, CT * B)
                link(dve.tensor_copy(mean[:, :, :], ps[:, 0, :, :]))
                link(dve.tensor_tensor(dev[:, :, :], mv[:, :, :, 0], mean[:, :, :], ALU.subtract))
                link(dve.tensor_tensor(dev[:, :, :], dev[:, :, :], dev[:, :, :], ALU.mult))
                dve.tensor_tensor(spread[:, :, :], dev[:, :, :], mv[:, :, :, 1], ALU.add).then_inc(s_spread, 1)
                dve.wait_ge(s_std, 1)
                link(dve.reciprocal(rstd[:, :, :], std[:, :, :]))
                for t in range(CT):
                    for b in range(B):
                        dve.tensor_scalar(x[:, t, b, :], x[:, t, b, :], mean[:, t, b:b + 1], rstd[:, t, b:b + 1],
                                          ALU.subtract, ALU.mult).then_inc(s_xn, 1)

            @block.tensor
            def _(pe):
                pe.wait_ge(s_gm, 16)
                pe.wait_ge(s_mv, CT * B)
                for o in range(CT):
                    for t in range(CT):
                        last = pe.matmul(ps[:, 0, o, :], gm[:, t, o * 128:(o + 1) * 128], mv[:, t, :, 0],
                                         start=t == 0, stop=t == CT - 1)
                last.then_inc(s_mean, 1)
                pe.wait_ge(s_spread, 1)
                for o in range(CT):
                    for t in range(CT):
                        last = pe.matmul(ps[:, 1, o, :], gm[:, t, o * 128:(o + 1) * 128], spread[:, t, :],
                                         start=t == 0, stop=t == CT - 1)
                last.then_inc(s_var, 1)

            @block.scalar
            def _(act):
                act.wait_ge(s_var, 1)
                act.activation(std[:, :, :], ps[:, 1, :, :], ACT.Sqrt, bias=epsc[:, :]).then_inc(s_std, 1)


PH, PW = H + 2, W + 2
CH = 8 * W
NC0 = L // CH
TAPS, CONV_B, SKIP, DT_B, A_LOG = 0, 9, 10, 11, 12
NPAR = A_LOG + NS


def scan_view(ap, k):
    if k >= 2:
        ap = ap[:, ::-1]
    if k % 2:
        return ap.rearrange("p (x y) -> p y x", y=H)
    return ap.rearrange("p (y x) -> p y x", x=W)


def conv_inputs(nc, xn, w_in, params, ident, u):
    with Phase(nc, "ci") as ph:
        x = ph.sb("x", [128, CT, B, L])
        wi = ph.sb("wi", [128, K, CT, D_IN])
        par = ph.sb("par", [128, K, 2, NPAR])
        idn = ph.sb("idn", [128, 128])
        diag = ph.sb("diag", [128, 2, 9, 128])
        pad = ph.sb("pad", [128, 2, PH, PW])
        ut = ph.sb("ut", [128, 2, L])
        pi = [ph.psum(f"pi{r}", [128, CH]) for r in range(2)]
        pc = [ph.psum(f"pc{r}", [128, CH]) for r in range(2)]
        s_w, s_zero, s_in, s_pad, s_diag, s_conv, s_u, s_out0, s_out1 = (
            ph.sem(n) for n in "w zero in pad diag conv u out0 out1".split())
        s_out = [s_out0, s_out1]
        s_x = [ph.sem(f"x{t}") for t in range(CT)]
        units = [(k, kind) for k in range(K) for kind in range(KINDS)]
        with nc.Block() as block:

            @block.sync
            def _(sp):
                sp.dma_start(wi[:, :, :, :], w_in).then_inc(s_w, 16)
                sp.dma_start(par[:, :, :, :], params).then_inc(s_w, 16)
                sp.dma_start(idn[:, :], ident).then_inc(s_w, 16)
                for t in range(CT):
                    sp.dma_start(x[:, t, :, :], xn.rearrange("(t p) (b n) -> t p b n", p=128, b=B)[t])\
                      .then_inc(s_x[t], 16)
                for n, (k, kind) in enumerate(units):
                    sp.wait_ge(s_u, NC0 * (n + 1))
                    sp.dma_start(u[n], ut[:, n % 2, :]).then_inc(s_out[n % 2], 16)
                for r in range(2):
                    sp.wait_ge(s_out[r], 16 * len(units) // 2)

            @block.gpsimd
            def _(pool):
                pool.memset(pad[:, :, :, :], 0.0).then_inc(s_zero, 1)
                pool.wait_ge(s_w, 48)
                for n, (k, kind) in enumerate(units):
                    if kind == 1:
                        continue
                    g = kind // 2
                    if k:
                        pool.wait_ge(s_conv, NC0 * (KINDS * (k - 1) + (2 if g == 0 else 3)))
                    for tap in range(9):
                        pool.tensor_scalar(diag[:, g, tap, :], idn[:, :], par[:, k, g, TAPS + tap:TAPS + tap + 1],
                                           None, ALU.mult).then_inc(s_diag, 1)

            @block.tensor
            def _(pe):
                for t in range(CT):
                    pe.wait_ge(s_x[t], 16)
                pe.wait_ge(s_w, 48)

                def project(n):
                    k, kind = units[n]
                    for c in range(NC0):
                        m = NC0 * n + c
                        if m >= 2:
                            pe.wait_ge(s_pad, m - 1)
                        if kind < 2:
                            parts = [(0, 128, 0, kind)]
                        else:
                            parts = [(0, LEFT, 128, 0), (LEFT, 128, 128, 1)]
                        for lo, hi, w0, b in parts:
                            for t in range(CT):
                                last = pe.matmul(pi[m % 2][lo:hi, :], wi[:, k, t, w0:w0 + hi - lo],
                                                 x[:, t, b, c * CH:(c + 1) * CH], start=t == 0, stop=t == CT - 1,
                                                 skip_group_check=True)
                        last.then_inc(s_in, 1)

                def convolve(n):
                    k, kind = units[n]
                    g = kind // 2
                    pe.wait_ge(s_pad, NC0 * (n + 1))
                    pe.wait_ge(s_diag, 9 * (2 * k + g + 1))
                    for c in range(NC0):
                        m = NC0 * n + c
                        if m >= 2:
                            pe.wait_ge(s_u, m - 1)
                        for tap in range(9):
                            dy, dx = tap // 3, tap % 3
                            last = pe.matmul(pc[m % 2][:, :], diag[:, g, tap, :],
                                             pad[:, n % 2, 8 * c + dy:8 * c + dy + 8, dx:dx + W],
                                             start=tap == 0, stop=tap == 8)
                        last.then_inc(s_conv, 1)

                project(0)
                for n in range(len(units)):
                    if n + 1 < len(units):
                        project(n + 1)
                    convolve(n)

            @block.vector
            def _(dve):
                dve.wait_ge(s_zero, 1)
                for n in range(len(units)):
                    for c in range(NC0):
                        m = NC0 * n + c
                        if c == 0 and n >= 2:
                            dve.wait_ge(s_conv, NC0 * (n - 1))
                        dve.wait_ge(s_in, m + 1)
                        dve.tensor_copy(pad[:, n % 2, 8 * c + 1:8 * c + 9, 1:W + 1],
                                        pi[m % 2][:, :].rearrange("p (y x) -> p y x", x=W)).then_inc(s_pad, 1)

            @block.scalar
            def _(act):
                act.wait_ge(s_w, 48)
                for n, (k, kind) in enumerate(units):
                    if n >= 2:
                        act.wait_ge(s_out[n % 2], 16 * (n // 2))
                    for c in range(NC0):
                        m = NC0 * n + c
                        act.wait_ge(s_conv, m + 1)
                        act.activation(scan_view(ut[:, n % 2, :], k)[:, 8 * c:8 * c + 8, :],
                                       pc[m % 2][:, :].rearrange("p (y x) -> p y x", x=W), ACT.Silu,
                                       bias=par[:, k, kind // 2, CONV_B:CONV_B + 1]).then_inc(s_u, 1)


def selective_scan(nc, u, w_x, w_dt, params, sel, ident, y):
    NB = 2 * B * NS
    HB = NB // 2
    ND = B * R
    WC = 512
    parts = spans(L, WC)
    NP = len(parts)
    with Phase(nc, "ss") as ph:
        ut = ph.sb("ut", [128, KINDS, L])
        wx = ph.sb("wx", [128, KINDS, 96])
        wd = ph.sb("wd", [ND, KINDS, 128])
        par = ph.sb("par", [128, 2, NPAR])
        sl = ph.sb("sl", [3 * HB, KINDS * NS, 128], BF16)
        idn = ph.sb("idn", [128, 128])
        skip = ph.sb("skip", [128, 2, 128])
        a_exp = ph.sb("a_exp", [128, 2, NS])
        a_rate = ph.sb("a_rate", [128, 2, NS])
        pb, pc = ph.sb("pb", [3 * HB, L], BF16), ph.sb("pc", [3 * HB, L], BF16)
        bc = [ph.sb(f"bc{i}", [NB, L], BF16) for i in range(3)]
        rest = ph.sb("rest", [NB, 2, WC])
        dts = ph.sb("dts", [ND, L])
        dt = ph.sb("dt", [128, L])
        du = ph.sb("du", [128, L])
        decay, drive, state, cb, read = ([ph.sb(f"{n}{r}", [128, L]) for r in range(2)]
                                         for n in ("decay", "drive", "state", "cb", "read"))
        yt = ph.sb("yt", [128, L])
        ps = ph.psum("ps", [128, 8, WC])
        (s_const, s_in, s_rate, s_skip, s_xd, s_b0, s_dts, s_rest, s_b1, s_b2, s_bc, s_dtp, s_a, s_v, s_dt,
         s_psb, s_drive, s_decay, s_state, s_psc, s_cb, s_read, s_psy, s_mark, s_y, s_ytfree, s_out, s_tile) = (
             ph.sem(n) for n in (
                 "const in rate skip xdbl bc0 dts rest bc1 bc2 bc dtproj actstep vecstep dt "
                 "psb drive decay state psc cb read psy mark y ytfree out tile").split())
        y_ps = ps[:, 0:NP, :].rearrange("p a b -> p (a b)")[:, 0:L]
        raw, e, log, series = state[0], decay[0], decay[1], drive[0]
        small = read[1][:, :].bitcast(mybir.dt.uint32)
        STATES = NS * KINDS

        def directions(eng, body):
            with eng.Fori(0, K) as k:
                body(k)

        def states(eng, k, t, body):
            with eng.Fori(0, NS // 2) as i:
                for r in range(2):
                    body(STATES * k + 2 * i + (NS * t + r), i, r)

        with nc.Block() as block:

            @block.sync
            def _(sp):
                sp.sem_inc(s_ytfree, 1)
                sp.dma_start(idn[:, :], ident).then_inc(s_const, 16)
                sp.dma_start(sl[:, :, :], sel).then_inc(s_const, 16)

                def body(k):
                    sp.wait_ge(s_y, KINDS * k + 1)
                    sp.dma_start(wx[:, :, :], w_x[k]).then_inc(s_in, 16)
                    sp.dma_start(wd[:, :, :], w_dt[k]).then_inc(s_in, 16)
                    sp.dma_start(par[:, :, :], params[k]).then_inc(s_in, 16)
                    sp.dma_start(ut[:, :, :], u.rearrange("(k t) p n -> k p t n", t=KINDS)[k]).then_inc(s_in, 16)
                    sp.wait_ge(s_b2, NP * k + NP)
                    for i in range(3):
                        for j, dst in enumerate((pb, pc)):
                            sp.dma_start(dst[HB * i:HB * (i + 1), :], bc[i][HB * j:HB * (j + 1), :]).then_inc(s_bc, 16)
                    for t in range(KINDS):
                        sp.wait_ge(s_y, KINDS * k + (t + 2))
                        sp.dma_start(y.rearrange("(k t) p n -> k t p n", t=KINDS)[k, t], yt[:, :]).then_inc(s_out, 16)
                        sp.wait_ge(s_out, 16 * KINDS * k + (16 * t + 16))
                        sp.sem_inc(s_ytfree, 1)

                directions(sp, body)

            @block.gpsimd
            def _(pool):
                def product(n, i, r):
                    pool.wait_ge(s_state, n + 3)
                    pool.wait_ge(s_cb, NP * n + (NP + 1))
                    pool.wait_ge(s_psy, n + 1)
                    pool.tensor_tensor(read[r][:, :], state[r][:, :], cb[r][:, :], ALU.mult).then_inc(s_read, 1)

                def body(k):
                    for c, (at, w) in enumerate(parts):
                        pool.wait_ge(s_b1, NP * k + (c + 1))
                        pool.tensor_tensor(bc[2][:, at:at + w], rest[:, c % 2, 0:w], bc[1][:, at:at + w],
                                           ALU.subtract).then_inc(s_b2, 1)
                    for t in range(KINDS):
                        states(pool, k, t, product)

                pool.sem_inc(s_read, 2)
                directions(pool, body)

            @block.tensor
            def _(pe):
                pe.sem_inc(s_psy, 2)
                pe.wait_ge(s_const, 32)

                def spread(n, i, r, t, c):
                    at, w = parts[c]
                    m = NP * r + c
                    row = sl[:, NS * t:NS * (t + 1), :][:, 2 * i + r, :]
                    pe.wait_ge(s_drive, NP * n + (c + 1))
                    pe.matmul(ps[:, 5 + m % 2, 0:w], row, pb[:, at:at + w], start=True, stop=True).then_inc(s_psb, 1)
                    pe.wait_ge(s_cb, NP * n + (c + 1))
                    pe.matmul(ps[:, 7, 0:w], row, pc[:, at:at + w], start=True, stop=True).then_inc(s_psc, 1)

                def gather(n, r, c, stop=False):
                    at, w = parts[c]
                    if c == 0:
                        pe.wait_ge(s_read, n + 1)
                    last = pe.matmul(ps[:, c, 0:w], idn[:, :], read[r][:, at:at + w], start=False, stop=stop,
                                     skip_group_check=True)
                    if c == NP - 1:
                        last.then_inc(s_psy, 1)

                def body(k):
                    pe.wait_ge(s_in, 64 * k + 64)
                    pe.wait_ge(s_y, KINDS * k + 1)
                    for c, (at, w) in enumerate(parts):
                        if c >= 2:
                            pe.wait_ge(s_rest, NP * k + (c - 1))
                            pe.wait_ge(s_dts, NP * k + (c - 1))
                        for t in range(KINDS):
                            last = pe.matmul(ps[0:96, 5 + c % 2, 0:w], wx[:, t, :], ut[:, t, at:at + w],
                                             start=t == 0, stop=t == KINDS - 1)
                        last.then_inc(s_xd, 1)
                    pe.wait_ge(s_dts, NP * k + NP)
                    for t in range(KINDS):
                        pe.wait_ge(s_y, KINDS * k + (t + 1))
                        pe.sem_inc(s_tile, 1)
                        for c, (at, w) in enumerate(parts):
                            last = pe.matmul(ps[:, c, 0:w], wd[:, t, :], dts[:, at:at + w], start=True, stop=True)
                        last.then_inc(s_dtp, 1)
                        if t == 0:
                            pe.wait_ge(s_skip, 2 * k + 2)
                            pe.wait_ge(s_bc, 96 * k + 96)
                        pe.wait_ge(s_a, 4 * KINDS * k + (4 * t + 2))
                        for c, (at, w) in enumerate(parts):
                            pe.matmul(ps[:, c, 0:w], skip[:, t // 2, :], ut[:, t, at:at + w], start=True, stop=False,
                                      skip_group_check=True)
                        n0 = STATES * k + NS * t
                        for r in range(2):
                            for c in range(NP):
                                spread(n0 + r, 0, r, t, c)
                        with pe.Fori(1, NS // 2) as i:
                            for r in range(2):
                                for c in range(NP):
                                    spread(n0 + 2 * i + r, i, r, t, c)
                                    gather(n0 + 2 * i + r, r, c)
                        for r in range(2):
                            for c in range(NP):
                                gather(n0 + (NS + r), r, c, stop=r == 1)

                directions(pe, body)

            @block.scalar
            def _(act):
                act.sem_inc(s_y, 1)
                act.sem_inc(s_cb, 1)

                def body(k):
                    act.wait_ge(s_in, 64 * k + 64)
                    act.activation(a_exp[:, :, :], par[:, :, A_LOG:NPAR], ACT.Exp).then_inc(s_rate, 1)
                    act.wait_ge(s_rate, 2 * k + 1)
                    act.activation(a_rate[:, :, :], a_exp[:, :, :], ACT.Copy, scale=-1.0).then_inc(s_rate, 1)
                    for c, (at, w) in enumerate(parts):
                        bank = ps[:, 5 + c % 2, 0:w]
                        act.wait_ge(s_xd, NP * k + (c + 1))
                        act.activation(bc[0][:, at:at + w], bank[0:NB, :], ACT.Copy).then_inc(s_b0, 1)
                        act.activation(dts[:, at:at + w], bank[NB:NB + ND, :], ACT.Copy).then_inc(s_dts, 1)
                        act.wait_ge(s_rest, NP * k + (c + 1))
                        act.activation(bc[1][:, at:at + w], rest[:, c % 2, 0:w], ACT.Copy).then_inc(s_b1, 1)
                    for t in range(KINDS):
                        b_dt = par[:, t // 2, DT_B:DT_B + 1]
                        step = 4 * KINDS * k + 4 * t
                        act.wait_ge(s_dtp, KINDS * k + (t + 1))
                        act.activation(raw[:, :], y_ps, ACT.Identity, bias=b_dt).then_inc(s_a, 1)
                        act.activation(log[:, :], y_ps, ACT.Abs, bias=b_dt).then_inc(s_a, 1)
                        act.wait_ge(s_a, step + 2)
                        act.activation(e[:, :], log[:, :], ACT.Exp, scale=-1.0).then_inc(s_a, 1)
                        act.wait_ge(s_a, step + 3)
                        act.activation(log[:, :], e[:, :], ACT.Ln, bias=1.0).then_inc(s_a, 1)
                        act.wait_ge(s_rate, 2 * k + 2)
                        act.wait_ge(s_dt, 2 * KINDS * k + (2 * t + 2))

                        def state_step(n, i, r):
                            act.wait_ge(s_state, n + 1)
                            act.activation(decay[r][:, :], dt[:, :], ACT.Exp,
                                           scale=cols(a_rate[:, t // 2, :], 1)[:, 2 * i + r, :]).then_inc(s_decay, 1)
                            act.wait_ge(s_read, n + 1)
                            for c, (at, w) in enumerate(parts):
                                act.wait_ge(s_psc, NP * n + (c + 1))
                                act.activation(cb[r][:, at:at + w], ps[:, 7, 0:w], ACT.Copy).then_inc(s_cb, 1)

                        states(act, k, t, state_step)
                        act.wait_ge(s_psy, STATES * k + (NS * (t + 1) + 2))
                        act.wait_ge(s_ytfree, KINDS * k + (t + 1))
                        act.activation(yt[:, :], y_ps, ACT.Copy).then_inc(s_y, 1)

                directions(act, body)

            @block.vector
            def _(dve):
                dve.sem_inc(s_drive, 2)
                dve.sem_inc(s_state, 2)

                def body(k):
                    dve.wait_ge(s_in, 64 * k + 64)
                    for g in range(2):
                        dve.tensor_scalar(skip[:, g, :], idn[:, :], par[:, g, SKIP:SKIP + 1], None,
                                          ALU.mult).then_inc(s_skip, 1)
                    for c, (at, w) in enumerate(parts):
                        dve.wait_ge(s_b0, NP * k + (c + 1))
                        if c >= 2:
                            dve.wait_ge(s_b2, NP * k + (c - 1))
                        dve.tensor_tensor(rest[:, c % 2, 0:w], ps[0:NB, 5 + c % 2, 0:w], bc[0][:, at:at + w],
                                          ALU.subtract).then_inc(s_rest, 1)
                    for t in range(KINDS):
                        steps = [0]
                        LINKS = 6

                        def link(ins):
                            steps[0] += 1
                            ins.then_inc(s_v, 1)
                            dve.wait_ge(s_v, LINKS * KINDS * k + (LINKS * t + steps[0]))

                        dve.wait_ge(s_a, 4 * KINDS * k + (4 * t + 4))
                        link(dve.tensor_scalar(series[:, :], e[:, :], -0.25, None, ALU.mult))
                        for coefficient in (1 / 3, -1 / 2, 1.0):
                            link(dve.scalar_tensor_tensor(series[:, :], series[:, :], coefficient, e[:, :],
                                                          ALU.add, ALU.mult))
                        link(dve.tensor_scalar(small, e[:, :], 0.015625, None, ALU.is_lt))
                        dve.sem_inc(s_mark, 1)
                        link(dve.copy_predicated(log[:, :], small, series[:, :]))
                        assert steps[0] == LINKS
                        dve.scalar_tensor_tensor(dt[:, :], raw[:, :], 0.0, log[:, :], ALU.max,
                                                 ALU.add).then_inc(s_dt, 1)
                        dve.wait_ge(s_dt, 2 * KINDS * k + (2 * t + 1))
                        dve.tensor_tensor(du[:, :], dt[:, :], ut[:, t, :], ALU.mult).then_inc(s_dt, 1)
                        dve.wait_ge(s_dt, 2 * KINDS * k + (2 * t + 2))
                        dve.sem_inc(s_mark, 1)

                        def state_step(n, i, r):
                            dve.wait_ge(s_state, n + 1)
                            for c, (at, w) in enumerate(parts):
                                dve.wait_ge(s_psb, NP * n + (c + 1))
                                dve.tensor_tensor(drive[r][:, at:at + w], ps[:, 5 + (NP * r + c) % 2, 0:w],
                                                  du[:, at:at + w], ALU.mult).then_inc(s_drive, 1)
                            dve.wait_ge(s_decay, n + 1)
                            dve.wait_ge(s_drive, NP * n + (NP + 2))
                            dve.wait_ge(s_read, n + 1)
                            dve.tensor_tensor_scan(state[r][:, :], decay[r][:, :], drive[r][:, :], 0.0, ALU.mult,
                                                   ALU.add).then_inc(s_state, 1)

                        states(dve, k, t, state_step)

                directions(dve, body)


def norm_project(nc, y, norm_w, norm_b, w_out, xc, out, eps=1e-5):
    NT = CI // 128
    with Phase(nc, "np") as ph:
        raw = ph.sb("raw", [128, 2, L])
        yr = ph.sb("yr", [128, NT, L])
        wo = ph.sb("wo", [128, NT, C])
        nw = ph.sb("nw", [128, NT])
        nb = ph.sb("nb", [128, NT])
        ones = ph.sb("ones", [128, 128])
        epsc = ph.sb("epsc", [128, 1])
        sq = ph.sb("sq", [128, NT, CH])
        yc = ph.sb("yc", [128, 2, NT, CH])
        std = ph.sb("std", [128, CH])
        rstd = ph.sb("rstd", [128, CH])
        x = ph.sb("x", [128, CT, L])
        pm = ph.psum("pm", [128, CH])
        pv = ph.psum("pv", [128, CH])
        po = [ph.psum(f"po{r}", [128, CH]) for r in range(2)]
        (s_w, s_ones, s_turned, s_mean, s_yc, s_sq, s_var, s_std, s_rstd, s_scaled, s_yn, s_o, s_sum, s_out) = (
            ph.sem(n) for n in "w ones turned mean yc sq var std rstd scaled yn o sum out".split())
        s_y = [ph.sem(f"y{r}") for r in range(2)]
        s_x = ph.sem("x")
        xc_v, out_v = (z.rearrange("(t p) (b n) -> b p t n", p=128, b=B) for z in (xc, out))

        def sources(j, b):
            if j < K:
                return [(0, 128, KINDS * j + b, 0, j)]
            return [(64 * h, 64 * h + 64, KINDS * (2 * (j - K) + h) + 2, 64 * b, 2 * (j - K) + h) for h in range(2)]

        with nc.Block() as block:

            @block.sync
            def _(sp):
                sp.dma_start(wo[:, :, :], w_out).then_inc(s_w, 16)
                sp.dma_start(nw[:, :], norm_w).then_inc(s_w, 16)
                sp.dma_start(nb[:, :], norm_b).then_inc(s_w, 16)
                loads = [0, 0]
                for b in range(B):
                    if b:
                        sp.wait_ge(s_out, 16 * b)
                    sp.dma_start(x[:, :, :], xc_v[b]).then_inc(s_x, 16)
                    for j in range(NT):
                        n = NT * b + j
                        if n >= 2:
                            sp.wait_ge(s_turned, n - 1)
                        for lo, hi, tile, p0, _ in sources(j, b):
                            sp.dma_start(raw[lo:hi, n % 2, :], y[tile, p0:p0 + hi - lo, :]).then_inc(s_y[n % 2], 16)
                    sp.wait_ge(s_sum, CT * NC0 * (b + 1))
                    sp.dma_start(out_v[b], x[:, :, :]).then_inc(s_out, 16)
                sp.wait_ge(s_out, 16 * B)

            @block.gpsimd
            def _(pool):
                pool.memset(ones[:, :], 1.0 / CI).then_inc(s_ones, 1)
                pool.memset(epsc[:, :], eps).then_inc(s_ones, 1)
                for m in range(B * NC0):
                    pool.wait_ge(s_rstd, m + 1)
                    for j in range(NT):
                        pool.tensor_tensor(yc[:, m % 2, j, :], yc[:, m % 2, j, :], rstd[:, :],
                                           ALU.mult).then_inc(s_scaled, 1)

            @block.vector
            def _(dve):
                dve.wait_ge(s_w, 48)
                seen = [0, 0]

                def center(m):
                    c = m % NC0
                    dve.wait_ge(s_mean, m + 1)
                    if m >= 2:
                        dve.wait_ge(s_o, CT * (m - 1))
                    for j in range(NT):
                        dve.tensor_tensor(yc[:, m % 2, j, :], yr[:, j, c * CH:(c + 1) * CH], pm[:, :],
                                          ALU.subtract).then_inc(s_yc, 1)

                def finish(m):
                    for o in range(CT):
                        c = m % NC0
                        dve.wait_ge(s_o, CT * m + o + 1)
                        dve.tensor_tensor(x[:, o, c * CH:(c + 1) * CH], po[(CT * m + o) % 2][:, :],
                                          x[:, o, c * CH:(c + 1) * CH], ALU.add).then_inc(s_sum, 1)

                for b in range(B):
                    if b:
                        dve.wait_ge(s_mean, NC0 * b)
                    for j in range(NT):
                        n = NT * b + j
                        pieces = sources(j, b)
                        seen[n % 2] += 16 * len(pieces)
                        dve.wait_ge(s_y[n % 2], seen[n % 2])
                        for lo, hi, _, _, k in pieces:
                            last = dve.tensor_copy(yr[lo:hi, j, :].rearrange("p (y x) -> p y x", x=W),
                                                   scan_view(raw[lo:hi, n % 2, :], k))
                        last.then_inc(s_turned, 1)
                    dve.wait_ge(s_turned, NT * (b + 1))
                    dve.wait_ge(s_x, 16 * (b + 1))
                    for c in range(NC0):
                        m = NC0 * b + c
                        center(m)
                        if c:
                            finish(m - 1)
                        dve.wait_ge(s_std, m + 1)
                        if m:
                            dve.wait_ge(s_scaled, NT * m)
                        dve.reciprocal(rstd[:, :], std[:, :]).then_inc(s_rstd, 1)
                    finish(NC0 * b + NC0 - 1)

            @block.scalar
            def _(act):
                act.wait_ge(s_w, 48)
                act.wait_ge(s_ones, 2)

                def squares(m):
                    for j in range(NT):
                        act.wait_ge(s_yc, NT * m + j + 1)
                        if m:
                            act.wait_ge(s_var, m)
                        act.activation(sq[:, j, :], yc[:, m % 2, j, :], ACT.Square).then_inc(s_sq, 1)
                    act.wait_ge(s_var, m + 1)
                    if m:
                        act.wait_ge(s_rstd, m)
                    act.activation(std[:, :], pv[:, :], ACT.Sqrt, bias=epsc[:, :]).then_inc(s_std, 1)

                for m in range(B * NC0):
                    squares(m)
                    for j in range(NT):
                        act.wait_ge(s_scaled, NT * m + j + 1)
                        act.activation(yc[:, m % 2, j, :], yc[:, m % 2, j, :], ACT.Identity, scale=nw[:, j:j + 1],
                                       bias=nb[:, j:j + 1]).then_inc(s_yn, 1)

            @block.tensor
            def _(pe):
                pe.wait_ge(s_ones, 2)
                pe.wait_ge(s_w, 48)

                def outputs(m):
                    pe.wait_ge(s_yn, NT * (m + 1))
                    for o in range(CT):
                        n = CT * m + o
                        if n >= 2:
                            pe.wait_ge(s_sum, n - 1)
                        for j in range(NT):
                            last = pe.matmul(po[n % 2][:, :], wo[:, j, o * 128:(o + 1) * 128], yc[:, m % 2, j, :],
                                             start=j == 0, stop=j == NT - 1)
                        last.then_inc(s_o, 1)

                for m in range(B * NC0):
                    b, c = m // NC0, m % NC0
                    if m and c == 0:
                        outputs(m - 1)
                    pe.wait_ge(s_turned, NT * (b + 1))
                    if m:
                        pe.wait_ge(s_yc, NT * m)
                    for j in range(NT):
                        last = pe.matmul(pm[:, :], ones[:, :], yr[:, j, c * CH:(c + 1) * CH], start=j == 0,
                                         stop=j == NT - 1)
                    last.then_inc(s_mean, 1)
                    if c:
                        outputs(m - 1)
                    pe.wait_ge(s_sq, NT * (m + 1))
                    if m:
                        pe.wait_ge(s_std, m)
                    for j in range(NT):
                        last = pe.matmul(pv[:, :], ones[:, :], sq[:, j, :], start=j == 0, stop=j == NT - 1)
                    last.then_inc(s_var, 1)
                outputs(B * NC0 - 1)


WIN_W = 5
WIN_C = 20
MAX_F32 = 3.4028234663852886e38


def box_similarity(nc, xc, xn, out, band, norm):
    LO = WIN_W // 2
    WP = W + WIN_W - 1
    NCH, RW = 6, 8
    CW = RW * W
    near = [[t for t in range(CT) if abs(t - o) <= 1] for o in range(CT)]
    with Phase(nc, "box") as ph:
        xin = ph.sb("xin", [128, 2, L])
        pad = ph.sb("pad", [128, 2, H, WP])
        pad2 = ph.sb("pad2", [128, 2, H, WP])
        pair = ph.sb("pair", [128, H, WP - 1])
        pair2 = ph.sb("pair2", [128, H, WP - 1])
        s1 = ph.sb("s1", [128, H, W])
        s2 = ph.sb("s2", [128, H, W])
        num = ph.sb("num", [128, CT, L])
        den = ph.sb("den", [128, CT, L])
        bandm = ph.sb("bandm", [128, CT, C])
        normt = ph.sb("normt", [128, RW, W])
        xres = ph.sb("xres", [128, 2, L])
        dn = ph.sb("dn", [128, CW])
        both = ph.sb("both", [128, CW])
        none = ph.sb("none", [128, CW])
        rec = ph.sb("rec", [128, CW])
        top = ph.sb("top", [128, CW])
        psn = [ph.psum(f"psn{r}", [128, CW]) for r in range(2)]
        psd = [ph.psum(f"psd{r}", [128, CW]) for r in range(2)]
        s_band, s_zero, s_padded, s_sum1, s_sum2, s_num, s_pe, s_div, s_link, s_pool = (
            ph.sem(n) for n in "band zero padded sum1 sum2 num pe div link pool".split())
        s_xin = [ph.sem(f"xin{r}") for r in range(2)]
        s_res = [ph.sem(f"res{r}") for r in range(2)]
        s_out = [ph.sem(f"out{r}") for r in range(2)]
        s_done = ph.sem("done")
        xc_v, xn_v, out_v = (a.rearrange("(t p) (b n) -> b t p n", p=128, b=B) for a in (xc, xn, out))
        units = [(b, t) for b in range(B) for t in range(CT)]
        with nc.Block() as block:

            @block.sync
            def _(sp):
                sp.dma_start(bandm[:, :, :], band.rearrange("(t p) c -> p t c", p=128)).then_inc(s_band, 16)
                sp.dma_start(normt[:, :, :], norm.partition_broadcast(128)).then_inc(s_band, 16)
                for u in range(2):
                    sp.dma_start(xres[:, u, :], xc_v[units[u][0], units[u][1]]).then_inc(s_res[u], 16)
                for u, (b, t) in enumerate(units):
                    if u >= 2:
                        sp.wait_ge(s_padded, 2 * (u - 1))
                    sp.dma_start(xin[:, u % 2, :], xn_v[b, t]).then_inc(s_xin[u % 2], 16)
                for u, (b, t) in enumerate(units):
                    sp.wait_ge(s_done, NCH * (u + 1))
                    sp.dma_start(out_v[b, t], xres[:, u % 2, :]).then_inc(s_out[u % 2], 16)
                    if u + 2 < len(units):
                        sp.wait_ge(s_out[u % 2], 16 * (u // 2 + 1))
                        sp.dma_start(xres[:, u % 2, :], xc_v[units[u + 2][0], units[u + 2][1]])\
                          .then_inc(s_res[u % 2], 16)
                for r in range(2):
                    sp.wait_ge(s_out[r], 16 * (len(units) // 2))

            @block.gpsimd
            def _(pool):
                pool.memset(pad[:, :, :, :], 0.0).then_inc(s_zero, 1)
                pool.memset(pad2[:, :, :, :], 0.0).then_inc(s_zero, 1)
                for u, (b, t) in enumerate(units):
                    q = pad2[:, u % 2, :, :]
                    pool.wait_ge(s_padded, 2 * u + 2)
                    if u:
                        pool.wait_ge(s_sum2, u)
                    pool.tensor_tensor(pair2[:, :, :], q[:, :, 0:WP - 1], q[:, :, 1:WP], ALU.add).then_inc(s_pool, 1)
                    pool.wait_ge(s_pool, 2 * u + 1)
                    pool.tensor_tensor(s2[:, :, :], pair2[:, :, 0:W], pair2[:, :, 2:W + 2], ALU.add).then_inc(s_pool, 1)
                    pool.wait_ge(s_pool, 2 * u + 2)
                    if b:
                        pool.wait_ge(s_pe, CT * NCH * b)
                    pool.tensor_tensor(den[:, t, :].rearrange("p (h w) -> p h w", w=W), s2[:, :, :],
                                       q[:, :, 4:W + 4], ALU.add).then_inc(s_sum2, 1)

            @block.scalar
            def _(act):
                act.wait_ge(s_zero, 2)

                def square(u):
                    b, t = units[u]
                    act.wait_ge(s_sum1, u + 1)
                    if b:
                        act.wait_ge(s_pe, CT * NCH * b)
                    act.activation(num[:, t, :].rearrange("p (h w) -> p h w", w=W), s1[:, :, :],
                                   ACT.Square).then_inc(s_num, 1)

                for u, (b, t) in enumerate(units):
                    x = xin[:, u % 2, :].rearrange("p (h w) -> p h w", w=W)
                    act.wait_ge(s_xin[u % 2], 16 * (u // 2) + 16)
                    if u >= 2:
                        act.wait_ge(s_sum1, u - 1)
                        act.wait_ge(s_sum2, u - 1)
                    act.activation(pad[:, u % 2, :, LO:LO + W], x, ACT.Copy).then_inc(s_padded, 1)
                    act.activation(pad2[:, u % 2, :, LO:LO + W], x, ACT.Square).then_inc(s_padded, 1)
                    if u:
                        square(u - 1)
                square(len(units) - 1)

            @block.tensor
            def _(pe):
                pe.wait_ge(s_band, 32)
                n = 0
                for b in range(B):
                    pe.wait_ge(s_num, CT * (b + 1))
                    pe.wait_ge(s_sum2, CT * (b + 1))
                    for o in range(CT):
                        for c in range(NCH):
                            if n >= 2:
                                pe.wait_ge(s_div, n - 1)
                            for ps, src in ((psn, num), (psd, den)):
                                for t in near[o]:
                                    last = pe.matmul(ps[n % 2][:, :], bandm[:, t, o * 128:(o + 1) * 128],
                                                     src[:, t, c * CW:(c + 1) * CW],
                                                     start=t == near[o][0], stop=t == near[o][-1])
                            last.then_inc(s_pe, 1)
                            n += 1

            @block.vector
            def _(dve):
                chain = [0]

                def link(ins):
                    chain[0] += 1
                    ins.then_inc(s_link, 1)
                    dve.wait_ge(s_link, chain[0])

                def sums(u):
                    q = pad[:, u % 2, :, :]
                    dve.wait_ge(s_padded, 2 * u + 2)
                    link(dve.tensor_tensor(pair[:, :, :], q[:, :, 0:WP - 1], q[:, :, 1:WP], ALU.add))
                    if u:
                        dve.wait_ge(s_num, u)
                    link(dve.tensor_tensor(s1[:, :, :], pair[:, :, 0:W], pair[:, :, 2:W + 2], ALU.add))
                    dve.tensor_tensor(s1[:, :, :], s1[:, :, :], q[:, :, 4:W + 4], ALU.add).then_inc(s_sum1, 1)
                    dve.wait_ge(s_sum1, u + 1)

                def divide(u, c, n):
                    if n == 0:
                        dve.wait_ge(s_band, 32)
                    res = xres[:, u % 2, c * CW:(c + 1) * CW]
                    dve.wait_ge(s_pe, n + 1)
                    link(dve.tensor_tensor(dn[:, :], psd[n % 2][:, :], normt[:, :, :].rearrange("p r w -> p (r w)"),
                                           ALU.mult))
                    link(dve.tensor_tensor(both[:, :], psn[n % 2][:, :], dn[:, :], ALU.add))
                    link(dve.tensor_scalar(none[:, :], both[:, :], 0.0, None, ALU.is_equal))
                    dve.tensor_tensor(dn[:, :], dn[:, :], none[:, :], ALU.add).then_inc(s_link, 1)
                    chain[0] += 1
                    dve.tensor_tensor(top[:, :], psn[n % 2][:, :], none[:, :], ALU.add).then_inc(s_div, 1)
                    dve.wait_ge(s_link, chain[0])
                    link(dve.reciprocal(rec[:, :], dn[:, :]))
                    dve.wait_ge(s_div, n + 1)
                    link(dve.tensor_tensor(top[:, :], top[:, :], rec[:, :], ALU.mult))
                    dve.scalar_tensor_tensor(res, top[:, :], MAX_F32, res, ALU.min, ALU.add).then_inc(s_done, 1)
                    dve.wait_ge(s_done, n + 1)

                for b in range(B):
                    for t in range(CT):
                        sums(CT * b + t)
                    for o in range(CT):
                        u = CT * b + o
                        dve.wait_ge(s_res[u % 2], 16 * (u // 2) + 16)
                        for c in range(NCH):
                            divide(u, c, NCH * u + c)


SWP = 384
NCP = L // SWP


def pairs(eng, n, body, peel=False):
    if peel:
        for r in range(2):
            body(r, 0, r)
    with eng.Fori(1 if peel else 0, n // 2) as i:
        for r in range(2):
            body(2 * i + r, i, r)


def project_split(nc, tag, xn, w, scale, bias, parts, plain):
    with Phase(nc, f"ps{tag}") as ph:
        x = ph.sb("x", [128, CT, T])
        wt = ph.sb("wt", [128, 2, CT, 128])
        sc = ph.sb("sc", [128, 2 * CT])
        bi = ph.sb("bi", [128, 2 * CT])
        y = ph.sb("y", [128, B, L])
        p = [ph.sb(f"p{a}", [128, B, L], BF16) for a in range(3)]
        rest = ph.sb("rest", [128, 2, SWP])
        ps = [ph.psum(f"ps{r}", [128, SWP]) for r in range(2)]
        s_aff, s_mm, s_y, s_p0, s_rest, s_p1, s_p2 = (
            ph.sem(n) for n in "affine matmul y part0 rest part1 part2".split())
        s_x = [ph.sem(f"x{t}") for t in range(CT)]
        s_w = [ph.sem(f"w{r}") for r in range(2)]
        s_stored = [ph.sem(f"stored{b}") for b in range(B)]
        NB = B * NCP
        JOBS = 2 * CT
        w_v = w.rearrange("(t p) (j m) -> j p t m", p=128, m=128)
        parts_v = parts.rearrange("a (s b t p) n -> s t b a p n", s=2, b=B, p=128)
        plain_v = plain.rearrange("(s b t p) n -> s t b p n", s=2, b=B, p=128)

        with nc.Block() as block:

            @block.sync
            def _(sp):
                sp.dma_start(sc[:, :], scale).then_inc(s_aff, 16)
                sp.dma_start(bi[:, :], bias).then_inc(s_aff, 16)
                for r in range(2):
                    sp.dma_start(wt[:, r, :, :], w_v[r]).then_inc(s_w[r], 16)
                for t in range(CT):
                    sp.dma_start(x[:, t, :], xn.rearrange("(t p) n -> t p n", p=128)[t]).then_inc(s_x[t], 16)

                def body(j, i, r):
                    if not (isinstance(i, int) and i == 0):
                        sp.wait_ge(s_mm, NB * j - NB)
                        sp.dma_start(wt[:, r, :, :], w_v[j]).then_inc(s_w[r], 16)
                    for b in range(B):
                        sp.wait_ge(s_p2, NB * j + NCP * (b + 1))
                        sp.dma_start(plain_v[j // CT, j % CT, b], y[:, b, :]).then_inc(s_stored[b], 16)
                        for a in range(3):
                            sp.dma_start(parts_v[j // CT, j % CT, b, a], p[a][:, b, :]).then_inc(s_stored[b], 16)

                pairs(sp, JOBS, body, peel=True)
                for b in range(B):
                    sp.wait_ge(s_stored[b], 64 * JOBS)

            @block.tensor
            def _(pe):
                for t in range(CT):
                    pe.wait_ge(s_x[t], 16)

                def body(j, i, r):
                    pe.wait_ge(s_w[r], 16 * i + 16)
                    for c in range(NB):
                        pe.wait_ge(s_y, NB * j + (c + 1))
                        for t in range(CT):
                            last = pe.matmul(ps[c % 2][:, :], wt[:, r, t, :], x[:, t, c * SWP:(c + 1) * SWP],
                                             start=t == 0, stop=t == CT - 1)
                        last.then_inc(s_mm, 1)

                pairs(pe, JOBS, body)

            @block.vector
            def _(dve):
                dve.sem_inc(s_y, 2)
                dve.wait_ge(s_aff, 32)

                def plain_chunk(j, c):
                    b, k = c // NCP, c % NCP
                    if k == 0 and not (isinstance(j, int) and j == 0):
                        dve.wait_ge(s_stored[b], 64 * j)
                    dve.wait_ge(s_mm, NB * j + (c + 1))
                    dve.tensor_scalar(y[:, b, k * SWP:(k + 1) * SWP], ps[c % 2][:, :], cols(bi[:, :], 1)[:, j, :],
                                      cols(sc[:, :], 1)[:, j, :], ALU.add, ALU.mult).then_inc(s_y, 1)

                def rest_chunk(j, c):
                    b, k = c // NCP, c % NCP
                    dve.wait_ge(s_p0, NB * j + (c + 1))
                    if c >= 2 or not (isinstance(j, int) and j == 0):
                        dve.wait_ge(s_p2, NB * j + (c - 1))
                    dve.tensor_tensor(rest[:, c % 2, :], y[:, b, k * SWP:(k + 1) * SWP],
                                      p[0][:, b, k * SWP:(k + 1) * SWP], ALU.subtract).then_inc(s_rest, 1)

                def body(j, i, r):
                    plain_chunk(j, 0)
                    for c in range(NB):
                        if c + 1 < NB:
                            plain_chunk(j, c + 1)
                        rest_chunk(j, c)

                pairs(dve, JOBS, body, peel=True)

            @block.scalar
            def _(act):
                def body(j, i, r):
                    for c in range(NB):
                        b, k = c // NCP, c % NCP
                        part = slice(k * SWP, (k + 1) * SWP)
                        act.wait_ge(s_y, NB * j + (c + 3))
                        act.activation(p[0][:, b, part], y[:, b, part], ACT.Copy).then_inc(s_p0, 1)
                        act.wait_ge(s_rest, NB * j + (c + 1))
                        act.activation(p[1][:, b, part], rest[:, c % 2, :], ACT.Copy).then_inc(s_p1, 1)

                pairs(act, JOBS, body)

            @block.gpsimd
            def _(pool):
                def body(j, i, r):
                    for c in range(NB):
                        b, k = c // NCP, c % NCP
                        part = slice(k * SWP, (k + 1) * SWP)
                        pool.wait_ge(s_p1, NB * j + (c + 1))
                        pool.tensor_tensor(p[2][:, b, part], rest[:, c % 2, :], p[1][:, b, part],
                                           ALU.subtract).then_inc(s_p2, 1)

                pairs(pool, JOBS, body)


def tiles(eng, body, peel=False):
    for b in range(B):
        first = 1 if peel and b == 0 else 0
        if first:
            for r in range(2):
                body(b, 0, r)
        with eng.Fori(first, QT // 2) as i:
            for r in range(2):
                body(b, i, r)


def values(nc, tag, xn, w, bias, v, nh, dh):
    with Phase(nc, f"va{tag}") as ph:
        x = ph.sb("x", [128, CT, T])
        wt = ph.sb("wt", [128, CT, C])
        bi = ph.sb("bi", [128, C])
        xs = ph.sb("xs", [128, 2, CT, 128])
        vs = ph.sb("vs", [128, 2, C])
        ps = [ph.psum(f"ps{r}", [128, C]) for r in range(2)]
        s_w, s_xs, s_mm, s_vs = (ph.sem(n) for n in "w xs matmul vs".split())
        s_x = [ph.sem(f"x{b}") for b in range(B)]
        s_out = [ph.sem(f"out{r}") for r in range(2)]
        x_t = x[:, :, :].rearrange("p t (b n w) -> p t b n w", w=128, b=B)
        v_v = v.rearrange("(b h) p t d -> b t p h d", b=B)

        with nc.Block() as block:

            @block.sync
            def _(sp):
                sp.dma_start(wt[:, :, :], w.rearrange("(t p) m -> p t m", p=128)[:, :, 2 * C:3 * C])\
                  .then_inc(s_w, 16)
                sp.dma_start(bi[:, :], bias.partition_broadcast(128)).then_inc(s_w, 16)
                for b in range(B):
                    sp.dma_start(x[:, :, b * L:(b + 1) * L],
                                 xn.rearrange("(t p) (b n) -> b p t n", p=128, b=B)[b]).then_inc(s_x[b], 16)

                def body(b, i, r):
                    sp.wait_ge(s_vs, QT * b + 2 * i + (r + 3))
                    sp.dma_start(v_v[b, 2 * i + r], vs[:, r, :].rearrange("p (h d) -> p h d", d=dh))\
                      .then_inc(s_out[r], 16)

                tiles(sp, body)
                for r in range(2):
                    sp.wait_ge(s_out[r], 16 * (B * QT // 2))

            @block.gpsimd
            def _(pool):
                def body(b, i, r):
                    pool.wait_ge(s_x[b], 16)
                    pool.wait_ge(s_mm, QT * b + 2 * i + (r + 1))
                    pool.tensor_copy(xs[:, r, :, :], x_t[:, :, b, 2 * i + r, :]).then_inc(s_xs, 1)

                tiles(pool, body)

            @block.tensor
            def _(pe):
                pe.sem_inc(s_mm, 2)
                pe.wait_ge(s_w, 32)

                def body(b, i, r):
                    n = QT * b + 2 * i
                    pe.wait_ge(s_xs, n + (r + 1))
                    pe.wait_ge(s_vs, n + (r + 1))
                    for t in range(CT):
                        last = pe.matmul(ps[r][:, :], xs[:, r, t, :], wt[:, t, :], start=t == 0, stop=t == CT - 1)
                    last.then_inc(s_mm, 1)

                tiles(pe, body)

            @block.vector
            def _(dve):
                dve.sem_inc(s_vs, 2)
                dve.wait_ge(s_w, 32)

                def body(b, i, r):
                    dve.wait_ge(s_mm, QT * b + 2 * i + (r + 3))
                    if b or not isinstance(i, int):
                        dve.wait_ge(s_out[r], 16 * (QT // 2 * b + i))
                    dve.tensor_tensor(vs[:, r, :], ps[r][:, :], bi[:, :], ALU.add).then_inc(s_vs, 1)

                tiles(dve, body, peel=True)


def project_out(nc, tag, att, w, bias, xc, out):
    with Phase(nc, f"po{tag}") as ph:
        a = ph.sb("a", [128, CT, B, L])
        x = ph.sb("x", [128, CT, B, L])
        wt = ph.sb("wt", [128, CT, C])
        bi = ph.sb("bi", [128, CT])
        ps = [ph.psum(f"ps{r}", [128, SWP]) for r in range(2)]
        s_w, s_mm, s_sum, s_out = (ph.sem(n) for n in "w matmul sum out".split())
        s_a = [ph.sem(f"a{b}") for b in range(B)]
        s_x = [ph.sem(f"x{b}") for b in range(B)]
        NB = CT * NCP
        att_v = att.rearrange("(b t p) n -> b p t n", b=B, p=128)
        xc_v, out_v = (z.rearrange("(t p) (b n) -> b p t n", p=128, b=B) for z in (xc, out))

        with nc.Block() as block:

            @block.sync
            def _(sp):
                sp.dma_start(wt[:, :, :], w.rearrange("(t p) m -> p t m", p=128)).then_inc(s_w, 16)
                sp.dma_start(bi[:, :], bias.rearrange("(t p) -> p t", p=128),
                             allow_slow_non_contiguous=True).then_inc(s_w, 16)
                for b in range(B):
                    sp.dma_start(a[:, :, b, :], att_v[b]).then_inc(s_a[b], 16)
                    sp.dma_start(x[:, :, b, :], xc_v[b]).then_inc(s_x[b], 16)
                for b in range(B):
                    sp.wait_ge(s_sum, NB * (b + 1) + 2)
                    sp.dma_start(out_v[b], x[:, :, b, :]).then_inc(s_out, 16)
                sp.wait_ge(s_out, 16 * B)

            def chunks(eng, body):
                for b in range(B):
                    with eng.Fori(0, NCP // 2) as i:
                        for m in range(2 * CT):
                            body(b, i, m)

            @block.tensor
            def _(pe):
                pe.wait_ge(s_w, 32)

                def body(b, i, m):
                    if m == 0:
                        pe.wait_ge(s_a[b], 16)
                    o = m % CT
                    pe.wait_ge(s_sum, NB * b + 2 * CT * i + (m + 1))
                    for t in range(CT):
                        last = pe.matmul(ps[m % 2][:, :], wt[:, t, o * 128:(o + 1) * 128],
                                         cols(a[:, t, b, :], SWP)[:, 2 * i + m // CT, :],
                                         start=t == 0, stop=t == CT - 1)
                    last.then_inc(s_mm, 1)

                chunks(pe, body)

            @block.vector
            def _(dve):
                dve.sem_inc(s_sum, 2)
                dve.wait_ge(s_w, 32)

                def body(b, i, m):
                    if m == 0:
                        dve.wait_ge(s_x[b], 16)
                    o = m % CT
                    xo = cols(x[:, o, b, :], SWP)[:, 2 * i + m // CT, :]
                    dve.wait_ge(s_mm, NB * b + 2 * CT * i + (m + 1))
                    dve.scalar_tensor_tensor(xo, ps[m % 2][:, :], bi[:, o:o + 1], xo, ALU.add,
                                             ALU.add).then_inc(s_sum, 1)

                chunks(dve, body)


def group_weights(nc, q, gpd, t_param, parts, ident):
    HP = NH1 * GP // 2
    TG = 4 * GP
    N = B * QT
    with Phase(nc, "gw") as ph:
        gp = ph.sb("gp", [128, CT, TG])
        idn = ph.sb("idn", [128, 128])
        qs = ph.sb("qs", [128, 2, CT, 128])
        tv, mt, et, lt, st, dt, rt = (ph.sb(f"t{i}", [128, 1]) for i in range(7))
        small = ph.sb("small", [128, 1], mybir.dt.uint32)
        top = ph.sb("top", [128, NH1])
        d = ph.sb("d", [128, NH1, GP])
        e = ph.sb("e", [128, NH1, GP])
        s = ph.sb("s", [128, NH1])
        r_s = ph.sb("r_s", [128, NH1])
        g = ph.sb("g", [128, 2, NH1, GP])
        rest = ph.sb("rest", [HP, 2, 128])
        p = [ph.sb(f"p{a}", [HP, 2, T], BF16) for a in range(3)]
        ps = [ph.psum(f"ps{r}", [128, NH1, GP]) for r in range(2)]
        pt = [ph.psum(f"pt{r}", [128, 2, 128]) for r in range(2)]
        (s_c, s_t, s_tlink, s_tact, s_log, s_top, s_d, s_e, s_s, s_rs, s_g, s_turn, s_p0, s_rest, s_p1, s_p2) = (
            ph.sem(n) for n in ("const t tlink tact logits top d exp sum rsum g turned part0 rest part1 "
                                "part2").split())
        s_q = [ph.sem(f"q{r}") for r in range(2)]
        s_out = ph.sem("out")
        q_v = q.rearrange("(b c p) (t w) -> b t p c w", b=B, p=128, w=128)
        out_v = parts.rearrange("a (b f p) n -> a f p b n", b=B, f=2)

        def at(a, n):
            return p[a][:, :, :].rearrange("p f (n w) -> p f n w", w=128)[:, :, n, :]

        with nc.Block() as block:

            @block.sync
            def _(sp):
                sp.dma_start(gp[:, :, :], gpd).then_inc(s_c, 16)
                sp.dma_start(idn[:, :], ident).then_inc(s_c, 16)
                sp.dma_start(tv[:, :], t_param.partition_broadcast(128)).then_inc(s_c, 16)

                def body(n, i, r):
                    sp.wait_ge(s_log, n + 1)
                    sp.dma_start(qs[:, r, :, :], q_v[n // QT, n % QT]).then_inc(s_q[r], 16)

                pairs(sp, N, body)
                sp.wait_ge(s_p2, N + 1)
                for a in range(3):
                    for f in range(2):
                        sp.dma_start(out_v[a, f], p[a][:, f, :].rearrange("p (b n) -> p b n", b=B)).then_inc(s_out, 16)
                sp.wait_ge(s_out, 96)

            @block.tensor
            def _(pe):
                pe.sem_inc(s_log, 2)
                pe.wait_ge(s_c, 48)

                def body(n, i, r):
                    pe.wait_ge(s_q[r], 16 * i + 16)
                    pe.wait_ge(s_d, n + 1)
                    for c in range(CT):
                        last = pe.matmul(ps[r][:, 4 * c:4 * c + 4, :], qs[:, r, c, :], gp[:, c, :],
                                         start=True, stop=True, skip_group_check=True)
                    last.then_inc(s_log, 1)
                    pe.wait_ge(s_g, n + 1)
                    pe.wait_ge(s_rest, n + 1)
                    for f in range(2):
                        last = pe.transpose(pt[r][0:HP, f, :], g[:, r, f * NH1 // 2:(f + 1) * NH1 // 2, :]
                                            .rearrange("p h m -> p (h m)"), idn[:, :])
                    last.then_inc(s_turn, 1)

                pairs(pe, N, body)

            @block.vector
            def _(dve):
                chain = [0]
                dve.sem_inc(s_d, 2)
                dve.sem_inc(s_rest, 2)

                def link(ins):
                    chain[0] += 1
                    ins.then_inc(s_tlink, 1)
                    dve.wait_ge(s_tlink, chain[0])

                dve.wait_ge(s_tact, 3)
                link(dve.tensor_scalar(st[:, :], et[:, :], -0.25, None, ALU.mult))
                for coefficient in (1 / 3, -1 / 2, 1.0):
                    link(dve.scalar_tensor_tensor(st[:, :], st[:, :], coefficient, et[:, :], ALU.add, ALU.mult))
                link(dve.tensor_scalar(small[:, :], et[:, :], 0.015625, None, ALU.is_lt))
                link(dve.copy_predicated(lt[:, :], small[:, :], st[:, :]))
                link(dve.scalar_tensor_tensor(dt[:, :], tv[:, :], 0.0, lt[:, :], ALU.max, ALU.add))
                dve.reciprocal(rt[:, :], dt[:, :]).then_inc(s_t, 1)

                def body(n, i, r):
                    dve.wait_ge(s_log, n + 3)
                    dve.tensor_reduce(top[:, :], ps[r][:, :, :], AX.X, ALU.max).then_inc(s_top, 1)
                    dve.wait_ge(s_top, n + 1)
                    dve.tensor_tensor(d[:, :, :], ps[r][:, :, :],
                                      top[:, :].unsqueeze(2).to_broadcast([128, NH1, GP]),
                                      ALU.subtract).then_inc(s_d, 1)
                    dve.wait_ge(s_e, n + 1)
                    dve.tensor_reduce(s[:, :], e[:, :, :], AX.X, ALU.add).then_inc(s_s, 1)
                    dve.wait_ge(s_s, n + 1)
                    dve.reciprocal(r_s[:, :], s[:, :]).then_inc(s_rs, 1)
                    dve.wait_ge(s_rs, n + 1)
                    dve.tensor_tensor(g[:, r, :, :], e[:, :, :],
                                      r_s[:, :].unsqueeze(2).to_broadcast([128, NH1, GP]), ALU.mult).then_inc(s_g, 1)
                    dve.wait_ge(s_p0, n + 1)
                    dve.wait_ge(s_p2, n + 1)
                    dve.tensor_tensor(rest[:, :, :], pt[r][0:HP, :, :], at(0, n), ALU.subtract).then_inc(s_rest, 1)

                pairs(dve, N, body)

            @block.scalar
            def _(act):
                act.wait_ge(s_c, 48)
                act.activation(mt[:, :], tv[:, :], ACT.Abs).then_inc(s_tact, 1)
                act.wait_ge(s_tact, 1)
                act.activation(et[:, :], mt[:, :], ACT.Exp, scale=-1.0).then_inc(s_tact, 1)
                act.wait_ge(s_tact, 2)
                act.activation(lt[:, :], et[:, :], ACT.Ln, bias=1.0).then_inc(s_tact, 1)
                act.wait_ge(s_t, 1)

                def body(n, i, r):
                    act.wait_ge(s_d, n + 3)
                    act.activation(e[:, :, :], d[:, :, :], ACT.Exp, scale=rt[:, :]).then_inc(s_e, 1)
                    act.wait_ge(s_turn, n + 1)
                    act.activation(at(0, n), pt[r][0:HP, :, :], ACT.Copy).then_inc(s_p0, 1)
                    act.wait_ge(s_rest, n + 3)
                    act.activation(at(1, n), rest[:, :, :], ACT.Copy).then_inc(s_p1, 1)

                pairs(act, N, body)

            @block.gpsimd
            def _(pool):
                pool.sem_inc(s_p2, 1)

                def body(n, i, r):
                    pool.wait_ge(s_p1, n + 1)
                    pool.tensor_tensor(at(2, n), rest[:, :, :], at(1, n), ALU.subtract).then_inc(s_p2, 1)

                pairs(pool, N, body)


def relative(nc, q, relw, parts):
    N = B * NH3
    with Phase(nc, "re") as ph:
        rel = ph.sb("rel", [D3, 2, 2 * H - 1])
        qs = ph.sb("qs", [D3, 2, L])
        p = [ph.sb(f"p{a}", [H, 2, L], BF16) for a in range(3)]
        rest = ph.sb("rest", [H, 2, 384])
        ps = [ph.psum(f"ps{r}", [H, 8, H]) for r in range(2)]
        s_rel, s_mm, s_p0, s_rest, s_p1, s_p2 = (ph.sem(n) for n in "rel matmul part0 rest part1 part2".split())
        s_begun = ph.sem("begun")
        s_q = [ph.sem(f"q{r}") for r in range(2)]
        s_out = ph.sem("out")
        NC = 12
        out_v = parts.rearrange("a (h s k) n -> h a k s n", s=2, k=H)

        def at(a, m):
            if m < NC // 2:
                return p[a][:, 0, 8 * m * W:8 * (m + 1) * W].rearrange("p (y x) -> p y x", x=W)
            x0 = 8 * (m - NC // 2)
            return p[a][:, 1, :].rearrange("p (y x) -> p x y", x=W)[:, x0:x0 + 8, :]

        with nc.Block() as block:

            @block.sync
            def _(sp):
                sp.dma_start(rel[:, :, :], relw).then_inc(s_rel, 16)
                q_v = q.rearrange("(h d) n -> h d n", d=D3)
                for r in range(2):
                    sp.dma_start(qs[:, r, :], q_v[r]).then_inc(s_q[r], 16)

                def body(h, i, r, more=True):
                    sp.wait_ge(s_p2, NC * h + NC)
                    for a in range(3):
                        sp.dma_start(out_v[h, a], p[a][:, :, :]).then_inc(s_out, 16)
                    if more:
                        sp.dma_start(qs[:, r, :], q_v[h + 2]).then_inc(s_q[r], 16)

                pairs(sp, N - 2, body)
                for r in range(2):
                    body(N - 2 + r, N // 2 - 1, r, False)
                sp.wait_ge(s_out, 48 * N)

            @block.tensor
            def _(pe):
                pe.wait_ge(s_rel, 16)

                def body(h, i, r):
                    pe.wait_ge(s_q[r], 16 * i + 16)
                    for m in range(NC):
                        s = m // (NC // 2)
                        pe.wait_ge(s_rest, NC * h + (m + 1))
                        pe.sem_inc(s_begun, 1)
                        for k in range(8):
                            pos = 8 * (m % (NC // 2)) + k
                            at_q = qs[:, r, pos * W:(pos + 1) * W] if s == 0 else \
                                qs[:, r, :].rearrange("p (y x) -> p x y", x=W)[:, pos, :]
                            last = pe.matmul(ps[m % 2][:, k, :], rel[:, s, H - 1 - pos:2 * H - 1 - pos], at_q,
                                             start=True, stop=True, skip_group_check=True)
                        last.then_inc(s_mm, 1)

                pairs(pe, N, body)

            @block.scalar
            def _(act):
                def body(h, i, r):
                    if not (isinstance(i, int) and i == 0 and r == 0):
                        act.wait_ge(s_out, 48 * h)
                    for m in range(NC):
                        act.wait_ge(s_mm, NC * h + (m + 1))
                        act.activation(at(0, m), ps[m % 2][:, :, :], ACT.Copy).then_inc(s_p0, 1)
                        act.wait_ge(s_rest, NC * h + (m + 3))
                        act.activation(at(1, m), rest[:, m % 2, :].rearrange("p (a b) -> p a b", b=W),
                                       ACT.Copy).then_inc(s_p1, 1)

                pairs(act, N, body, peel=True)

            @block.vector
            def _(dve):
                dve.sem_inc(s_rest, 2)

                def body(h, i, r):
                    for m in range(NC):
                        dve.wait_ge(s_p0, NC * h + (m + 1))
                        if m >= 2 or not (isinstance(i, int) and i == 0 and r == 0):
                            dve.wait_ge(s_p2, NC * h + (m - 1))
                        dve.tensor_tensor(rest[:, m % 2, :].rearrange("p (a b) -> p a b", b=W), ps[m % 2][:, :, :],
                                          at(0, m), ALU.subtract).then_inc(s_rest, 1)

                pairs(dve, N, body, peel=True)

            @block.gpsimd
            def _(pool):
                def body(h, i, r):
                    for m in range(NC):
                        pool.wait_ge(s_p1, NC * h + (m + 1))
                        pool.tensor_tensor(at(2, m), rest[:, m % 2, :].rearrange("p (a b) -> p a b", b=W), at(1, m),
                                           ALU.subtract).then_inc(s_p2, 1)

                pairs(pool, N, body)


class Head:

    def __init__(self, n, buf, turn, rolled=False):
        self.n, self.buf, self.turn, self.rolled = n, buf, turn, rolled


def in_heads(eng, n, first, step, last):
    def step_at(i, u, rolled):
        s = 3 * i + u
        step(Head(s + 1, (u + 1) % 3, i + (u + 1) // 3, rolled), Head(s, u, i, rolled))

    first(Head(0, 0, 0))
    rounds = (n - 1) // 3
    with eng.Fori(0, rounds) as i:
        for u in range(3):
            step_at(i, u, True)
    for u in range(n - 1 - 3 * rounds):
        step_at(rounds, u, False)
    last(Head(n - 1, (n - 1) % 3, (n - 1) // 3))


def attention(nc, tag, nhb, dh, loads, score_sets, bias_set, rows, v_dram, att_out, bias_dram, identb,
              gate=None, ind=None, ones_in=None):
    NSUB = 2
    SW = 384
    CB = NSUB * SW
    NCB = L // CB
    NSA = 3 if gate else 2
    CA = NSA * SW
    NCA = L // CA
    G = 128 // dh
    OW = L // G
    OS = OW // (2 if gate else 3)
    NO = OW // OS
    O_BANK = 8 - NO if gate else 4
    O0 = 3 * QT
    B0 = 2 * QT * NCB
    E0 = B0
    T_BANK, T_COL = (O_BANK, OS) if gate else (7, 0)
    with Phase(nc, f"at{tag}") as ph:
        ops = {n: ph.sb(n, [128, 3, L], BF16) for n in loads}
        v = ph.sb("v", [128, 3, QT, dh])
        if ind is not None:
            ops["ind"] = ph.sb("ind", [128, 1, L], BF16)
        idb = ph.sb("idb", [128, 128], BF16)
        junk = ph.sb("junk", [128, 2, CA], BF16)
        e = ph.sb("e", [128, 2, CB]) if gate else None
        w = ph.sb("w", [128, 2, L])
        vs = ph.sb("vs", [128, 2, dh])
        nmax = ph.sb("nmax", [128, QT, NCA])
        zsum = ph.sb("zsum", [128, QT, NCA])
        nm = ph.sb("nm", [128, QT])
        diff = ph.sb("diff", [128, QT, NCA])
        ediff = ph.sb("ediff", [128, QT, NCA])
        ze = ph.sb("ze", [128, QT, NCA])
        z = ph.sb("z", [128, QT])
        lnz = ph.sb("lnz", [128, QT])
        bias = ph.sb("bias", [128, QT])
        rest = ph.sb("rest", [128, QT])
        bparts = ph.sb("bparts", [128, 128], BF16)
        bturned = ph.sb("bturned", [128, 128], BF16)
        dpart = ph.sb("dpart", [128, 2, NCB])
        djunk = ph.sb("djunk", [128, 2, NCB])
        dsum = ph.sb("dsum", [128, 2])
        drec = ph.sb("drec", [128, 2])
        osb = ph.sb("osb", [128, NO, OS])
        ps = ph.psum("ps", [128, 8, 512])
        psb = ps[:, :, :].bitcast(BF16)
        (s_const, s_sa, s_max, s_exp, s_diff, s_ediff, s_link, s_z, s_lnz, s_bparts, s_turn, s_turned, s_bout,
         s_brow, s_st, s_gate, s_e, s_w, s_vs, s_o, s_osb, s_stored, s_dsum, s_drec, s_ofree, s_bfree, s_id, s_begun, s_zero, s_moving) = (ph.sem(n) for n in (
             "const scoresA maxed exped diff ediff link zsum lnz bparts turn turned biasout "
             "brow scoresB gate expB weighted vscaled outprod osb stored dsum drec ofree bfree id begun zero moving").split())
        s_ops = [ph.sem(f"ops{r}") for r in range(3)]
        n_loads = sum(len(x) for x in loads.values()) + 1

        def sa(buf):
            return ps[:, NSA * buf:NSA * buf + NSA, 0:SW]

        def st(buf):
            return ps[:, NSUB * buf:NSUB * buf + NSUB, 0:SW]

        gps = ps[:, 2 * NSUB:3 * NSUB, 0:SW]
        ops_ps = ps[:, O_BANK:O_BANK + NO, 0:OS]
        tps = psb[:, T_BANK, 2 * T_COL:2 * T_COL + 128]

        def side(name, r):
            return ops[name][:, 0 if name == "ind" else r, :]

        with nc.Block() as block:

            @block.sync
            def _(sp):
                sp.sem_inc(s_ofree, 1)
                sp.sem_inc(s_bfree, 1)
                sp.dma_start(idb[:, :], identb).then_inc(s_id, 16)
                if ind is not None:
                    sp.dma_start(ops["ind"][0:ind.shape[0], 0, :], ind).then_inc(s_id, 16)

                def load(s, r):
                    for name, parts in loads.items():
                        for dram, part, n, at in parts:
                            src = dram[part].rearrange("(h r) n -> h r n", r=n)[s]
                            sp.dma_start(ops[name][at:at + n, r, :], src).then_inc(s_ops[r], 16)
                    sp.dma_start(v[:, r, :, :], v_dram[s]).then_inc(s_ops[r], 16)

                def bias_row(h):
                    sp.wait_ge(s_turned, h.n + 1)
                    sp.dma_start(bias_dram, bturned[0:3 * QT, :]).then_inc(s_bout, 16)
                    sp.wait_ge(s_bout, 16 * h.n + 16)
                    sp.sem_inc(s_bfree, 1)
                    sp.dma_start(ops[score_sets[bias_set][0]][rows:rows + 3, h.buf, :],
                                 bias_dram.rearrange("(a t) w -> a (t w)", a=3)).then_inc(s_brow, 16)
                    sp.wait_ge(s_brow, 16 * h.n + 16)

                def store(h):
                    sp.wait_ge(s_osb, h.n + 2)
                    dst = att_out.rearrange("(h d) (g n) -> h g d n", d=dh, g=G)[h.n]
                    for g in range(G):
                        sp.dma_start(dst[g], osb[g * dh:(g + 1) * dh, :, :].rearrange("p a b -> p (a b)"))\
                          .then_inc(s_stored, 16)
                    sp.wait_ge(s_stored, 16 * G * h.n + 16 * G)
                    sp.sem_inc(s_ofree, 1)

                def first(h):
                    for r in range(3):
                        load(r, r)
                    bias_row(h)

                def step(h, before):
                    store(before)
                    bias_row(h)
                    if h.rolled:
                        load(before.n + 3, before.buf)

                in_heads(sp, nhb, first, step, store)

            @block.gpsimd
            def _(pool):
                if ones_in:
                    for r in range(3):
                        pool.memset(ops[ones_in][rows:rows + 3, r, :], 1.0).then_inc(s_const, 1)

                def values(h):
                    pool.wait_ge(s_ops[h.buf], 16 * n_loads * h.turn + 16 * n_loads)
                    pool.sem_inc(s_moving, 1)
                    v_t = v[:, h.buf, :, :]
                    with pool.Fori(0, QT // 2) as j:
                        for k in range(2):
                            pool.wait_ge(s_o, QT * h.n + 2 * j + (k - 1 + O0))
                            pool.tensor_copy(vs[:, k, :], v_t[:, 2 * j + k, :]).then_inc(s_vs, 1)

                if not gate:
                    in_heads(pool, nhb, lambda h: None, lambda h, before: values(before), values)

            @block.tensor
            def _(pe):
                pe.sem_inc(s_o, O0)
                pe.wait_ge(s_id, 32 if ind is not None else 16)
                if ones_in:
                    pe.wait_ge(s_const, 3)

                def product(out, lhs, rhs, n_rows, buf, tile, at, start, stop):
                    for sub in range(out.shape[1]):
                        last = pe.matmul(out[:, sub, :], cols(side(lhs, buf)[0:n_rows, :], 128)[:, tile, :],
                                         side(rhs, buf)[0:n_rows, at + sub * SW:at + (sub + 1) * SW],
                                         start=start, stop=stop, skip_group_check=True)
                    return last

                def score(h):
                    pe.wait_ge(s_ops[h.buf], 16 * n_loads * h.turn + 16 * n_loads)
                    pe.wait_ge(s_w if gate else s_e, NCB * QT * h.n + NCB * QT)
                    pe.sem_inc(s_begun, 1)
                    with pe.Fori(0, QT // 2) as i:
                        for k in range(2):
                            for c in range(NCA):
                                m = NCA * k + c
                                pe.wait_ge(s_exp, QT * NCA * h.n + 2 * NCA * i + (m + 1))
                                for n, (q, kk, n_rows) in enumerate(score_sets):
                                    last = product(sa(m % 2), q, kk, n_rows, h.buf, 2 * i + k, c * CA, n == 0,
                                                   n == len(score_sets) - 1)
                                last.then_inc(s_sa, 1)

                def keys(h, i, k):
                    for c in range(NCB):
                        m = NCB * k + c
                        n_b = QT * NCB * h.n + 2 * NCB * i + m
                        pe.wait_ge(s_e, n_b + (E0 - 1))
                        for n, (q, kk, n_rows) in enumerate(score_sets):
                            last = product(st(m % 2), kk, q, n_rows + (3 if n == bias_set else 0), h.buf,
                                           2 * i + k, c * CB, n == 0, n == len(score_sets) - 1)
                        last.then_inc(s_st, 1)
                        if gate:
                            pe.wait_ge(s_w, n_b + B0)
                            product(gps, gate[1], gate[0], gate[2], h.buf, 2 * i + k, c * CB, True,
                                    True).then_inc(s_gate, 1)

                def values(h, n_t, k, start, stop):
                    pe.wait_ge(s_vs, n_t + 1)
                    if not gate:
                        pe.wait_ge(s_e, NCB * n_t + (NCB + E0))
                    for o in range(NO):
                        for g in range(G):
                            last = pe.matmul(ps[g * dh:(g + 1) * dh, O_BANK + o, 0:OS], vs[:, k, :],
                                             w[:, k, g * OW + o * OS:g * OW + (o + 1) * OS],
                                             start=start, stop=stop, skip_group_check=True)
                    last.then_inc(s_o, 1)

                def attend(h, scored):
                    pe.wait_ge(s_exp, QT * NCA * scored + 2)
                    pe.wait_ge(s_brow, 16 * h.n + 16)
                    keys(h, 0, 0)
                    keys(h, 0, 1)
                    pe.wait_ge(s_osb, h.n + 1)
                    values(h, QT * h.n, 0, True, False)
                    with pe.Fori(1, QT // 2) as i:
                        for k in range(2):
                            keys(h, i, k)
                            values(h, QT * h.n + 2 * i + (k - 1), 1 - k, False, False)
                    values(h, QT * h.n + (QT - 1), 1, False, True)

                def turn_bias(h):
                    pe.wait_ge(s_bparts, h.n + 1)
                    pe.wait_ge(s_osb, h.n + 1)
                    pe.transpose(tps, bparts[:, :], idb[:, :]).then_inc(s_turn, 1)

                def first(h):
                    score(h)
                    turn_bias(h)

                def step(h, before):
                    score(h)
                    attend(before, h.n + 1)
                    turn_bias(h)

                in_heads(pe, nhb, first, step, lambda h: attend(h, nhb))

            @block.scalar
            def _(act):
                act.sem_inc(s_exp, 2)
                act.sem_inc(s_e, E0)

                def score(h):
                    with act.Fori(0, QT // 2) as i:
                        for k in range(2):
                            for c in range(NCA):
                                m = NCA * k + c
                                act.wait_ge(s_max, QT * NCA * h.n + 2 * NCA * i + (m + 1))
                                act.activation(junk[:, m % 2, :].rearrange("p (a b) -> p a b", b=SW), sa(m % 2),
                                               ACT.Exp, bias=nmax[:, 2 * i + k, c:c + 1],
                                               accum_out=zsum[:, 2 * i + k, c:c + 1]).then_inc(s_exp, 1)
                    act.wait_ge(s_diff, h.n + 1)
                    act.activation(ediff[:, :, :], diff[:, :, :], ACT.Exp).then_inc(s_ediff, 1)
                    act.wait_ge(s_z, h.n + 1)
                    act.activation(lnz[:, :], z[:, :], ACT.Ln).then_inc(s_lnz, 1)

                def attend(h):
                    with act.Fori(0, QT // 2) as i:
                        for k in range(2):
                            for c in range(NCB):
                                m = NCB * k + c
                                n_b = QT * NCB * h.n + 2 * NCB * i + m
                                act.wait_ge(s_st, n_b + 1)
                                if gate:
                                    act.wait_ge(s_w, n_b + (B0 - 1))
                                    out = e[:, m % 2, :]
                                else:
                                    act.wait_ge(s_o, QT * h.n + 2 * i + (k - 1 + O0))
                                    out = w[:, k, c * CB:(c + 1) * CB]
                                act.activation(out.rearrange("p (a b) -> p a b", b=SW), st(m % 2),
                                               ACT.Exp).then_inc(s_e, 1)

                def step(h, before):
                    score(h)
                    attend(before)

                in_heads(act, nhb, score, step, attend)

            @block.vector
            def _(dve):
                dve.sem_inc(s_w, B0)
                dve.sem_inc(s_osb, 1)
                dve.memset(bparts[:, :], 0.0).then_inc(s_zero, 1)
                dve.wait_ge(s_zero, 1)
                N_FIN = 6

                def score(h):
                    with dve.Fori(0, QT // 2) as i:
                        for k in range(2):
                            for c in range(NCA):
                                m = NCA * k + c
                                dve.wait_ge(s_sa, QT * NCA * h.n + 2 * NCA * i + (m + 1))
                                dve.tensor_reduce(nmax[:, 2 * i + k, c:c + 1], sa(m % 2), AX.XY, ALU.max,
                                                  negate=True).then_inc(s_max, 1)
                    dve.wait_ge(s_exp, QT * NCA * h.n + (QT * NCA + 2))
                    dve.wait_ge(s_max, QT * NCA * h.n + QT * NCA)
                    done = N_FIN * h.n

                    def link(n, ins):
                        ins.then_inc(s_link, 1)
                        dve.wait_ge(s_link, done + n)

                    link(1, dve.tensor_reduce(nm[:, :], nmax[:, :, :], AX.X, ALU.min))
                    dve.tensor_tensor(diff[:, :, :], nm[:, :].unsqueeze(2).to_broadcast([128, QT, NCA]),
                                      nmax[:, :, :], ALU.subtract).then_inc(s_diff, 1)
                    dve.wait_ge(s_ediff, h.n + 1)
                    link(2, dve.tensor_tensor(ze[:, :, :], zsum[:, :, :], ediff[:, :, :], ALU.mult))
                    dve.tensor_reduce(z[:, :], ze[:, :, :], AX.X, ALU.add).then_inc(s_z, 1)
                    dve.wait_ge(s_lnz, h.n + 1)
                    link(3, dve.tensor_tensor(bias[:, :], nm[:, :], lnz[:, :], ALU.subtract))
                    link(4, dve.tensor_copy(bparts[:, 0 * QT:1 * QT], bias[:, :]))
                    link(5, dve.tensor_tensor(rest[:, :], bias[:, :], bparts[:, 0 * QT:1 * QT], ALU.subtract))
                    link(6, dve.tensor_copy(bparts[:, 1 * QT:2 * QT], rest[:, :]))
                    dve.tensor_tensor(bparts[:, 2 * QT:3 * QT], rest[:, :], bparts[:, 1 * QT:2 * QT],
                                      ALU.subtract).then_inc(s_bparts, 1)

                def attend(h):
                    v_t = v[:, h.buf, :, :]
                    if gate:
                        with dve.Fori(0, QT // 2) as i:
                            for k in range(2):
                                n_t = QT * h.n + 2 * i + k
                                dve.wait_ge(s_o, n_t + (O0 - 1))
                                for c in range(NCB):
                                    m = NCB * k + c
                                    n_b = QT * NCB * h.n + 2 * NCB * i + m
                                    dve.wait_ge(s_e, n_b + (E0 + 1))
                                    dve.wait_ge(s_gate, n_b + 1)
                                    dve.scalar_tensor_tensor(
                                        w[:, k, c * CB:(c + 1) * CB].rearrange("p (a b) -> p a b", b=SW), gps, 1.0,
                                        e[:, m % 2, :].rearrange("p (a b) -> p a b", b=SW), ALU.mult, ALU.mult,
                                        accum_out=dpart[:, k, c:c + 1]).then_inc(s_w, 1)
                                dve.wait_ge(s_w, n_b + (B0 + 1))
                                dve.tensor_scalar(djunk[:, k, :], dpart[:, k, :], 1.0, 1e-8, ALU.mult, ALU.add,
                                                  accum_out=dsum[:, k:k + 1]).then_inc(s_dsum, 1)
                                dve.wait_ge(s_dsum, n_t + 1)
                                dve.reciprocal(drec[:, k:k + 1], dsum[:, k:k + 1]).then_inc(s_drec, 1)
                                dve.wait_ge(s_drec, n_t + 1)
                                dve.tensor_scalar(vs[:, k, :], v_t[:, 2 * i + k, :], drec[:, k:k + 1], None,
                                                  ALU.mult).then_inc(s_vs, 1)
                    dve.wait_ge(s_o, QT * h.n + (QT + O0))
                    dve.wait_ge(s_ofree, h.n + 1)
                    dve.tensor_copy(osb[:, :, :], ops_ps).then_inc(s_osb, 1)

                def turned(h):
                    dve.wait_ge(s_turn, h.n + 1)
                    dve.wait_ge(s_bfree, h.n + 1)
                    dve.tensor_copy(bturned[:, :], tps).then_inc(s_turned, 1)

                def first(h):
                    score(h)
                    turned(h)

                def step(h, before):
                    score(h)
                    attend(before)
                    turned(h)

                in_heads(dve, nhb, first, step, attend)


def network(nc, a, out):
    def dram(name, shape, dt=F32):
        return nc.dram_tensor(name, shape, dt).ap()

    def pieces(src, order, n):
        return [(src, p, n, n * i) for i, p in enumerate(order)]

    x0, x1, x2, x3, x4, xn = (dram(n, [C, T]) for n in "x0 x1 x2 x3 x4 xn".split())
    split = dram("split", [3, 2 * B * C, L], BF16)
    q, k = split[:, 0:B * C, :], split[:, B * C:, :]
    plain = dram("plain", [2 * B * C, L])
    attended = dram("attended", [B * C, L])
    to_channels(nc, a["x"], x0, a["ident"])

    u, y = dram("u", [K * KINDS, 128, L]), dram("y", [K * KINDS, 128, L])
    group_norm(nc, "0", x0, xn, a["group_mean"])
    conv_inputs(nc, xn, a["w_in"], a["params0"], a["ident"], u)
    selective_scan(nc, u, a["w_x"], a["w_dt"], a["params"], a["one_hot"], a["ident"], y)
    norm_project(nc, y, a["norm_w"], a["norm_b"], a["w_out"], x0, x1)

    v1 = dram("v1", [B * NH1, 128, QT, D1])
    g = dram("g", [3, B * NH1 * GP, L], BF16)
    turned1 = dram("turned1", [3 * QT, 128], BF16)
    group_norm(nc, "1", x1, xn, a["group_mean"])
    project_split(nc, "1", xn, a["w_qkv1"], a["scale1"], a["bias1"], split, plain)
    values(nc, "1", xn, a["w_qkv1"], a["zeros"], v1, NH1, D1)
    group_weights(nc, plain[0:B * C, :], a["gaussians"], a["t_param"], g, a["ident"])
    attention(nc, "1", B * NH1, D1,
              dict(qa=pieces(q, (0, 1, 2), D1), qb=pieces(q, (0, 1, 0), D1),
                   ka=pieces(k, (0, 0, 0), D1), kb=pieces(k, (1, 1, 2), D1),
                   gi=pieces(g, (0, 1, 2, 0, 1, 0), GP), gj=pieces(g, (0, 0, 0, 1, 1, 2), GP)),
              [("qa", "ka", 3 * D1), ("qb", "kb", 3 * D1)], 0, 3 * D1, v1, attended, turned1, a["ident_b"],
              gate=("gi", "gj", 6 * GP), ones_in="ka")
    project_out(nc, "1", attended, a["w_proj1"], a["zeros"], x1, x2)

    group_norm(nc, "2", x2, xn, a["group_mean"])
    box_similarity(nc, x2, xn, x3, a["band"], a["window"])

    v3 = dram("v3", [B * NH3, 128, QT, D3])
    rel = dram("rel", [3, B * NH3 * 2 * H, L], BF16)
    turned3 = dram("turned3", [3 * QT, 128], BF16)
    group_norm(nc, "3", x3, xn, a["group_mean"])
    project_split(nc, "3", xn, a["w_qkv3"], a["scale3"], a["bias3"], split, plain)
    values(nc, "3", xn, a["w_qkv3"], a["bias_v3"], v3, NH3, D3)
    relative(nc, plain[0:B * C, :], a["rel_w"], rel)
    attention(nc, "3", B * NH3, D3,
              dict(qa=pieces(q, (0, 1), D3), qb=pieces(q, (2, 0), D3),
                   ka=pieces(k, (0, 0), D3), kb=pieces(k, (1, 1), D3), kc=pieces(k, (0, 2), D3),
                   r1=pieces(rel, (0,), 2 * H), r2=pieces(rel, (1,), 2 * H), r3=pieces(rel, (2,), 2 * H)),
              [("qa", "ka", 128), ("qa", "kb", 128), ("qb", "kc", 128),
               ("r1", "ind", 2 * H), ("r2", "ind", 2 * H), ("r3", "ind", 2 * H)], 3, 2 * H, v3, attended, turned3,
              a["ident_b"], ind=a["indicator"])
    project_out(nc, "3", attended, a["w_proj3"], a["bias_proj3"], x3, x4)

    to_tokens(nc, x4, out, a["ident"])


def layouts(inputs):
    import numpy as np
    bfloat16 = mybir.dt.np(BF16)
    f = np.float32
    i = {n: np.asarray(z) for n, z in inputs.items()}
    a = dict(x=i["x"].reshape(T, C))

    group = np.arange(C) // GN_GROUP
    a["group_mean"] = (group[:, None] == group[None]).astype(f) / GN_GROUP
    a["ident"] = np.eye(128, dtype=f)
    a["ident_b"] = a["ident"].astype(bfloat16)
    a["zeros"] = np.zeros(C, f)
    chan = np.arange(C)
    lo = WIN_C // 2
    a["band"] = ((chan[:, None] >= chan[None] - lo) & (chan[:, None] < chan[None] - lo + WIN_C)).astype(f)
    count = np.array([sum(0 <= w + s < W for s in range(-(WIN_W // 2), WIN_W // 2 + 1)) for w in range(W)], f)
    a["window"] = np.tile(count, 8)

    a["w_in"] = i["L0_conv_in_proj_w"].reshape(K, D_IN, CT, 128).transpose(3, 0, 2, 1)
    par = np.concatenate([i["L0_conv_conv_w"].reshape(CI, 9), i["L0_conv_conv_b"][:, None], i["L0_conv_Ds"][:, None],
                          i["L0_conv_dt_projs_bias"].reshape(CI, 1), i["L0_conv_A_logs"]], 1).reshape(K, D_IN, NPAR)
    a["params"] = np.stack([par[:, :128], np.concatenate([par[:, 128:], par[:, 128:]], 1)], 2)
    a["params0"] = a["params"].transpose(1, 0, 2, 3)
    kinds = [[(0, slice(0, 128), slice(0, 128))], [(1, slice(0, 128), slice(0, 128))],
             [(0, slice(0, LEFT), slice(128, D_IN)), (1, slice(LEFT, 128), slice(128, D_IN))]]
    w_x = np.zeros((K, 128, KINDS, 96), f)
    w_dt = np.zeros((K, B * R, KINDS, 128), f)
    one_hot = np.zeros((3, B, NS, KINDS, NS, 128), f)
    xw, dw = i["L0_conv_x_proj_weight"].transpose(0, 2, 1), i["L0_conv_dt_projs_weight"].transpose(0, 2, 1)
    for t, parts in enumerate(kinds):
        for b, to, of in parts:
            w_x[:, to, t, NS * b:NS * (b + 1)] = xw[:, of, R:R + NS]
            w_x[:, to, t, NS * (B + b):NS * (B + b + 1)] = xw[:, of, R + NS:]
            w_x[:, to, t, 2 * B * NS + R * b:2 * B * NS + R * (b + 1)] = xw[:, of, :R]
            w_dt[:, R * b:R * (b + 1), t, to] = dw[:, :, of]
            for s in range(NS):
                one_hot[:, b, s, t, s, to] = 1
    a["w_x"], a["w_dt"] = w_x, w_dt
    a["one_hot"] = one_hot.reshape(3 * B * NS, KINDS * NS, 128).astype(bfloat16)

    def by_tiles(z):
        z = z.reshape(K, D_IN, -1)
        return np.stack([z[k, :128] for k in range(K)] + [np.concatenate([z[k, 128:], z[k + 1, 128:]])
                                                          for k in range(0, K, 2)], 1)

    a["norm_w"] = by_tiles(i["L0_conv_out_norm_w"])[:, :, 0]
    a["norm_b"] = by_tiles(i["L0_conv_out_norm_b"])[:, :, 0]
    a["w_out"] = by_tiles(i["L0_conv_out_proj_w"].T)

    def affine(scale):
        s = np.ones((128, 2 * CT), f)
        s[:, CT:] = scale
        return s

    a["w_qkv1"], a["w_proj1"], a["t_param"] = i["L1_conv_W_qkv"], i["L1_conv_W_proj"], i["L1_conv_t_param"]
    a["scale1"], a["bias1"] = affine(D1 ** -0.5), np.zeros((128, 2 * CT), f)
    gp = i["L1_conv_gp_w"].reshape(NH1, GP, D1)
    a["gaussians"] = np.zeros((128, CT, 4 * GP), f)
    for h in range(NH1):
        r = h % 4
        a["gaussians"][D1 * r:D1 * (r + 1), h // 4, GP * r:GP * (r + 1)] = gp[h].T

    a["w_qkv3"], a["w_proj3"], a["bias_proj3"] = i["L3_conv_qkv_w"], i["L3_conv_proj_w"], i["L3_conv_proj_b"]
    a["scale3"] = affine(D3 ** -0.5)
    a["bias3"] = i["L3_conv_qkv_b"][:2 * C].reshape(2 * CT, 128).T
    a["bias_v3"] = i["L3_conv_qkv_b"][2 * C:]
    rows = np.minimum(2 * H - 2 - np.arange(2 * H - 1), i["L3_conv_rel_pos_h"].shape[0] - 1)
    a["rel_w"] = np.stack([i["L3_conv_rel_pos_h"][rows].T, i["L3_conv_rel_pos_w"][rows].T], 1)
    indicator = np.ones((2 * H + 3, L), f)
    token = np.arange(L)
    indicator[:H] = token // W == np.arange(H)[:, None]
    indicator[H:2 * H] = token % W == np.arange(W)[:, None]
    a["indicator"] = indicator.astype(bfloat16)
    return {n: np.ascontiguousarray(z) for n, z in a.items()}


def kernel(**inputs):
    import numpy as np
    import concourse.bacc as bacc
    from concourse.bass_utils import run_bass_kernel_spmd

    nc = bacc.Bacc("TRN2", target_bir_lowering=False, num_devices=1)
    arrays = {f"in_{n}": z for n, z in layouts(inputs).items()}
    args = {n[3:]: nc.dram_tensor(n, z.shape, mybir.dt.from_np(z.dtype), kind="ExternalInput").ap()
            for n, z in arrays.items()}
    out = nc.dram_tensor("out", (T, C), F32, kind="ExternalOutput").ap()
    network(nc, args, out)
    r = run_bass_kernel_spmd(nc, [arrays], core_ids=[0])
    return r.results[0]["out"].reshape(B, H, W, C)
```

```python
import concourse.bass as bass
from concourse import mybir
from contextlib import ExitStack

F32 = mybir.dt.float32
BF16 = mybir.dt.bfloat16
ALU = mybir.AluOpType
ACT = mybir.ActivationFunctionType
AX = mybir.AxisListType

B, H, W, C = 2, 48, 48, 384
L = H * W
T = B * L
CT = C // 128
GN_GROUP = C // 32
CI = 2 * C
K = 4
D_IN = CI // K
NS = 16
R = 12
KINDS = 3
LEFT = D_IN - 128
NH1, D1, GP = 12, 32, 20
NH3, D3 = 6, 64
QT = L // 128
BY, BX = 8, 16
NBX = W // BX
HALF = H // BY // 2
BROW = NBX * 128
REL_W, REL_H = 3 * BX, 3 * HALF * BY
REL = REL_W + REL_H


class Phase:

    def __init__(self, nc, name):
        self.nc, self.name, self.stack, self.sems = nc, name, ExitStack(), []

    def __enter__(self):
        self.stack.__enter__()
        return self

    def sb(self, name, shape, dt=F32):
        return self.stack.enter_context(self.nc.sbuf_tensor(f"{self.name}_{name}", shape, dt))

    def psum(self, name, shape, dt=F32):
        return self.stack.enter_context(self.nc.psum_tensor(f"{self.name}_{name}", shape, dt))

    def sem(self, name):
        s = self.nc.alloc_semaphore(f"{self.name}_{name}")
        self.sems.append(s)
        return s

    def __exit__(self, *a):
        self.stack.__exit__(*a)
        if a[0] is None:
            self.nc.clear_and_free_semaphores(self.sems)
            self.nc.all_engine_barrier()


def cols(ap, width):
    return ap.rearrange("p (n w) -> p n w", w=width)


def spans(total, width):
    return [(s, min(width, total - s)) for s in range(0, total, width)]


def to_channels(nc, x, xc, ident):
    with Phase(nc, "tc") as ph:
        tok = ph.sb("tok", [128, 2, C])
        idn = ph.sb("idn", [128, 128])
        xcm = ph.sb("xcm", [128, CT, T])
        ps = [ph.psum(f"ps{r}", [128, CT, 128]) for r in range(2)]
        s_idn, s_turned, s_copied, s_stored = (ph.sem(n) for n in ("idn", "turned", "copied", "stored"))
        s_tok = [ph.sem(f"tok{r}") for r in range(2)]
        x_v = x.rearrange("(n p) c -> n p c", p=128)
        xcm_v = xcm[:, :, :].rearrange("p t (n w) -> p t n w", w=128)
        with nc.Block() as block:

            @block.sync
            def _(sp):
                sp.dma_start(idn[:, :], ident).then_inc(s_idn, 16)
                for r in range(2):
                    sp.dma_start(tok[:, r, :], x_v[r]).then_inc(s_tok[r], 16)
                with sp.Fori(1, T // 256) as i:
                    for r in range(2):
                        sp.wait_ge(s_turned, 2 * i + r - 1)
                        sp.dma_start(tok[:, r, :], x_v[2 * i + r]).then_inc(s_tok[r], 16)
                sp.wait_ge(s_copied, T // 128)
                sp.dma_start(xc.rearrange("(t p) n -> p t n", p=128), xcm[:, :, :]).then_inc(s_stored, 16)
                sp.wait_ge(s_stored, 16)

            @block.tensor
            def _(pe):
                pe.wait_ge(s_idn, 16)

                def turn(i, r, peeled):
                    pe.wait_ge(s_tok[r], 16 * i + 16)
                    if not peeled:
                        pe.wait_ge(s_copied, 2 * i + r - 1)
                    for t in range(CT):
                        last = pe.transpose(ps[r][:, t, :], tok[:, r, t * 128:(t + 1) * 128], idn[:, :])
                    last.then_inc(s_turned, 1)

                for r in range(2):
                    turn(0, r, True)
                with pe.Fori(1, T // 256) as i:
                    for r in range(2):
                        turn(i, r, False)

            @block.vector
            def _(dve):
                with dve.Fori(0, T // 256) as i:
                    for r in range(2):
                        dve.wait_ge(s_turned, 2 * i + r + 1)
                        dve.tensor_copy(xcm_v[:, :, 2 * i + r, :], ps[r][:, :, :]).then_inc(s_copied, 1)


def to_tokens(nc, xc, out, ident):
    with Phase(nc, "tt") as ph:
        chn = ph.sb("chn", [128, 2, CT, 128])
        tok = ph.sb("tok", [128, 2, C])
        idn = ph.sb("idn", [128, 128])
        ps = [ph.psum(f"ps{r}", [128, CT, 128]) for r in range(2)]
        s_idn, s_turned, s_copied = (ph.sem(n) for n in ("idn", "turned", "copied"))
        s_chn = [ph.sem(f"chn{r}") for r in range(2)]
        s_out = [ph.sem(f"out{r}") for r in range(2)]
        xc_v = xc.rearrange("(t p) (n w) -> n p t w", p=128, w=128)
        out_v = out.rearrange("(n p) c -> n p c", p=128)
        with nc.Block() as block:

            @block.sync
            def _(sp):
                sp.dma_start(idn[:, :], ident).then_inc(s_idn, 16)
                for r in range(2):
                    sp.dma_start(chn[:, r, :, :], xc_v[r]).then_inc(s_chn[r], 16)
                with sp.Fori(1, T // 256) as i:
                    for r in range(2):
                        sp.wait_ge(s_turned, 2 * i + r - 1)
                        sp.dma_start(chn[:, r, :, :], xc_v[2 * i + r]).then_inc(s_chn[r], 16)

            @block.tensor
            def _(pe):
                pe.wait_ge(s_idn, 16)

                def turn(i, r, peeled):
                    pe.wait_ge(s_chn[r], 16 * i + 16)
                    if not peeled:
                        pe.wait_ge(s_copied, 2 * i + r - 1)
                    for t in range(CT):
                        last = pe.transpose(ps[r][:, t, :], chn[:, r, t, :], idn[:, :])
                    last.then_inc(s_turned, 1)

                for r in range(2):
                    turn(0, r, True)
                with pe.Fori(1, T // 256) as i:
                    for r in range(2):
                        turn(i, r, False)

            @block.vector
            def _(dve):
                def copy(i, r, peeled):
                    dve.wait_ge(s_turned, 2 * i + r + 1)
                    if not peeled:
                        dve.wait_ge(s_out[r], 16 * i)
                    dve.tensor_copy(tok[:, r, :], ps[r][:, :, :].rearrange("p t w -> p (t w)")).then_inc(s_copied, 1)

                for r in range(2):
                    copy(0, r, True)
                with dve.Fori(1, T // 256) as i:
                    for r in range(2):
                        copy(i, r, False)

            @block.scalar
            def _(act):
                with act.Fori(0, T // 256) as i:
                    for r in range(2):
                        act.wait_ge(s_copied, 2 * i + r + 1)
                        act.dma_start(out_v[2 * i + r], tok[:, r, :]).then_inc(s_out[r], 16)
                for r in range(2):
                    act.wait_ge(s_out[r], 16 * (T // 256))


def rows_first(ap):
    return ap.rearrange("p (b y x) -> p y b x", b=NBX, y=BY)


def group_norm(nc, tag, xc, xn, gmat, blocks=False, eps=1e-5):
    NCH = 6
    NPIECE = L // BROW if blocks else 1
    with Phase(nc, f"gn{tag}") as ph:
        x = ph.sb("x", [128, CT, B, L])
        xo = ph.sb("xo", [128, CT, B, L]) if blocks else x
        gm = ph.sb("gm", [128, CT, C])
        stats = ph.sb("stats", [128, CT, B, NCH, 6])
        mv = ph.sb("mv", [128, CT, B, 2])
        mean = ph.sb("mean", [128, CT, B])
        dev = ph.sb("dev", [128, CT, B])
        spread = ph.sb("spread", [128, CT, B])
        std = ph.sb("std", [128, CT, B])
        rstd = ph.sb("rstd", [128, CT, B])
        epsc = ph.sb("epsc", [128, 1])
        ps = ph.psum("ps", [128, 2, CT, B])
        s_gm, s_mv, s_mean, s_spread, s_var, s_std, s_xn, s_out, s_link = (
            ph.sem(n) for n in ("gm", "mv", "mean", "spread", "var", "std", "xn", "out", "link"))
        s_x = [ph.sem(f"x{t}") for t in range(CT)]
        xc_v = xc.rearrange("(t p) (b n) -> t p b n", p=128, b=B)
        xn_v = xn.rearrange("(t p) (b n) -> t p b n", p=128, b=B)
        with nc.Block() as block:

            @block.sync
            def _(sp):
                for t in range(CT):
                    sp.dma_start(x[:, t, :, :], xc_v[t]).then_inc(s_x[t], 16)
                sp.dma_start(gm[:, :, :], gmat.rearrange("(t p) c -> p t c", p=128)).then_inc(s_gm, 16)
                for t in range(CT):
                    sp.wait_ge(s_xn, B * NPIECE * (t + 1))
                    sp.dma_start(xn_v[t], xo[:, t, :, :]).then_inc(s_out, 16)
                sp.wait_ge(s_out, 16 * CT)

            @block.vector
            def _(dve):
                chain = [0]

                def link(ins):
                    chain[0] += 1
                    ins.then_inc(s_link, 1)
                    dve.wait_ge(s_link, chain[0])

                dve.memset(epsc[:, :], eps)
                for t in range(CT):
                    dve.wait_ge(s_x[t], 16)
                    for b in range(B):
                        for c, (s, w) in enumerate(spans(L, L // NCH)):
                            last = dve.bn_stats(stats[:, t, b, c, :], x[:, t, b, s:s + w])
                link(last)
                for t in range(CT):
                    for b in range(B):
                        dve.bn_aggr(mv[:, t, b, :], stats[:, t, b, :, :].rearrange("p n s -> p (n s)")).then_inc(s_mv, 1)
                dve.wait_ge(s_mean, 1)
                dve.wait_ge(s_mv, CT * B)
                link(dve.tensor_copy(mean[:, :, :], ps[:, 0, :, :]))
                link(dve.tensor_tensor(dev[:, :, :], mv[:, :, :, 0], mean[:, :, :], ALU.subtract))
                link(dve.tensor_tensor(dev[:, :, :], dev[:, :, :], dev[:, :, :], ALU.mult))
                dve.tensor_tensor(spread[:, :, :], dev[:, :, :], mv[:, :, :, 1], ALU.add).then_inc(s_spread, 1)
                dve.wait_ge(s_std, 1)
                link(dve.reciprocal(rstd[:, :, :], std[:, :, :]))
                for t in range(CT):
                    for b in range(B):
                        for s, w in spans(L, L // NPIECE):
                            src, dst = x[:, t, b, s:s + w], xo[:, t, b, s:s + w]
                            if blocks:
                                src, dst = src.rearrange("p (y b x) -> p y b x", b=NBX, y=BY), rows_first(dst)
                            dve.tensor_scalar(dst, src, mean[:, t, b:b + 1], rstd[:, t, b:b + 1],
                                              ALU.subtract, ALU.mult).then_inc(s_xn, 1)

            @block.tensor
            def _(pe):
                pe.wait_ge(s_gm, 16)
                pe.wait_ge(s_mv, CT * B)
                for o in range(CT):
                    for t in range(CT):
                        last = pe.matmul(ps[:, 0, o, :], gm[:, t, o * 128:(o + 1) * 128], mv[:, t, :, 0],
                                         start=t == 0, stop=t == CT - 1)
                last.then_inc(s_mean, 1)
                pe.wait_ge(s_spread, 1)
                for o in range(CT):
                    for t in range(CT):
                        last = pe.matmul(ps[:, 1, o, :], gm[:, t, o * 128:(o + 1) * 128], spread[:, t, :],
                                         start=t == 0, stop=t == CT - 1)
                last.then_inc(s_var, 1)

            @block.scalar
            def _(act):
                act.wait_ge(s_var, 1)
                act.activation(std[:, :, :], ps[:, 1, :, :], ACT.Sqrt, bias=epsc[:, :]).then_inc(s_std, 1)


PH, PW = H + 2, W + 2
CH = 8 * W
NC0 = L // CH
TAPS, CONV_B, SKIP, DT_B, A_LOG = 0, 9, 10, 11, 12
NPAR = A_LOG + NS


def scan_view(ap, k):
    if k >= 2:
        ap = ap[:, ::-1]
    if k % 2:
        return ap.rearrange("p (x y) -> p y x", y=H)
    return ap.rearrange("p (y x) -> p y x", x=W)


def conv_inputs(nc, xn, w_in, params, ident, u):
    PE_TAPS, V_TAPS = 3, 6
    with Phase(nc, "ci") as ph:
        x = ph.sb("x", [128, CT, B, L])
        wi = ph.sb("wi", [128, K, CT, D_IN])
        par = ph.sb("par", [128, K, 2, NPAR])
        idn = ph.sb("idn", [128, 128])
        diag = ph.sb("diag", [128, 2, PE_TAPS, 128])
        pad = ph.sb("pad", [128, 2, PH, PW])
        ut = ph.sb("ut", [128, 2, L])
        sums = ph.sb("sums", [128, 2, CH])
        pi = [ph.psum(f"pi{r}", [128, CH]) for r in range(2)]
        pc = [ph.psum(f"pc{r}", [128, CH]) for r in range(2)]
        s_w, s_zero, s_projected, s_placed, s_diag, s_conv, s_taps, s_silu, s_out0, s_out1 = (
            ph.sem(n) for n in "w zero in pad diag conv taps u out0 out1".split())
        s_out = [s_out0, s_out1]
        s_x = [ph.sem(f"x{t}") for t in range(CT)]
        units = [(k, kind) for k in range(K) for kind in range(KINDS)]
        with nc.Block() as block:

            @block.sync
            def _(sp):
                sp.dma_start(wi[:, :, :, :], w_in).then_inc(s_w, 16)
                sp.dma_start(par[:, :, :, :], params).then_inc(s_w, 16)
                sp.dma_start(idn[:, :], ident).then_inc(s_w, 16)
                for t in range(CT):
                    sp.dma_start(x[:, t, :, :], xn.rearrange("(t p) (b n) -> t p b n", p=128, b=B)[t])\
                      .then_inc(s_x[t], 16)
                for n, (k, kind) in enumerate(units):
                    sp.wait_ge(s_silu, NC0 * (n + 1))
                    sp.dma_start(u[n], ut[:, n % 2, :]).then_inc(s_out[n % 2], 16)
                for r in range(2):
                    sp.wait_ge(s_out[r], 16 * len(units) // 2)

            @block.gpsimd
            def _(pool):
                pool.memset(pad[:, :, :, :], 0.0).then_inc(s_zero, 1)
                pool.wait_ge(s_w, 48)
                for n, (k, kind) in enumerate(units):
                    if kind == 1:
                        continue
                    g = kind // 2
                    if k:
                        pool.wait_ge(s_conv, NC0 * (KINDS * (k - 1) + (2 if g == 0 else 3)))
                    for tap in range(PE_TAPS):
                        pool.tensor_scalar(diag[:, g, tap, :], idn[:, :], par[:, k, g, TAPS + tap:TAPS + tap + 1],
                                           None, ALU.mult).then_inc(s_diag, 1)

            @block.tensor
            def _(pe):
                for t in range(CT):
                    pe.wait_ge(s_x[t], 16)
                pe.wait_ge(s_w, 48)

                def project(n, chunks):
                    k, kind = units[n]
                    for c in chunks:
                        m = NC0 * n + c
                        if m >= 2:
                            pe.wait_ge(s_placed, m - 1)
                        if kind < 2:
                            parts = [(0, 128, 0, kind)]
                        else:
                            parts = [(0, LEFT, 128, 0), (LEFT, 128, 128, 1)]
                        for lo, hi, w0, b in parts:
                            for t in range(CT):
                                last = pe.matmul(pi[m % 2][lo:hi, :], wi[:, k, t, w0:w0 + hi - lo],
                                                 x[:, t, b, c * CH:(c + 1) * CH], start=t == 0, stop=t == CT - 1,
                                                 skip_group_check=True)
                        last.then_inc(s_projected, 1)

                def convolve(n, chunks):
                    k, kind = units[n]
                    g = kind // 2
                    if 0 in chunks:
                        pe.wait_ge(s_placed, NC0 * (n + 1))
                        pe.wait_ge(s_diag, PE_TAPS * (2 * k + g + 1))
                    for c in chunks:
                        m = NC0 * n + c
                        if m >= 2:
                            pe.wait_ge(s_taps, V_TAPS * (m - 2) + 1)
                        for tap in range(PE_TAPS):
                            dy, dx = tap // 3, tap % 3
                            last = pe.matmul(pc[m % 2][:, :], diag[:, g, tap, :],
                                             pad[:, n % 2, 8 * c + dy:8 * c + dy + 8, dx:dx + W],
                                             start=tap == 0, stop=tap == PE_TAPS - 1)
                        last.then_inc(s_conv, 1)

                project(0, range(NC0))
                for n in range(len(units)):
                    for c in range(NC0):
                        convolve(n, [c])
                        if n + 1 < len(units):
                            project(n + 1, [c])

            @block.vector
            def _(dve):
                dve.wait_ge(s_w, 48)
                for n, (k, kind) in enumerate(units):
                    for c in range(NC0):
                        m = NC0 * n + c
                        dve.wait_ge(s_conv, m + 1)
                        if m >= 2:
                            dve.wait_ge(s_silu, m - 1)
                        acc = sums[:, m % 2, :].rearrange("p (y x) -> p y x", x=W)
                        before = pc[m % 2][:, :].rearrange("p (y x) -> p y x", x=W)
                        for j in range(V_TAPS):
                            tap = PE_TAPS + j
                            dy, dx = tap // 3, tap % 3
                            if j:
                                dve.wait_ge(s_taps, V_TAPS * m + j)
                            dve.scalar_tensor_tensor(acc, pad[:, n % 2, 8 * c + dy:8 * c + dy + 8, dx:dx + W],
                                                     par[:, k, kind // 2, TAPS + tap:TAPS + tap + 1], before,
                                                     ALU.mult, ALU.add).then_inc(s_taps, 1)
                            before = acc

            @block.scalar
            def _(act):
                act.wait_ge(s_zero, 1)
                act.wait_ge(s_w, 48)

                def place(n, chunks):
                    for c in chunks:
                        m = NC0 * n + c
                        if c == 0 and n >= 2:
                            act.wait_ge(s_conv, NC0 * (n - 1))
                            act.wait_ge(s_taps, V_TAPS * NC0 * (n - 1))
                        act.wait_ge(s_projected, m + 1)
                        act.activation(pad[:, n % 2, 8 * c + 1:8 * c + 9, 1:W + 1],
                                       pi[m % 2][:, :].rearrange("p (y x) -> p y x", x=W), ACT.Copy).then_inc(s_placed, 1)

                def finish(n, chunks):
                    k, kind = units[n]
                    if n >= 2:
                        act.wait_ge(s_out[n % 2], 16 * (n // 2))
                    for c in chunks:
                        m = NC0 * n + c
                        act.wait_ge(s_taps, V_TAPS * (m + 1))
                        act.activation(scan_view(ut[:, n % 2, :], k)[:, 8 * c:8 * c + 8, :],
                                       sums[:, m % 2, :].rearrange("p (y x) -> p y x", x=W), ACT.Silu,
                                       bias=par[:, k, kind // 2, CONV_B:CONV_B + 1]).then_inc(s_silu, 1)

                place(0, range(NC0))
                for n in range(len(units)):
                    for c in range(NC0):
                        if n + 1 < len(units):
                            place(n + 1, [c])
                        finish(n, [c])


def selective_scan(nc, u, w_x, w_dt, params, sel, ident, y):
    NB = 2 * B * NS
    HB = NB // 2
    ND = B * R
    WC = 512
    parts = spans(L, WC)
    NP = len(parts)
    with Phase(nc, "ss") as ph:
        ut = ph.sb("ut", [128, KINDS, L])
        wx = ph.sb("wx", [128, KINDS, 96])
        wd = ph.sb("wd", [ND, KINDS, 128])
        par = ph.sb("par", [128, 2, NPAR])
        sl = ph.sb("sl", [3 * HB, KINDS * NS, 128], BF16)
        idn = ph.sb("idn", [128, 128])
        skip = ph.sb("skip", [128, 2, 128])
        a_exp = ph.sb("a_exp", [128, 2, NS])
        a_rate = ph.sb("a_rate", [128, 2, NS])
        pb, pc = ph.sb("pb", [3 * HB, L], BF16), ph.sb("pc", [3 * HB, L], BF16)
        bc = [ph.sb(f"bc{i}", [NB, L], BF16) for i in range(3)]
        rest = ph.sb("rest", [NB, 2, WC])
        dts = ph.sb("dts", [ND, L])
        dt = ph.sb("dt", [128, L])
        du = ph.sb("du", [128, L])
        decay, drive, state, cb, read = ([ph.sb(f"{n}{r}", [128, L]) for r in range(2)]
                                         for n in ("decay", "drive", "state", "cb", "read"))
        yt = ph.sb("yt", [128, L])
        ps = ph.psum("ps", [128, 8, WC])
        s_const, s_loaded, s_rate, s_skip, s_xdbl, s_dts, s_part0, s_rest, s_part1, s_part2, s_bc_placed = (
            ph.sem(n) for n in "const loaded rate skip xdbl dts part0 rest part1 part2 bc_placed".split())
        s_dt_products, s_dt_read, s_exped, s_log, s_small, s_link, s_dt = (
            ph.sem(n) for n in "dt_products dt_read exped log small link dt".split())
        s_b_spread, s_drive, s_decay, s_state, s_c_spread, s_c_taken, s_product, s_gathered = (
            ph.sem(n) for n in "b_spread drive decay state c_spread c_taken product gathered".split())
        s_y_taken, s_y_stored, s_out = (ph.sem(n) for n in "y_taken y_stored out".split())
        s_mark, s_pool_mark, s_begun = (ph.sem(n) for n in "mark pool_mark begun".split())
        y_ps = ps[:, 0:NP, :].rearrange("p a b -> p (a b)")[:, 0:L]
        raw, e, log, series = state[0], decay[0], decay[1], drive[0]
        small = cb[0][:, :].bitcast(mybir.dt.uint32)
        STATES = NS * KINDS
        LAG = 2

        def directions(eng, body):
            with eng.Fori(0, K) as k:
                body(k)

        def states(eng, k, t, body):
            with eng.Fori(0, NS // 2) as i:
                for r in range(2):
                    body(STATES * k + 2 * i + (NS * t + r), i, r)

        with nc.Block() as block:

            @block.sync
            def _(sp):
                sp.sem_inc(s_y_stored, 1)
                sp.dma_start(idn[:, :], ident).then_inc(s_const, 16)
                sp.dma_start(sl[:, :, :], sel).then_inc(s_const, 16)

                def load(k):
                    sp.dma_start(wx[:, :, :], w_x[k]).then_inc(s_loaded, 16)
                    sp.dma_start(wd[:, :, :], w_dt[k]).then_inc(s_loaded, 16)
                    sp.dma_start(par[:, :, :], params[k]).then_inc(s_loaded, 16)
                    sp.dma_start(ut[:, :, :], u.rearrange("(k t) p n -> k p t n", t=KINDS)[k]).then_inc(s_loaded, 16)

                def body(k, more=True):
                    sp.wait_ge(s_part2, NP * k + NP)
                    for i in range(3):
                        for j, dst in enumerate((pb, pc)):
                            sp.dma_start(dst[HB * i:HB * (i + 1), :], bc[i][HB * j:HB * (j + 1), :]).then_inc(s_bc_placed, 16)
                    for t in range(KINDS):
                        if more and t == KINDS - 1:
                            sp.wait_ge(s_dt, 2 * KINDS * k + 2 * KINDS)
                            sp.wait_ge(s_b_spread, NP * STATES * k + (NP * NS * t + 1))
                            load(k + 1)
                        sp.wait_ge(s_y_taken, KINDS * k + (t + 2))
                        sp.dma_start(y.rearrange("(k t) p n -> k t p n", t=KINDS)[k, t], yt[:, :]).then_inc(s_out, 16)
                        sp.wait_ge(s_out, 16 * KINDS * k + (16 * t + 16))
                        sp.sem_inc(s_y_stored, 1)

                load(0)
                with sp.Fori(0, K - 1) as k:
                    body(k)
                body(K - 1, False)

            @block.gpsimd
            def _(pool):
                def product(n, i, r):
                    pool.wait_ge(s_state, n + 3)
                    pool.wait_ge(s_c_taken, NP * n + (NP + 1))
                    pool.wait_ge(s_gathered, n + 1)
                    pool.tensor_tensor(read[r][:, :], state[r][:, :], cb[r][:, :], ALU.mult).then_inc(s_product, 1)

                def body(k):
                    for c, (at, w) in enumerate(parts):
                        pool.wait_ge(s_part1, NP * k + (c + 1))
                        pool.tensor_tensor(bc[2][:, at:at + w], rest[:, c % 2, 0:w], bc[1][:, at:at + w],
                                           ALU.subtract).then_inc(s_part2, 1)
                    for t in range(KINDS):
                        pool.wait_ge(s_exped, KINDS * k + (t + 1))
                        pool.sem_inc(s_pool_mark, 1)
                        pool.tensor_scalar(small, e[:, :], 0.015625, None, ALU.is_lt).then_inc(s_small, 1)
                        states(pool, k, t, product)

                pool.sem_inc(s_product, 2)
                directions(pool, body)

            @block.tensor
            def _(pe):
                pe.sem_inc(s_gathered, 2)
                pe.wait_ge(s_const, 32)

                def spread(n, i, r, t, c):
                    at, w = parts[c]
                    m = NP * r + c
                    row = sl[:, NS * t:NS * (t + 1), :][:, 2 * i + r, :]
                    pe.wait_ge(s_drive, NP * n + (c + 1))
                    pe.matmul(ps[:, 5 + m % 2, 0:w], row, pb[:, at:at + w], start=True, stop=True).then_inc(s_b_spread, 1)
                    pe.wait_ge(s_c_taken, NP * n + (c + 1))
                    pe.matmul(ps[:, 7, 0:w], row, pc[:, at:at + w], start=True, stop=True).then_inc(s_c_spread, 1)

                def gather(n, r, c, stop=False):
                    at, w = parts[c]
                    if c == 0:
                        pe.wait_ge(s_product, n + 3)
                    last = pe.matmul(ps[:, c, 0:w], idn[:, :], read[r][:, at:at + w], start=False, stop=stop,
                                     skip_group_check=True)
                    if c == NP - 1:
                        last.then_inc(s_gathered, 1)

                def late_gather(n, r, c):
                    if c < LAG:
                        gather(n - 3, 1 - r, c - LAG + NP)
                    else:
                        gather(n - 2, r, c - LAG)

                def dt_rows(k, t):
                    for c, (at, w) in enumerate(parts):
                        pe.wait_ge(s_dt_read, 2 * NP * KINDS * k + (2 * NP * t + 2 * c + 2))
                        pe.matmul(ps[:, 5 + c % 2, 0:w], wd[:, t, :], dts[:, at:at + w], start=True,
                                  stop=True).then_inc(s_dt_products, 1)

                def body(k):
                    pe.wait_ge(s_loaded, 64 * k + 64)
                    pe.wait_ge(s_y_taken, KINDS * k + 1)
                    for c, (at, w) in enumerate(parts):
                        if c >= 2:
                            pe.wait_ge(s_rest, NP * k + (c - 1))
                            pe.wait_ge(s_dts, NP * k + (c - 1))
                        for t in range(KINDS):
                            last = pe.matmul(ps[0:96, 5 + c % 2, 0:w], wx[:, t, :], ut[:, t, at:at + w],
                                             start=t == 0, stop=t == KINDS - 1)
                        last.then_inc(s_xdbl, 1)
                    pe.wait_ge(s_dts, NP * k + NP)
                    pe.wait_ge(s_rest, NP * k + NP)
                    dt_rows(k, 0)
                    pe.wait_ge(s_skip, 2 * k + 2)
                    pe.wait_ge(s_bc_placed, 96 * k + 96)
                    for t in range(KINDS):
                        pe.wait_ge(s_y_taken, KINDS * k + (t + 1))
                        pe.sem_inc(s_begun, 1)
                        for c, (at, w) in enumerate(parts):
                            pe.matmul(ps[:, c, 0:w], skip[:, t // 2, :], ut[:, t, at:at + w], start=True, stop=False,
                                      skip_group_check=True)
                        pe.wait_ge(s_dt_read, 2 * NP * KINDS * k + (2 * NP * (t + 1) + 4))
                        n0 = STATES * k + NS * t
                        for n in range(4):
                            for c in range(NP):
                                spread(n0 + n, n // 2, n % 2, t, c)
                                if n > 2 or n == 2 and c >= LAG:
                                    late_gather(n0 + n, n % 2, c)
                        with pe.Fori(2, NS // 2) as i:
                            for r in range(2):
                                for c in range(NP):
                                    spread(n0 + 2 * i + r, i, r, t, c)
                                    late_gather(n0 + 2 * i + r, r, c)
                        for c in range(NP - LAG, NP):
                            gather(n0 + (NS - 3), 1, c)
                        if t + 1 < KINDS:
                            pe.wait_ge(s_drive, NP * (n0 + NS) + 2)
                            dt_rows(k, t + 1)
                        for n in (NS - 2, NS - 1):
                            for c in range(NP):
                                gather(n0 + n, n % 2, c, stop=n == NS - 1)

                directions(pe, body)

            @block.scalar
            def _(act):
                act.sem_inc(s_y_taken, 1)
                act.sem_inc(s_c_taken, 1)
                act.sem_inc(s_dt_read, 4)

                def body(k):
                    act.wait_ge(s_loaded, 64 * k + 64)
                    act.activation(a_exp[:, :, :], par[:, :, A_LOG:NPAR], ACT.Exp).then_inc(s_rate, 1)
                    act.wait_ge(s_rate, 2 * k + 1)
                    act.activation(a_rate[:, :, :], a_exp[:, :, :], ACT.Copy, scale=-1.0).then_inc(s_rate, 1)
                    for c, (at, w) in enumerate(parts):
                        bank = ps[:, 5 + c % 2, 0:w]
                        act.wait_ge(s_xdbl, NP * k + (c + 1))
                        act.activation(bc[0][:, at:at + w], bank[0:NB, :], ACT.Copy).then_inc(s_part0, 1)
                        act.activation(dts[:, at:at + w], bank[NB:NB + ND, :], ACT.Copy).then_inc(s_dts, 1)
                        act.wait_ge(s_rest, NP * k + (c + 1))
                        act.activation(bc[1][:, at:at + w], rest[:, c % 2, 0:w], ACT.Copy).then_inc(s_part1, 1)

                    def dt_exp(t):
                        b_dt = par[:, t // 2, DT_B:DT_B + 1]
                        for c, (at, w) in enumerate(parts):
                            bank = ps[:, 5 + c % 2, 0:w]
                            act.wait_ge(s_dt_products, NP * KINDS * k + (NP * t + c + 1))
                            act.activation(log[:, at:at + w], bank, ACT.Abs, bias=b_dt).then_inc(s_dt_read, 1)
                            act.activation(raw[:, at:at + w], bank, ACT.Identity, bias=b_dt).then_inc(s_dt_read, 1)
                        act.wait_ge(s_dt_read, 2 * NP * KINDS * k + (2 * NP * (t + 1) + 4))
                        act.activation(e[:, :], log[:, :], ACT.Exp, scale=-1.0).then_inc(s_exped, 1)
                        act.wait_ge(s_exped, KINDS * k + (t + 1))
                        act.activation(log[:, :], e[:, :], ACT.Ln, bias=1.0).then_inc(s_log, 1)

                    dt_exp(0)
                    for t in range(KINDS):
                        act.wait_ge(s_rate, 2 * k + 2)
                        act.wait_ge(s_dt, 2 * KINDS * k + (2 * t + 1))

                        def decays(n, i, r, half):
                            if half == 0:
                                act.wait_ge(s_state, n + 1)
                            part = slice(half * L // 2, (half + 1) * L // 2)
                            act.activation(decay[r][:, part], dt[:, part], ACT.Exp,
                                           scale=cols(a_rate[:, t // 2, :], 1)[:, 2 * i + r, :]).then_inc(s_decay, 1)

                        def state_step(n, i, r, more=True):
                            act.wait_ge(s_product, n + 1)
                            for c, (at, w) in enumerate(parts):
                                act.wait_ge(s_c_spread, NP * n + (c + 1))
                                act.activation(cb[r][:, at:at + w], ps[:, 7, 0:w], ACT.Copy).then_inc(s_c_taken, 1)
                                if more and c in (1, 3):
                                    decays(n + 1, i + r, 1 - r, c // 2)

                        n0 = STATES * k + NS * t
                        for half in range(2):
                            decays(n0, 0, 0, half)
                        with act.Fori(0, NS // 2 - 1) as i:
                            for r in range(2):
                                state_step(n0 + 2 * i + r, i, r)
                        for r in range(2):
                            state_step(n0 + (NS - 2 + r), NS // 2 - 1, r, r == 0)
                        if t + 1 < KINDS:
                            act.wait_ge(s_state, n0 + (NS + 2))
                            act.wait_ge(s_product, n0 + (NS + 1))
                            dt_exp(t + 1)
                        act.wait_ge(s_gathered, STATES * k + (NS * (t + 1) + 2))
                        act.wait_ge(s_y_stored, KINDS * k + (t + 1))
                        act.activation(yt[:, :], y_ps, ACT.Copy).then_inc(s_y_taken, 1)

                directions(act, body)

            @block.vector
            def _(dve):
                dve.sem_inc(s_drive, 2)
                dve.sem_inc(s_state, 2)

                def body(k):
                    dve.wait_ge(s_loaded, 64 * k + 64)
                    for g in range(2):
                        dve.tensor_scalar(skip[:, g, :], idn[:, :], par[:, g, SKIP:SKIP + 1], None,
                                          ALU.mult).then_inc(s_skip, 1)
                    for c, (at, w) in enumerate(parts):
                        dve.wait_ge(s_part0, NP * k + (c + 1))
                        if c >= 2:
                            dve.wait_ge(s_part2, NP * k + (c - 1))
                        dve.tensor_tensor(rest[:, c % 2, 0:w], ps[0:NB, 5 + c % 2, 0:w], bc[0][:, at:at + w],
                                          ALU.subtract).then_inc(s_rest, 1)
                    for t in range(KINDS):
                        steps = [0]
                        LINKS = 4

                        def link(ins):
                            steps[0] += 1
                            ins.then_inc(s_link, 1)
                            dve.wait_ge(s_link, LINKS * KINDS * k + (LINKS * t + steps[0]))

                        dve.wait_ge(s_exped, KINDS * k + (t + 1))
                        link(dve.tensor_scalar(series[:, :], e[:, :], 1 / 3, None, ALU.mult))
                        for coefficient in (-1 / 2, 1.0):
                            link(dve.scalar_tensor_tensor(series[:, :], series[:, :], coefficient, e[:, :],
                                                          ALU.add, ALU.mult))
                        dve.wait_ge(s_log, KINDS * k + (t + 1))
                        dve.wait_ge(s_small, KINDS * k + (t + 1))
                        dve.sem_inc(s_mark, 1)
                        link(dve.copy_predicated(log[:, :], small, series[:, :]))
                        assert steps[0] == LINKS
                        dve.scalar_tensor_tensor(dt[:, :], raw[:, :], 0.0, log[:, :], ALU.max,
                                                 ALU.add).then_inc(s_dt, 1)
                        dve.wait_ge(s_dt, 2 * KINDS * k + (2 * t + 1))
                        dve.tensor_tensor(du[:, :], dt[:, :], ut[:, t, :], ALU.mult).then_inc(s_dt, 1)
                        dve.wait_ge(s_dt, 2 * KINDS * k + (2 * t + 2))
                        dve.sem_inc(s_mark, 1)

                        def state_step(n, i, r):
                            dve.wait_ge(s_state, n + 1)
                            for c, (at, w) in enumerate(parts):
                                dve.wait_ge(s_b_spread, NP * n + (c + 1))
                                dve.tensor_tensor(drive[r][:, at:at + w], ps[:, 5 + (NP * r + c) % 2, 0:w],
                                                  du[:, at:at + w], ALU.mult).then_inc(s_drive, 1)
                            dve.wait_ge(s_decay, 2 * n + 2)
                            dve.wait_ge(s_drive, NP * n + (NP + 2))
                            dve.wait_ge(s_product, n + 1)
                            dve.tensor_tensor_scan(state[r][:, :], decay[r][:, :], drive[r][:, :], 0.0, ALU.mult,
                                                   ALU.add).then_inc(s_state, 1)

                        states(dve, k, t, state_step)

                directions(dve, body)


def norm_project(nc, y, norm_w, norm_b, w_out, xc, out, eps=1e-5):
    NT = CI // 128
    with Phase(nc, "np") as ph:
        raw = ph.sb("raw", [128, 2, L])
        yr = ph.sb("yr", [128, NT, L])
        wo = ph.sb("wo", [128, NT, C])
        nw = ph.sb("nw", [128, NT])
        nb = ph.sb("nb", [128, NT])
        ones = ph.sb("ones", [128, 128])
        epsc = ph.sb("epsc", [128, 1])
        sq = ph.sb("sq", [128, NT, CH])
        yc = ph.sb("yc", [128, 3, NT, CH])
        std = ph.sb("std", [128, CH])
        rstd = ph.sb("rstd", [128, CH])
        x = ph.sb("x", [128, B, CT, L])
        pm = ph.psum("pm", [128, CH])
        pv = ph.psum("pv", [128, CH])
        po = [ph.psum(f"po{r}", [128, CH]) for r in range(2)]
        (s_w, s_ones, s_turned, s_mean, s_centred, s_squared, s_var, s_std, s_rstd, s_scaled, s_affine, s_projected, s_sum, s_out) = (
            ph.sem(n) for n in "w ones turned mean yc sq var std rstd scaled yn o sum out".split())
        s_y_loaded = [ph.sem(f"y{r}") for r in range(2)]
        s_x = [ph.sem(f"x{b}") for b in range(B)]
        N = B * NC0
        xc_v, out_v = (z.rearrange("(t p) (b n) -> b p t n", p=128, b=B) for z in (xc, out))

        def sources(j, b):
            if j < K:
                return [(0, 128, KINDS * j + b, 0, j)]
            return [(64 * h, 64 * h + 64, KINDS * (2 * (j - K) + h) + 2, 64 * b, 2 * (j - K) + h) for h in range(2)]

        with nc.Block() as block:

            @block.sync
            def _(sp):
                sp.dma_start(wo[:, :, :], w_out).then_inc(s_w, 16)
                sp.dma_start(nw[:, :], norm_w).then_inc(s_w, 16)
                sp.dma_start(nb[:, :], norm_b).then_inc(s_w, 16)
                for b in range(B):
                    for j in range(NT):
                        n = NT * b + j
                        if n >= 2:
                            sp.wait_ge(s_turned, n - 1)
                        for lo, hi, tile, p0, _ in sources(j, b):
                            sp.dma_start(raw[lo:hi, n % 2, :], y[tile, p0:p0 + hi - lo, :]).then_inc(s_y_loaded[n % 2], 16)
                    sp.dma_start(x[:, b, :, :], xc_v[b]).then_inc(s_x[b], 16)
                for b in range(B):
                    sp.wait_ge(s_sum, CT * NC0 * (b + 1))
                    sp.dma_start(out_v[b], x[:, b, :, :]).then_inc(s_out, 16)
                sp.wait_ge(s_out, 16 * B)

            @block.gpsimd
            def _(pool):
                pool.memset(ones[:, :], 1.0 / CI).then_inc(s_ones, 1)
                pool.memset(epsc[:, :], eps).then_inc(s_ones, 1)
                for m in range(N):
                    pool.wait_ge(s_rstd, m + 1)
                    for j in range(NT):
                        pool.tensor_tensor(yc[:, m % 3, j, :], yc[:, m % 3, j, :], rstd[:, :],
                                           ALU.mult).then_inc(s_scaled, 1)

            @block.vector
            def _(dve):
                dve.wait_ge(s_w, 48)
                seen = [0, 0]

                def turn(b):
                    if b:
                        dve.wait_ge(s_mean, NC0 * b)
                    for j in range(NT):
                        n = NT * b + j
                        pieces = sources(j, b)
                        seen[n % 2] += 16 * len(pieces)
                        dve.wait_ge(s_y_loaded[n % 2], seen[n % 2])
                        for lo, hi, _, _, k in pieces:
                            last = dve.tensor_copy(yr[lo:hi, j, :].rearrange("p (y x) -> p y x", x=W),
                                                   scan_view(raw[lo:hi, n % 2, :], k))
                        last.then_inc(s_turned, 1)
                    dve.wait_ge(s_turned, NT * (b + 1))

                def center(m):
                    c = m % NC0
                    dve.wait_ge(s_mean, m + 1)
                    if m >= 3:
                        dve.wait_ge(s_projected, CT * (m - 2))
                    for j in range(NT):
                        dve.tensor_tensor(yc[:, m % 3, j, :], yr[:, j, c * CH:(c + 1) * CH], pm[:, :],
                                          ALU.subtract).then_inc(s_centred, 1)

                def invert(m):
                    dve.wait_ge(s_std, m + 1)
                    if m:
                        dve.wait_ge(s_scaled, NT * m)
                    dve.reciprocal(rstd[:, :], std[:, :]).then_inc(s_rstd, 1)

                def finish(m):
                    b, c = m // NC0, m % NC0
                    dve.wait_ge(s_x[b], 16)
                    for o in range(CT):
                        old = x[:, b, o, c * CH:(c + 1) * CH]
                        dve.wait_ge(s_projected, CT * m + o + 1)
                        dve.tensor_tensor(old, po[(CT * m + o) % 2][:, :], old, ALU.add).then_inc(s_sum, 1)

                turn(0)
                center(0)
                for m in range(N):
                    if (m + 1) % NC0:
                        center(m + 1)
                    invert(m)
                    if m:
                        finish(m - 1)
                    if m + 1 < N and (m + 1) % NC0 == 0:
                        turn((m + 1) // NC0)
                        center(m + 1)
                finish(N - 1)

            @block.scalar
            def _(act):
                act.wait_ge(s_w, 48)
                act.wait_ge(s_ones, 2)

                def squares(m):
                    if m:
                        act.wait_ge(s_var, m)
                    for j in range(NT):
                        act.wait_ge(s_centred, NT * m + j + 1)
                        act.activation(sq[:, j, :], yc[:, m % 3, j, :], ACT.Square).then_inc(s_squared, 1)

                def affine(m):
                    for j in range(NT):
                        act.wait_ge(s_scaled, NT * m + j + 1)
                        act.activation(yc[:, m % 3, j, :], yc[:, m % 3, j, :], ACT.Identity, scale=nw[:, j:j + 1],
                                       bias=nb[:, j:j + 1]).then_inc(s_affine, 1)

                squares(0)
                for m in range(N):
                    act.wait_ge(s_var, m + 1)
                    if m:
                        act.wait_ge(s_rstd, m)
                    act.activation(std[:, :], pv[:, :], ACT.Sqrt, bias=epsc[:, :]).then_inc(s_std, 1)
                    if (m + 1) % NC0:
                        squares(m + 1)
                    affine(m)
                    if m + 1 < N and (m + 1) % NC0 == 0:
                        squares(m + 1)

            @block.tensor
            def _(pe):
                pe.wait_ge(s_ones, 2)
                pe.wait_ge(s_w, 48)

                def outputs(m):
                    pe.wait_ge(s_affine, NT * (m + 1))
                    for o in range(CT):
                        n = CT * m + o
                        if n >= 2:
                            pe.wait_ge(s_sum, n - 1)
                        for j in range(NT):
                            last = pe.matmul(po[n % 2][:, :], wo[:, j, o * 128:(o + 1) * 128], yc[:, m % 3, j, :],
                                             start=j == 0, stop=j == NT - 1)
                        last.then_inc(s_projected, 1)

                def mean(m):
                    b, c = m // NC0, m % NC0
                    pe.wait_ge(s_turned, NT * (b + 1))
                    if m:
                        pe.wait_ge(s_centred, NT * m)
                    for j in range(NT):
                        last = pe.matmul(pm[:, :], ones[:, :], yr[:, j, c * CH:(c + 1) * CH], start=j == 0,
                                         stop=j == NT - 1)
                    last.then_inc(s_mean, 1)

                def variance(m):
                    pe.wait_ge(s_squared, NT * (m + 1))
                    if m:
                        pe.wait_ge(s_std, m)
                    for j in range(NT):
                        last = pe.matmul(pv[:, :], ones[:, :], sq[:, j, :], start=j == 0, stop=j == NT - 1)
                    last.then_inc(s_var, 1)

                mean(0)
                for m in range(N):
                    if (m + 1) % NC0:
                        mean(m + 1)
                    variance(m)
                    if m:
                        outputs(m - 1)
                    if m + 1 < N and (m + 1) % NC0 == 0:
                        mean(m + 1)
                outputs(N - 1)


WIN_W = 5
WIN_C = 20
MAX_F32 = 3.4028234663852886e38


def box_similarity(nc, xc, xn, out, band, norm):
    LO = WIN_W // 2
    WP = W + WIN_W - 1
    NCH, RW = 6, 8
    CW = RW * W
    near = [[t for t in range(CT) if abs(t - o) <= 1] for o in range(CT)]
    with Phase(nc, "box") as ph:
        xin = ph.sb("xin", [128, 2, L])
        pad = ph.sb("pad", [128, 2, H, WP])
        pad2 = ph.sb("pad2", [128, 2, H, WP])
        pair = ph.sb("pair", [128, H, WP - 1])
        pair2 = ph.sb("pair2", [128, H, WP - 1])
        s1 = ph.sb("s1", [128, H, W])
        s2 = ph.sb("s2", [128, H, W])
        num = ph.sb("num", [128, CT, L])
        den = ph.sb("den", [128, CT, L])
        bandm = ph.sb("bandm", [128, CT, C])
        normt = ph.sb("normt", [128, RW, W])
        xres = ph.sb("xres", [128, 2, L])
        dn = ph.sb("dn", [128, CW])
        both = ph.sb("both", [128, CW])
        none = ph.sb("none", [128, CW])
        rec = ph.sb("rec", [128, CW])
        top = ph.sb("top", [128, CW])
        psn = [ph.psum(f"psn{r}", [128, CW]) for r in range(2)]
        psd = [ph.psum(f"psd{r}", [128, CW]) for r in range(2)]
        s_band, s_zero, s_padded, s_sum1, s_sum2, s_num, s_pe, s_div, s_link, s_pool = (
            ph.sem(n) for n in "band zero padded sum1 sum2 num pe div link pool".split())
        s_xin = [ph.sem(f"xin{r}") for r in range(2)]
        s_res = [ph.sem(f"res{r}") for r in range(2)]
        s_out = [ph.sem(f"out{r}") for r in range(2)]
        s_done = ph.sem("done")
        xc_v, xn_v, out_v = (a.rearrange("(t p) (b n) -> b t p n", p=128, b=B) for a in (xc, xn, out))
        units = [(b, t) for b in range(B) for t in range(CT)]
        with nc.Block() as block:

            @block.sync
            def _(sp):
                sp.dma_start(bandm[:, :, :], band.rearrange("(t p) c -> p t c", p=128)).then_inc(s_band, 16)
                sp.dma_start(normt[:, :, :], norm.partition_broadcast(128)).then_inc(s_band, 16)
                for u in range(2):
                    sp.dma_start(xres[:, u, :], xc_v[units[u][0], units[u][1]]).then_inc(s_res[u], 16)
                for u, (b, t) in enumerate(units):
                    if u >= 2:
                        sp.wait_ge(s_padded, 2 * (u - 1))
                    sp.dma_start(xin[:, u % 2, :], xn_v[b, t]).then_inc(s_xin[u % 2], 16)
                for u, (b, t) in enumerate(units):
                    sp.wait_ge(s_done, NCH * (u + 1))
                    sp.dma_start(out_v[b, t], xres[:, u % 2, :]).then_inc(s_out[u % 2], 16)
                    if u + 2 < len(units):
                        sp.wait_ge(s_out[u % 2], 16 * (u // 2 + 1))
                        sp.dma_start(xres[:, u % 2, :], xc_v[units[u + 2][0], units[u + 2][1]])\
                          .then_inc(s_res[u % 2], 16)
                for r in range(2):
                    sp.wait_ge(s_out[r], 16 * (len(units) // 2))

            @block.gpsimd
            def _(pool):
                pool.memset(pad[:, :, :, :], 0.0).then_inc(s_zero, 1)
                pool.memset(pad2[:, :, :, :], 0.0).then_inc(s_zero, 1)
                for u, (b, t) in enumerate(units):
                    q = pad2[:, u % 2, :, :]
                    pool.wait_ge(s_padded, 2 * u + 2)
                    if u:
                        pool.wait_ge(s_sum2, u)
                    pool.tensor_tensor(pair2[:, :, :], q[:, :, 0:WP - 1], q[:, :, 1:WP], ALU.add).then_inc(s_pool, 1)
                    pool.wait_ge(s_pool, 2 * u + 1)
                    pool.tensor_tensor(s2[:, :, :], pair2[:, :, 0:W], pair2[:, :, 2:W + 2], ALU.add).then_inc(s_pool, 1)
                    pool.wait_ge(s_pool, 2 * u + 2)
                    if b:
                        pool.wait_ge(s_pe, CT * NCH * b)
                    pool.tensor_tensor(den[:, t, :].rearrange("p (h w) -> p h w", w=W), s2[:, :, :],
                                       q[:, :, 4:W + 4], ALU.add).then_inc(s_sum2, 1)

            @block.scalar
            def _(act):
                act.wait_ge(s_zero, 2)

                def square(u):
                    b, t = units[u]
                    act.wait_ge(s_sum1, u + 1)
                    if b:
                        act.wait_ge(s_pe, CT * NCH * b)
                    act.activation(num[:, t, :].rearrange("p (h w) -> p h w", w=W), s1[:, :, :],
                                   ACT.Square).then_inc(s_num, 1)

                for u, (b, t) in enumerate(units):
                    x = xin[:, u % 2, :].rearrange("p (h w) -> p h w", w=W)
                    act.wait_ge(s_xin[u % 2], 16 * (u // 2) + 16)
                    if u >= 2:
                        act.wait_ge(s_sum1, u - 1)
                        act.wait_ge(s_sum2, u - 1)
                    act.activation(pad[:, u % 2, :, LO:LO + W], x, ACT.Copy).then_inc(s_padded, 1)
                    act.activation(pad2[:, u % 2, :, LO:LO + W], x, ACT.Square).then_inc(s_padded, 1)
                    if u:
                        square(u - 1)
                square(len(units) - 1)

            @block.tensor
            def _(pe):
                pe.wait_ge(s_band, 32)
                n = 0
                for b in range(B):
                    pe.wait_ge(s_num, CT * (b + 1))
                    pe.wait_ge(s_sum2, CT * (b + 1))
                    for o in range(CT):
                        for c in range(NCH):
                            if n >= 2:
                                pe.wait_ge(s_div, n - 1)
                            for ps, src in ((psn, num), (psd, den)):
                                for t in near[o]:
                                    last = pe.matmul(ps[n % 2][:, :], bandm[:, t, o * 128:(o + 1) * 128],
                                                     src[:, t, c * CW:(c + 1) * CW],
                                                     start=t == near[o][0], stop=t == near[o][-1])
                            last.then_inc(s_pe, 1)
                            n += 1

            @block.vector
            def _(dve):
                chain = [0]

                def link(ins):
                    chain[0] += 1
                    ins.then_inc(s_link, 1)
                    dve.wait_ge(s_link, chain[0])

                def sums(u):
                    q = pad[:, u % 2, :, :]
                    dve.wait_ge(s_padded, 2 * u + 2)
                    link(dve.tensor_tensor(pair[:, :, :], q[:, :, 0:WP - 1], q[:, :, 1:WP], ALU.add))
                    if u:
                        dve.wait_ge(s_num, u)
                    link(dve.tensor_tensor(s1[:, :, :], pair[:, :, 0:W], pair[:, :, 2:W + 2], ALU.add))
                    dve.tensor_tensor(s1[:, :, :], s1[:, :, :], q[:, :, 4:W + 4], ALU.add).then_inc(s_sum1, 1)
                    dve.wait_ge(s_sum1, u + 1)

                def divide(u, c, n):
                    if n == 0:
                        dve.wait_ge(s_band, 32)
                    res = xres[:, u % 2, c * CW:(c + 1) * CW]
                    dve.wait_ge(s_pe, n + 1)
                    link(dve.tensor_tensor(dn[:, :], psd[n % 2][:, :], normt[:, :, :].rearrange("p r w -> p (r w)"),
                                           ALU.mult))
                    link(dve.tensor_tensor(both[:, :], psn[n % 2][:, :], dn[:, :], ALU.add))
                    link(dve.tensor_scalar(none[:, :], both[:, :], 0.0, None, ALU.is_equal))
                    dve.tensor_tensor(dn[:, :], dn[:, :], none[:, :], ALU.add).then_inc(s_link, 1)
                    chain[0] += 1
                    dve.tensor_tensor(top[:, :], psn[n % 2][:, :], none[:, :], ALU.add).then_inc(s_div, 1)
                    dve.wait_ge(s_link, chain[0])
                    link(dve.reciprocal(rec[:, :], dn[:, :]))
                    dve.wait_ge(s_div, n + 1)
                    link(dve.tensor_tensor(top[:, :], top[:, :], rec[:, :], ALU.mult))
                    dve.scalar_tensor_tensor(res, top[:, :], MAX_F32, res, ALU.min, ALU.add).then_inc(s_done, 1)
                    dve.wait_ge(s_done, n + 1)

                for b in range(B):
                    for t in range(CT):
                        sums(CT * b + t)
                    for o in range(CT):
                        u = CT * b + o
                        dve.wait_ge(s_res[u % 2], 16 * (u // 2) + 16)
                        for c in range(NCH):
                            divide(u, c, NCH * u + c)


SWP = 384
NCP = L // SWP


def pairs(eng, n, body, peel=False):
    if peel:
        for r in range(2):
            body(r, 0, r)
    with eng.Fori(1 if peel else 0, n // 2) as i:
        for r in range(2):
            body(2 * i + r, i, r)


def project_split(nc, tag, xn, w, scale, bias, parts, plain):
    with Phase(nc, f"ps{tag}") as ph:
        x = ph.sb("x", [128, CT, T])
        wt = ph.sb("wt", [128, 2, CT, 128])
        sc = ph.sb("sc", [128, 2 * CT])
        bi = ph.sb("bi", [128, 2 * CT])
        y = ph.sb("y", [128, 2, B, L])
        p = [ph.sb(f"p{a}", [128, 2, B, L], BF16) for a in range(3)]
        rest = ph.sb("rest", [128, 2, SWP])
        ps = [ph.psum(f"ps{r}", [128, SWP]) for r in range(2)]
        s_aff, s_mm, s_y, s_p0, s_rest, s_p1, s_p2 = (
            ph.sem(n) for n in "affine matmul y part0 rest part1 part2".split())
        s_x = [ph.sem(f"x{t}") for t in range(CT)]
        s_w = [ph.sem(f"w{r}") for r in range(2)]
        s_stored = [[ph.sem(f"stored{r}{b}") for b in range(B)] for r in range(2)]
        NB = B * NCP
        JOBS = 2 * CT
        w_v = w.rearrange("(t p) (j m) -> j p t m", p=128, m=128)
        parts_v = parts.rearrange("a (s b t p) n -> s t b a p n", s=2, b=B, p=128)
        plain_v = plain.rearrange("(s b t p) n -> s t b p n", s=2, b=B, p=128)

        with nc.Block() as block:

            @block.sync
            def _(sp):
                sp.dma_start(sc[:, :], scale).then_inc(s_aff, 16)
                sp.dma_start(bi[:, :], bias).then_inc(s_aff, 16)
                for r in range(2):
                    sp.dma_start(wt[:, r, :, :], w_v[r]).then_inc(s_w[r], 16)
                for t in range(CT):
                    sp.dma_start(x[:, t, :], xn.rearrange("(t p) n -> t p n", p=128)[t]).then_inc(s_x[t], 16)

                def body(j, i, r):
                    if not (isinstance(j, int) and j == 0):
                        sp.wait_ge(s_mm, NB * j)
                        sp.dma_start(wt[:, 1 - r, :, :], w_v[j + 1]).then_inc(s_w[1 - r], 16)
                    for b in range(B):
                        sp.wait_ge(s_p2, NB * j + NCP * (b + 1))
                        sp.dma_start(plain_v[j // CT, j % CT, b], y[:, r, b, :]).then_inc(s_stored[r][b], 16)
                        for a in range(3):
                            sp.dma_start(parts_v[j // CT, j % CT, b, a], p[a][:, r, b, :]).then_inc(s_stored[r][b], 16)

                pairs(sp, JOBS, body, peel=True)
                for r in range(2):
                    for b in range(B):
                        sp.wait_ge(s_stored[r][b], 64 * (JOBS // 2))
                sp.wait_ge(s_w[0], 16 * (JOBS // 2 + 1))

            @block.tensor
            def _(pe):
                for t in range(CT):
                    pe.wait_ge(s_x[t], 16)

                def body(j, i, r):
                    pe.wait_ge(s_w[r], 16 * i + 16)
                    for c in range(NB):
                        pe.wait_ge(s_y, NB * j + (c + 1))
                        for t in range(CT):
                            last = pe.matmul(ps[c % 2][:, :], wt[:, r, t, :], x[:, t, c * SWP:(c + 1) * SWP],
                                             start=t == 0, stop=t == CT - 1)
                        last.then_inc(s_mm, 1)

                pairs(pe, JOBS, body)

            @block.vector
            def _(dve):
                dve.sem_inc(s_y, 2)
                dve.wait_ge(s_aff, 32)

                def plain_chunk(j, i, r, c):
                    b, k = c // NCP, c % NCP
                    if k == 0 and not (isinstance(i, int) and i == 0):
                        dve.wait_ge(s_stored[r][b], 64 * i)
                    dve.wait_ge(s_mm, NB * j + (c + 1))
                    dve.tensor_scalar(y[:, r, b, k * SWP:(k + 1) * SWP], ps[c % 2][:, :], cols(bi[:, :], 1)[:, j, :],
                                      cols(sc[:, :], 1)[:, j, :], ALU.add, ALU.mult).then_inc(s_y, 1)

                def rest_chunk(j, r, c):
                    b, k = c // NCP, c % NCP
                    dve.wait_ge(s_p0, NB * j + (c + 1))
                    if c >= 2 or not (isinstance(j, int) and j == 0):
                        dve.wait_ge(s_p2, NB * j + (c - 1))
                    dve.tensor_tensor(rest[:, c % 2, :], y[:, r, b, k * SWP:(k + 1) * SWP],
                                      p[0][:, r, b, k * SWP:(k + 1) * SWP], ALU.subtract).then_inc(s_rest, 1)

                def body(j, i, r):
                    plain_chunk(j, i, r, 0)
                    for c in range(NB):
                        if c + 1 < NB:
                            plain_chunk(j, i, r, c + 1)
                        rest_chunk(j, r, c)

                pairs(dve, JOBS, body, peel=True)

            @block.scalar
            def _(act):
                def body(j, i, r):
                    for c in range(NB):
                        b, k = c // NCP, c % NCP
                        part = slice(k * SWP, (k + 1) * SWP)
                        act.wait_ge(s_y, NB * j + (c + 3))
                        act.activation(p[0][:, r, b, part], y[:, r, b, part], ACT.Copy).then_inc(s_p0, 1)
                        act.wait_ge(s_rest, NB * j + (c + 1))
                        act.activation(p[1][:, r, b, part], rest[:, c % 2, :], ACT.Copy).then_inc(s_p1, 1)

                pairs(act, JOBS, body)

            @block.gpsimd
            def _(pool):
                def body(j, i, r):
                    for c in range(NB):
                        b, k = c // NCP, c % NCP
                        part = slice(k * SWP, (k + 1) * SWP)
                        pool.wait_ge(s_p1, NB * j + (c + 1))
                        pool.tensor_tensor(p[2][:, r, b, part], rest[:, c % 2, :], p[1][:, r, b, part],
                                           ALU.subtract).then_inc(s_p2, 1)

                pairs(pool, JOBS, body)


def tiles(eng, body, peel=False):
    for b in range(B):
        first = 1 if peel and b == 0 else 0
        if first:
            for r in range(2):
                body(b, 0, r)
        with eng.Fori(first, QT // 2) as i:
            for r in range(2):
                body(b, i, r)


def values(nc, tag, xn, w, bias, v, nh, dh):
    with Phase(nc, f"va{tag}") as ph:
        x = ph.sb("x", [128, CT, T])
        wt = ph.sb("wt", [128, CT, C])
        bi = ph.sb("bi", [128, C])
        xs = ph.sb("xs", [128, 2, CT, 128])
        vs = ph.sb("vs", [128, 2, C])
        ps = [ph.psum(f"ps{r}", [128, C]) for r in range(2)]
        s_w, s_xs, s_mm, s_vs = (ph.sem(n) for n in "w xs matmul vs".split())
        s_x = [ph.sem(f"x{b}") for b in range(B)]
        s_out = [ph.sem(f"out{r}") for r in range(2)]
        x_t = x[:, :, :].rearrange("p t (b n w) -> p t b n w", w=128, b=B)
        v_v = v.rearrange("(b h) p t d -> b t p h d", b=B)

        with nc.Block() as block:

            @block.sync
            def _(sp):
                sp.dma_start(wt[:, :, :], w.rearrange("(t p) m -> p t m", p=128)[:, :, 2 * C:3 * C])\
                  .then_inc(s_w, 16)
                sp.dma_start(bi[:, :], bias.partition_broadcast(128)).then_inc(s_w, 16)
                for b in range(B):
                    sp.dma_start(x[:, :, b * L:(b + 1) * L],
                                 xn.rearrange("(t p) (b n) -> b p t n", p=128, b=B)[b]).then_inc(s_x[b], 16)

                def body(b, i, r):
                    sp.wait_ge(s_vs, QT * b + 2 * i + (r + 3))
                    sp.dma_start(v_v[b, 2 * i + r], vs[:, r, :].rearrange("p (h d) -> p h d", d=dh))\
                      .then_inc(s_out[r], 16)

                tiles(sp, body)
                for r in range(2):
                    sp.wait_ge(s_out[r], 16 * (B * QT // 2))

            @block.gpsimd
            def _(pool):
                def body(b, i, r):
                    pool.wait_ge(s_x[b], 16)
                    pool.wait_ge(s_mm, QT * b + 2 * i + (r + 1))
                    pool.tensor_copy(xs[:, r, :, :], x_t[:, :, b, 2 * i + r, :]).then_inc(s_xs, 1)

                tiles(pool, body)

            @block.tensor
            def _(pe):
                pe.sem_inc(s_mm, 2)
                pe.wait_ge(s_w, 32)

                def body(b, i, r):
                    n = QT * b + 2 * i
                    pe.wait_ge(s_xs, n + (r + 1))
                    pe.wait_ge(s_vs, n + (r + 1))
                    for t in range(CT):
                        last = pe.matmul(ps[r][:, :], xs[:, r, t, :], wt[:, t, :], start=t == 0, stop=t == CT - 1)
                    last.then_inc(s_mm, 1)

                tiles(pe, body)

            @block.vector
            def _(dve):
                dve.sem_inc(s_vs, 2)
                dve.wait_ge(s_w, 32)

                def body(b, i, r):
                    dve.wait_ge(s_mm, QT * b + 2 * i + (r + 3))
                    if b or not isinstance(i, int):
                        dve.wait_ge(s_out[r], 16 * (QT // 2 * b + i))
                    dve.tensor_tensor(vs[:, r, :], ps[r][:, :], bi[:, :], ALU.add).then_inc(s_vs, 1)

                tiles(dve, body, peel=True)


def project_out(nc, tag, att, w, bias, xc, out, sums=None, inverse=None):
    with Phase(nc, f"po{tag}") as ph:
        a = ph.sb("a", [128, CT, B, L])
        x = ph.sb("x", [128, CT, B, L])
        wt = ph.sb("wt", [128, CT, C])
        bi = ph.sb("bi", [128, CT])
        ps = [ph.psum(f"ps{r}", [128, SWP]) for r in range(2)]
        s_w, s_mm, s_sum, s_out = (ph.sem(n) for n in "w matmul sum out".split())
        s_a = [ph.sem(f"a{b}") for b in range(B)]
        s_x = [ph.sem(f"x{b}") for b in range(B)]
        NB = CT * NCP
        if sums is not None:
            nhb = sums.shape[0]
            rows = B * C // nhb
            zin = ph.sb("zin", [128, nhb * L // 128])
            zrec = ph.sb("zrec", [128, nhb * L // 128])
            inv = ph.sb("inv", [128, CT, B, L])
            s_zin, s_zrec, s_zout, s_scaled = (ph.sem(n) for n in "zin zrec zout scaled".split())
            s_inv = [ph.sem(f"inv{b}") for b in range(B)]
        att_v = att.rearrange("(b t p) n -> b p t n", b=B, p=128)
        xc_v, out_v = (z.rearrange("(t p) (b n) -> b p t n", p=128, b=B) for z in (xc, out))

        with nc.Block() as block:

            @block.sync
            def _(sp):
                if sums is not None:
                    sp.dma_start(zin[:, :], sums.rearrange("h n -> (h n)").rearrange("(p q) -> p q", p=128)).then_inc(s_zin, 16)
                sp.dma_start(wt[:, :, :], w.rearrange("(t p) m -> p t m", p=128)).then_inc(s_w, 16)
                sp.dma_start(bi[:, :], bias.rearrange("(t p) -> p t", p=128),
                             allow_slow_non_contiguous=True).then_inc(s_w, 16)
                if sums is not None:
                    sp.wait_ge(s_zrec, 1)
                    sp.dma_start(inverse.rearrange("h n -> (h n)").rearrange("(p q) -> p q", p=128), zrec[:, :])\
                      .then_inc(s_zout, 16)
                    sp.wait_ge(s_zout, 16)
                for b in range(B):
                    sp.dma_start(a[:, :, b, :], att_v[b]).then_inc(s_a[b], 16)
                    if sums is not None:
                        for h in range(nhb // B):
                            at = h * rows
                            sp.dma_start(inv[at % 128:at % 128 + rows, at // 128, b, :],
                                         inverse[nhb // B * b + h].partition_broadcast(rows)).then_inc(s_inv[b], 16)
                    sp.dma_start(x[:, :, b, :], xc_v[b]).then_inc(s_x[b], 16)
                for b in range(B):
                    sp.wait_ge(s_sum, NB * (b + 1) + 2)
                    sp.dma_start(out_v[b], x[:, :, b, :]).then_inc(s_out, 16)
                sp.wait_ge(s_out, 16 * B)

            def chunks(eng, body):
                for b in range(B):
                    with eng.Fori(0, NCP // 2) as i:
                        for m in range(2 * CT):
                            body(b, i, m)

            @block.tensor
            def _(pe):
                pe.wait_ge(s_w, 32)

                def body(b, i, m):
                    if m == 0:
                        pe.wait_ge(s_a[b], 16)
                        if sums is not None:
                            pe.wait_ge(s_scaled, CT * (b + 1))
                    o = m % CT
                    pe.wait_ge(s_sum, NB * b + 2 * CT * i + (m + 1))
                    for t in range(CT):
                        last = pe.matmul(ps[m % 2][:, :], wt[:, t, o * 128:(o + 1) * 128],
                                         cols(a[:, t, b, :], SWP)[:, 2 * i + m // CT, :],
                                         start=t == 0, stop=t == CT - 1)
                    last.then_inc(s_mm, 1)

                chunks(pe, body)

            @block.vector
            def _(dve):
                dve.sem_inc(s_sum, 2)
                dve.wait_ge(s_w, 32)

                if sums is not None:
                    dve.wait_ge(s_zin, 16)
                    dve.reciprocal(zrec[:, :], zin[:, :]).then_inc(s_zrec, 1)
                    for b in range(B):
                        dve.wait_ge(s_a[b], 16)
                        dve.wait_ge(s_inv[b], 16 * nhb // B)
                        for t in range(CT):
                            dve.tensor_tensor(a[:, t, b, :], a[:, t, b, :], inv[:, t, b, :],
                                              ALU.mult).then_inc(s_scaled, 1)

                def body(b, i, m):
                    if m == 0:
                        dve.wait_ge(s_x[b], 16)
                    o = m % CT
                    xo = cols(x[:, o, b, :], SWP)[:, 2 * i + m // CT, :]
                    new = ps[m % 2][:, :]
                    pieces = [(xo, new)]
                    if sums is not None:
                        old = xo.rearrange("p (y b x) -> p y b x", b=NBX, y=BY)
                        pieces = [(old[:, :, k], rows_first(new)[:, :, k]) for k in range(NBX)]
                    dve.wait_ge(s_mm, NB * b + 2 * CT * i + (m + 1))
                    for old, new in pieces:
                        last = dve.scalar_tensor_tensor(old, new, bi[:, o:o + 1], old, ALU.add, ALU.add)
                    last.then_inc(s_sum, 1)

                chunks(dve, body)


def group_weights(nc, q, gpd, t_param, parts, ident):
    HP = NH1 * GP // 2
    TG = 4 * GP
    N = B * QT
    with Phase(nc, "gw") as ph:
        gp = ph.sb("gp", [128, CT, TG])
        idn = ph.sb("idn", [128, 128])
        qs = ph.sb("qs", [128, 2, CT, 128])
        tv, mt, et, lt, st, dt, rt = (ph.sb(f"t{i}", [128, 1]) for i in range(7))
        small = ph.sb("small", [128, 1], mybir.dt.uint32)
        top = ph.sb("top", [128, 2, NH1])
        d = ph.sb("d", [128, 2, NH1, GP])
        e = ph.sb("e", [128, 2, NH1, GP])
        s = ph.sb("s", [128, NH1])
        r_s = ph.sb("r_s", [128, NH1])
        g = ph.sb("g", [128, 2, NH1, GP])
        rest = ph.sb("rest", [HP, 2, 128])
        p = [ph.sb(f"p{a}", [HP, 2, T], BF16) for a in range(3)]
        ps = [ph.psum(f"ps{r}", [128, NH1, GP]) for r in range(2)]
        pt = [ph.psum(f"pt{r}", [128, 2, 128]) for r in range(2)]
        (s_c, s_t, s_tlink, s_tact, s_log, s_top, s_d, s_e, s_s, s_rs, s_g, s_turn, s_p0, s_rest, s_p1, s_p2) = (
            ph.sem(n) for n in ("const t tlink tact logits top d exp sum rsum g turned part0 rest part1 "
                                "part2").split())
        s_q = [ph.sem(f"q{r}") for r in range(2)]
        s_out = ph.sem("out")
        q_v = q.rearrange("(b c p) (t w) -> b t p c w", b=B, p=128, w=128)
        out_v = parts.rearrange("a (b f p) n -> a f p b n", b=B, f=2)

        def at(a, n):
            return p[a][:, :, :].rearrange("p f (n w) -> p f n w", w=128)[:, :, n, :]

        def staggered(eng, front, back):
            front(0, 0, 0)
            with eng.Fori(0, N // 2 - 1) as i:
                front(2 * i + 1, i, 1)
                back(2 * i, i, 0)
                front(2 * i + 2, i + 1, 0)
                back(2 * i + 1, i, 1)
            front(N - 1, N // 2 - 1, 1)
            back(N - 2, N // 2 - 1, 0)
            back(N - 1, N // 2 - 1, 1)

        with nc.Block() as block:

            @block.sync
            def _(sp):
                sp.dma_start(gp[:, :, :], gpd).then_inc(s_c, 16)
                sp.dma_start(idn[:, :], ident).then_inc(s_c, 16)
                sp.dma_start(tv[:, :], t_param.partition_broadcast(128)).then_inc(s_c, 16)

                def body(n, i, r):
                    sp.wait_ge(s_log, n + 1)
                    sp.dma_start(qs[:, r, :, :], q_v[n // QT, n % QT]).then_inc(s_q[r], 16)

                pairs(sp, N, body)
                sp.wait_ge(s_p2, N + 1)
                for a in range(3):
                    for f in range(2):
                        sp.dma_start(out_v[a, f], p[a][:, f, :].rearrange("p (b n) -> p b n", b=B)).then_inc(s_out, 16)
                sp.wait_ge(s_out, 96)

            @block.tensor
            def _(pe):
                pe.sem_inc(s_log, 2)
                pe.wait_ge(s_c, 48)

                def logits(n, i, r):
                    pe.wait_ge(s_q[r], 16 * i + 16)
                    pe.wait_ge(s_d, n + 1)
                    for c in range(CT):
                        last = pe.matmul(ps[r][:, 4 * c:4 * c + 4, :], qs[:, r, c, :], gp[:, c, :],
                                         start=True, stop=True, skip_group_check=True)
                    last.then_inc(s_log, 1)

                def turn(n, i, r):
                    pe.wait_ge(s_g, n + 1)
                    pe.wait_ge(s_rest, n + 1)
                    for f in range(2):
                        last = pe.transpose(pt[r][0:HP, f, :], g[:, r, f * NH1 // 2:(f + 1) * NH1 // 2, :]
                                            .rearrange("p h m -> p (h m)"), idn[:, :])
                    last.then_inc(s_turn, 1)

                staggered(pe, logits, turn)

            @block.vector
            def _(dve):
                chain = [0]
                dve.sem_inc(s_d, 2)
                dve.sem_inc(s_rest, 2)

                def link(ins):
                    chain[0] += 1
                    ins.then_inc(s_tlink, 1)
                    dve.wait_ge(s_tlink, chain[0])

                dve.wait_ge(s_tact, 3)
                link(dve.tensor_scalar(st[:, :], et[:, :], -0.25, None, ALU.mult))
                for coefficient in (1 / 3, -1 / 2, 1.0):
                    link(dve.scalar_tensor_tensor(st[:, :], st[:, :], coefficient, et[:, :], ALU.add, ALU.mult))
                link(dve.tensor_scalar(small[:, :], et[:, :], 0.015625, None, ALU.is_lt))
                link(dve.copy_predicated(lt[:, :], small[:, :], st[:, :]))
                link(dve.scalar_tensor_tensor(dt[:, :], tv[:, :], 0.0, lt[:, :], ALU.max, ALU.add))
                dve.reciprocal(rt[:, :], dt[:, :]).then_inc(s_t, 1)

                def front(n, i, r):
                    dve.wait_ge(s_log, n + 3)
                    dve.tensor_reduce(top[:, r, :], ps[r][:, :, :], AX.X, ALU.max).then_inc(s_top, 1)
                    dve.wait_ge(s_top, n + 1)
                    dve.tensor_tensor(d[:, r, :, :], ps[r][:, :, :],
                                      top[:, r, :].unsqueeze(2).to_broadcast([128, NH1, GP]),
                                      ALU.subtract).then_inc(s_d, 1)

                def back(n, i, r):
                    dve.wait_ge(s_e, n + 1)
                    dve.tensor_reduce(s[:, :], e[:, r, :, :], AX.X, ALU.add).then_inc(s_s, 1)
                    dve.wait_ge(s_s, n + 1)
                    dve.reciprocal(r_s[:, :], s[:, :]).then_inc(s_rs, 1)
                    dve.wait_ge(s_rs, n + 1)
                    dve.tensor_tensor(g[:, r, :, :], e[:, r, :, :],
                                      r_s[:, :].unsqueeze(2).to_broadcast([128, NH1, GP]), ALU.mult).then_inc(s_g, 1)
                    dve.wait_ge(s_p0, n + 1)
                    dve.wait_ge(s_p2, n + 1)
                    dve.tensor_tensor(rest[:, :, :], pt[r][0:HP, :, :], at(0, n), ALU.subtract).then_inc(s_rest, 1)

                staggered(dve, front, back)

            @block.scalar
            def _(act):
                act.wait_ge(s_c, 48)
                act.activation(mt[:, :], tv[:, :], ACT.Abs).then_inc(s_tact, 1)
                act.wait_ge(s_tact, 1)
                act.activation(et[:, :], mt[:, :], ACT.Exp, scale=-1.0).then_inc(s_tact, 1)
                act.wait_ge(s_tact, 2)
                act.activation(lt[:, :], et[:, :], ACT.Ln, bias=1.0).then_inc(s_tact, 1)
                act.wait_ge(s_t, 1)

                def front(n, i, r):
                    act.wait_ge(s_d, n + 3)
                    act.activation(e[:, r, :, :], d[:, r, :, :], ACT.Exp, scale=rt[:, :]).then_inc(s_e, 1)

                def back(n, i, r):
                    act.wait_ge(s_turn, n + 1)
                    act.activation(at(0, n), pt[r][0:HP, :, :], ACT.Copy).then_inc(s_p0, 1)
                    act.wait_ge(s_rest, n + 3)
                    act.activation(at(1, n), rest[:, :, :], ACT.Copy).then_inc(s_p1, 1)

                staggered(act, front, back)

            @block.gpsimd
            def _(pool):
                pool.sem_inc(s_p2, 1)

                def body(n, i, r):
                    pool.wait_ge(s_p1, n + 1)
                    pool.tensor_tensor(at(2, n), rest[:, :, :], at(1, n), ALU.subtract).then_inc(s_p2, 1)

                pairs(pool, N, body)


def relative(nc, q, relw, rel_w, rel_h):
    N = B * NH3
    with Phase(nc, "re") as ph:
        rel = ph.sb("rel", [D3, 2, 2 * H - 1])
        qs = ph.sb("qs", [D3, 2, L])
        p = [[ph.sb(f"p{a}{r}", [H, 2, L], BF16) for a in range(3)] for r in range(2)]
        rest = ph.sb("rest", [H, 2, 8, H])
        ps = [ph.psum(f"ps{r}", [H, 8, H]) for r in range(2)]
        s_rel, s_mm, s_p0, s_rest, s_p1, s_p2 = (ph.sem(n) for n in "rel matmul part0 rest part1 part2".split())
        s_begun = ph.sem("begun")
        s_q = [ph.sem(f"q{r}") for r in range(2)]
        s_out = [ph.sem(f"out{r}") for r in range(2)]
        NC = 12
        STORES = 3 * (NBX + 2)

        def by_column(ap):
            return ap.rearrange("p (r b y x) -> p b x r y", b=NBX, y=BY, x=BX)

        def at(r, a, m):
            if m < NC // 2:
                return rows_first(p[r][a][:, 0, m * BROW:(m + 1) * BROW])
            c = m - NC // 2
            return by_column(p[r][a][:, 1, :])[:, c // 2, 8 * (c % 2):8 * (c % 2) + 8]

        def of(ap, m):
            return ap.rearrange("p k (b x) -> p k b x", b=NBX) if m < NC // 2 else \
                ap.rearrange("p k (r y) -> p k r y", y=BY)

        with nc.Block() as block:

            @block.sync
            def _(sp):
                sp.dma_start(rel[:, :, :], relw).then_inc(s_rel, 16)
                q_v = q.rearrange("(h d) n -> h d n", d=D3)
                for r in range(2):
                    sp.dma_start(qs[:, r, :], q_v[r]).then_inc(s_q[r], 16)

                def body(h, i, r, more=True):
                    sp.wait_ge(s_p2, NC * h + NC)
                    for a in range(3):
                        for bx in range(NBX):
                            sp.dma_start(rel_w[h, bx, BX * a:BX * (a + 1), :], p[r][a][BX * bx:BX * (bx + 1), 1, :])\
                              .then_inc(s_out[r], 16)
                        for half in range(2):
                            n = HALF * BY
                            sp.dma_start(rel_h[h, half, n * a:n * (a + 1), :], p[r][a][n * half:n * (half + 1), 0, :])\
                              .then_inc(s_out[r], 16)
                    if more:
                        sp.dma_start(qs[:, r, :], q_v[h + 2]).then_inc(s_q[r], 16)

                pairs(sp, N - 2, body)
                for r in range(2):
                    body(N - 2 + r, N // 2 - 1, r, False)
                for r in range(2):
                    sp.wait_ge(s_out[r], 16 * STORES * (N // 2))

            @block.tensor
            def _(pe):
                pe.wait_ge(s_rel, 16)

                def body(h, i, r):
                    pe.wait_ge(s_q[r], 16 * i + 16)
                    for m in range(NC):
                        s = m // (NC // 2)
                        pe.wait_ge(s_rest, NC * h + (m + 1))
                        pe.sem_inc(s_begun, 1)
                        for k in range(8):
                            pos = 8 * (m % (NC // 2)) + k
                            at_q = rows_first(qs[:, r, m * BROW:(m + 1) * BROW])[:, k] if s == 0 else \
                                by_column(qs[:, r, :])[:, pos // BX, pos % BX]
                            last = pe.matmul(of(ps[m % 2][:, :, :], m)[:, k], rel[:, s, H - 1 - pos:2 * H - 1 - pos], at_q,
                                             start=True, stop=True, skip_group_check=True)
                        last.then_inc(s_mm, 1)

                pairs(pe, N, body)

            @block.scalar
            def _(act):
                def body(h, i, r):
                    if not (isinstance(i, int) and i == 0):
                        act.wait_ge(s_out[r], 16 * STORES * i)
                    for m in range(NC):
                        act.wait_ge(s_mm, NC * h + (m + 1))
                        act.activation(at(r, 0, m), of(ps[m % 2][:, :, :], m), ACT.Copy).then_inc(s_p0, 1)
                        act.wait_ge(s_rest, NC * h + (m + 3))
                        act.activation(at(r, 1, m), of(rest[:, m % 2, :, :], m),
                                       ACT.Copy).then_inc(s_p1, 1)

                pairs(act, N, body, peel=True)

            @block.vector
            def _(dve):
                dve.sem_inc(s_rest, 2)

                def body(h, i, r):
                    for m in range(NC):
                        dve.wait_ge(s_p0, NC * h + (m + 1))
                        if m >= 2 or not (isinstance(i, int) and i == 0 and r == 0):
                            dve.wait_ge(s_p2, NC * h + (m - 1))
                        dve.tensor_tensor(of(rest[:, m % 2, :, :], m), of(ps[m % 2][:, :, :], m),
                                          at(r, 0, m), ALU.subtract).then_inc(s_rest, 1)

                pairs(dve, N, body, peel=True)

            @block.gpsimd
            def _(pool):
                def body(h, i, r):
                    for m in range(NC):
                        pool.wait_ge(s_p1, NC * h + (m + 1))
                        pool.tensor_tensor(at(r, 2, m), of(rest[:, m % 2, :, :], m), at(r, 1, m),
                                           ALU.subtract).then_inc(s_p2, 1)

                pairs(pool, N, body)


class Head:

    def __init__(self, n, buf, turn):
        self.n, self.buf, self.turn = n, buf, turn


def in_heads(eng, n, first, step, last):
    def step_at(i, u, rolled):
        s = 3 * i + u
        step(Head(s + 1, (u + 1) % 3, i + (u + 1) // 3), Head(s, u, i), rolled)

    first(Head(0, 0, 0))
    rounds = (n - 1) // 3
    with eng.Fori(0, rounds) as i:
        for u in range(3):
            step_at(i, u, True)
    for u in range(n - 1 - 3 * rounds):
        step_at(rounds, u, False)
    last(Head(n - 1, (n - 1) % 3, (n - 1) // 3))


def gated_attention(nc, nhb, dh, loads, score_sets, gate, v_dram, att_out, bias_dram, identb):
    SW = 384
    NC = L // SW
    AHEAD = 6
    CHUNKS = QT * NC
    G = 128 // dh
    OW = L // G
    NO = 2
    OS = OW // NO
    SCORE_A, SCORE_B, GATE, O_BANK = range(0, 2), range(2, 4), range(4, 6), 6
    NA = len(SCORE_A)
    EB = 4
    bias_rows = score_sets[0][2]
    with Phase(nc, "at1") as ph:
        ops = {n: ph.sb(n, [128, 3, L], BF16) for n in loads}
        v = ph.sb("v", [128, 3, QT, dh])
        idb = ph.sb("idb", [128, 128], BF16)
        junk = ph.sb("junk", [128, NA, SW], BF16)
        e = ph.sb("e", [128, EB, SW])
        w = ph.sb("w", [128, 2, L])
        vs = ph.sb("vs", [128, 2, dh])
        nmax = ph.sb("nmax", [128, QT, NC])
        zsum = ph.sb("zsum", [128, QT, NC])
        nm = ph.sb("nm", [128, QT])
        diff = ph.sb("diff", [128, QT, NC])
        ediff = ph.sb("ediff", [128, QT, NC])
        ze = ph.sb("ze", [128, QT, NC])
        z = ph.sb("z", [128, QT])
        lnz = ph.sb("lnz", [128, QT])
        bias = ph.sb("bias", [128, QT])
        rest = ph.sb("rest", [128, QT])
        bparts = ph.sb("bparts", [128, 128], BF16)
        bturned = ph.sb("bturned", [128, 128], BF16)
        dpart = ph.sb("dpart", [128, 2, NC])
        djunk = ph.sb("djunk", [128, 2, NC])
        zero = ph.sb("zero", [128, 2])
        dsum = ph.sb("dsum", [128, 2])
        drec = ph.sb("drec", [128, 2])
        osb = ph.sb("osb", [128, NO, OS])
        ps = ph.psum("ps", [128, 8, 512])
        (s_const, s_scored, s_max_taken, s_exped, s_diff, s_ediff, s_link, s_sum, s_log, s_bias_parts, s_turn, s_turned, s_bias_out,
         s_bias_row, s_keys_scored, s_gate, s_keys_exped, s_weighted, s_values, s_output, s_output_taken, s_stored, s_dsum, s_drec, s_output_stored, s_bias_stored, s_id,
         s_warm, s_begun, s_zero) = (ph.sem(n) for n in (
             "const scoresA maxed exped diff ediff link zsum lnz bparts turn turned biasout "
             "brow scoresB gate expB weighted vscaled outprod osb stored dsum drec ofree bfree id "
             "warm begun zero").split())
        s_ops = [ph.sem(f"ops{r}") for r in range(3)]
        n_loads = sum(len(x) for x in loads.values()) + 1
        tps = ps[:, :, :].bitcast(BF16)[:, SCORE_A[0], 0:128]

        def bank(first, c):
            return ps[:, first[c % len(first)], 0:SW]

        def nothing(*_):
            pass

        def steps(eng, pair, sums=nothing, logs=nothing, turn=nothing, flush=nothing, begin=nothing,
                  attend=nothing, end=nothing):
            def step(h, one, two):
                begin(h)
                if one:
                    sums(one)
                if h or two:
                    pair(h, 0, two, QT - AHEAD, False)
                if one:
                    logs(one)
                if h or two:
                    pair(h, 2, two, QT - AHEAD + 2, False)
                if one:
                    turn(one, h)
                if h or two:
                    pair(h, 4, two, QT - AHEAD + 4, False)
                if two:
                    flush(two)
                if h or one:
                    if one:
                        attend(one)
                    pair(h, AHEAD, one, 0, True)
                    with eng.Fori(1, (QT - AHEAD) // 2) as i:
                        pair(h, AHEAD + 2 * i, one, 2 * i, False)
                end(h, one, two)

            def head(n, i=0):
                return Head(n + 3 * i, n % 3, i + n // 3)

            step(head(0), None, None)
            step(head(1), head(0), None)
            rounds, left = (nhb - 2) // 3, (nhb - 2) % 3
            with eng.Fori(0, rounds) as i:
                for u in range(2, 5):
                    step(head(u, i), head(u - 1, i), head(u - 2, i))
            for u in range(nhb - left, nhb):
                step(head(u), head(u - 1), head(u - 2))
            step(None, head(nhb - 1), head(nhb - 2))
            step(None, None, head(nhb - 1))

        with nc.Block() as block:

            @block.sync
            def _(sp):
                sp.sem_inc(s_output_stored, 1)
                sp.sem_inc(s_bias_stored, 1)
                sp.dma_start(idb[:, :], identb).then_inc(s_id, 16)

                def load(s, r):
                    for name, parts in loads.items():
                        for dram, part, n, at in parts:
                            src = dram[part].rearrange("(h r) n -> h r n", r=n)[s]
                            sp.dma_start(ops[name][at:at + n, r, :], src).then_inc(s_ops[r], 16)
                    sp.dma_start(v[:, r, :, :], v_dram[s]).then_inc(s_ops[r], 16)

                def bias_row(h):
                    sp.wait_ge(s_turned, h.n + 1)
                    sp.dma_start(bias_dram, bturned[0:3 * QT, :]).then_inc(s_bias_out, 16)
                    sp.wait_ge(s_bias_out, 16 * h.n + 16)
                    sp.sem_inc(s_bias_stored, 1)
                    sp.dma_start(ops[score_sets[0][0]][bias_rows:bias_rows + 3, h.buf, :],
                                 bias_dram.rearrange("(a t) w -> a (t w)", a=3)).then_inc(s_bias_row, 16)
                    sp.wait_ge(s_bias_row, 16 * h.n + 16)

                def store(h):
                    sp.wait_ge(s_output_taken, h.n + 2)
                    dst = att_out.rearrange("(h d) (g n) -> h g d n", d=dh, g=G)[h.n]
                    for g in range(G):
                        sp.dma_start(dst[g], osb[g * dh:(g + 1) * dh, :, :].rearrange("p a b -> p (a b)"))\
                          .then_inc(s_stored, 16)
                    sp.wait_ge(s_stored, 16 * G * h.n + 16 * G)
                    sp.sem_inc(s_output_stored, 1)

                for r in range(3):
                    load(r, r)
                bias_row(Head(0, 0, 0))

                def step(one, two, more):
                    bias_row(one)
                    store(two)
                    if more:
                        load(two.n + 3, two.buf)

                rounds = (nhb - 3) // 3
                with sp.Fori(0, rounds) as i:
                    for u in range(3):
                        step(Head(3 * i + u + 1, (u + 1) % 3, None), Head(3 * i + u, u, None), True)
                for n in range(3 * rounds, nhb - 1):
                    step(Head(n + 1, (n + 1) % 3, None), Head(n, n % 3, None), n + 3 < nhb)
                store(Head(nhb - 1, (nhb - 1) % 3, None))

            @block.gpsimd
            def _(pool):
                for r in range(3):
                    pool.memset(ops[score_sets[0][1]][bias_rows:bias_rows + 3, r, :], 1.0).then_inc(s_const, 1)

            @block.tensor
            def _(pe):
                pe.sem_inc(s_output, 2)
                pe.wait_ge(s_id, 16)
                pe.wait_ge(s_const, 3)

                def product(out, lhs, rhs, rows, buf, tile, c, start, stop):
                    return pe.matmul(out, cols(ops[lhs][0:rows, buf, :], 128)[:, tile, :],
                                     ops[rhs][0:rows, buf, c * SW:(c + 1) * SW], start=start, stop=stop)

                def begin(h):
                    if h:
                        pe.wait_ge(s_ops[h.buf], 16 * n_loads * h.turn + 16 * n_loads)
                        pe.sem_inc(s_begun, 1)

                def score(h, t, c):
                    pe.wait_ge(s_exped, CHUNKS * h.n + NC * t + (c + 1))
                    for n, (q, k, rows) in enumerate(score_sets):
                        last = product(bank(SCORE_A, c), q, k, rows, h.buf, t, c, n == 0, n == len(score_sets) - 1)
                    last.then_inc(s_scored, 1)

                def keys(h, t, c):
                    pe.wait_ge(s_keys_exped, CHUNKS * h.n + NC * t + (c + 1))
                    for n, (q, k, rows) in enumerate(score_sets):
                        last = product(bank(SCORE_B, c), k, q, rows + (3 if n == 0 else 0), h.buf, t, c, n == 0,
                                       n == len(score_sets) - 1)
                    last.then_inc(s_keys_scored, 1)

                def weights(h, t, c):
                    pe.wait_ge(s_weighted, CHUNKS * h.n + NC * t + (c + 5 - len(GATE)))
                    product(bank(GATE, c), gate[1], gate[0], gate[2], h.buf, t, c, True, True).then_inc(s_gate, 1)

                def values(h, t, k, o, start=False, stop=False):
                    if o == 0:
                        pe.wait_ge(s_values, QT * h.n + t + 1)
                    for g in range(G):
                        last = pe.matmul(ps[g * dh:(g + 1) * dh, O_BANK + o, 0:OS], vs[:, k, :],
                                         w[:, k, g * OW + o * OS:g * OW + (o + 1) * OS],
                                         start=start, stop=stop, skip_group_check=True)
                    if o == NO - 1:
                        last.then_inc(s_output, 1)

                def pair(a, ta, b, tb, opening):
                    for k in range(2):
                        first = opening and k == 0
                        for c in range(NC):
                            if b:
                                keys(b, tb + k, c)
                            if a:
                                score(a, ta + k, c)
                            if b and c:
                                weights(b, tb + k, c - 1)
                            elif b and not first:
                                weights(b, tb + (k - 1), NC - 1)
                            if not b:
                                continue
                            if c >= NC - NO and not first:
                                if opening and c == NC - NO:
                                    pe.wait_ge(s_output_taken, b.n + 1)
                                values(b, tb + (k - 1), 1 - k, c - (NC - NO), start=opening)

                def turn(one, h):
                    pe.wait_ge(s_bias_parts, one.n + 1)
                    pe.wait_ge(s_exped, CHUNKS * (one.n + 1) + (4 * NC + NA if h else NA))
                    pe.transpose(tps, bparts[:, :], idb[:, :]).then_inc(s_turn, 1)
                    pe.wait_ge(s_turned, one.n + 1)

                def flush(two):
                    weights(two, QT - 1, NC - 1)
                    for o in range(NO):
                        values(two, QT - 1, 1, o, stop=True)

                def attend(one):
                    pe.wait_ge(s_bias_row, 16 * one.n + 16)

                steps(pe, pair, turn=turn, flush=flush, begin=begin, attend=attend)

            @block.scalar
            def _(act):
                act.sem_inc(s_exped, NA)
                act.sem_inc(s_keys_exped, 2)
                act.sem_inc(s_warm, 1)
                act.wait_ge(s_zero, 2)

                def pair(a, ta, b, tb, opening):
                    for k in range(2):
                        for c in range(NC):
                            if b:
                                n_b = CHUNKS * b.n + NC * (tb + k)
                                act.wait_ge(s_keys_scored, n_b + (c + 1))
                                act.wait_ge(s_weighted, n_b + (c + 1))
                                act.activation(e[:, (NC * k + c) % EB, :], bank(SCORE_B, c), ACT.Exp).then_inc(s_keys_exped, 1)
                            if a:
                                act.wait_ge(s_max_taken, CHUNKS * a.n + NC * (ta + k) + (c + 1))
                                act.activation(junk[:, c % NA, :], bank(SCORE_A, c), ACT.Exp,
                                               bias=nmax[:, ta + k, c:c + 1],
                                               accum_out=zsum[:, ta + k, c:c + 1]).then_inc(s_exped, 1)

                def sums(one):
                    act.wait_ge(s_diff, one.n + 1)
                    act.activation(ediff[:, :, :], diff[:, :, :], ACT.Exp).then_inc(s_ediff, 1)

                def logs(one):
                    act.wait_ge(s_sum, one.n + 1)
                    act.activation(lnz[:, :], z[:, :], ACT.Ln).then_inc(s_log, 1)
                    act.wait_ge(s_warm, one.n + 1)
                    act.activation(zero[:, 1:2], zero[:, 0:1], ACT.Exp).then_inc(s_warm, 1)

                def turn(one, h):
                    act.wait_ge(s_turn, one.n + 1)
                    act.wait_ge(s_bias_stored, one.n + 1)
                    act.activation(bturned[:, :], tps, ACT.Copy).then_inc(s_turned, 1)

                steps(act, pair, sums=sums, logs=logs, turn=turn)

            @block.vector
            def _(dve):
                dve.sem_inc(s_weighted, 4)
                dve.sem_inc(s_output_taken, 1)
                dve.memset(bparts[:, :], 0.0).then_inc(s_zero, 1)
                dve.memset(zero[:, :], 0.0).then_inc(s_zero, 1)
                dve.wait_ge(s_zero, 2)
                N_LINK = 6

                def link(h, n, ins):
                    ins.then_inc(s_link, 1)
                    dve.wait_ge(s_link, N_LINK * h.n + n)

                def weigh(h, t, k, c):
                    n_b = CHUNKS * h.n + NC * t + c
                    if c == 0:
                        dve.wait_ge(s_output, QT * h.n + t + 1)
                    dve.wait_ge(s_keys_exped, n_b + 3)
                    dve.wait_ge(s_gate, n_b + 1)
                    dve.scalar_tensor_tensor(w[:, k, c * SW:(c + 1) * SW], bank(GATE, c), 1.0,
                                             e[:, (NC * k + c) % EB, :], ALU.mult, ALU.mult,
                                             accum_out=dpart[:, k, c:c + 1]).then_inc(s_weighted, 1)

                def scale_values(h, t, k, step):
                    n_t = QT * h.n + t
                    if step == 0:
                        dve.wait_ge(s_weighted, NC * n_t + (NC + 4))
                        dve.tensor_scalar(djunk[:, k, :], dpart[:, k, :], 1.0, 1e-8, ALU.mult, ALU.add,
                                          accum_out=dsum[:, k:k + 1]).then_inc(s_dsum, 1)
                    elif step == 1:
                        dve.wait_ge(s_dsum, n_t + 1)
                        dve.reciprocal(drec[:, k:k + 1], dsum[:, k:k + 1]).then_inc(s_drec, 1)
                    else:
                        dve.wait_ge(s_drec, n_t + 1)
                        dve.tensor_scalar(vs[:, k, :], v[:, h.buf, t, :], drec[:, k:k + 1], None,
                                          ALU.mult).then_inc(s_values, 1)

                def pair(a, ta, b, tb, opening):
                    for k in range(2):
                        for c in range(NC):
                            if a:
                                dve.wait_ge(s_scored, CHUNKS * a.n + NC * (ta + k) + (c + 1))
                                dve.tensor_reduce(nmax[:, ta + k, c:c + 1], bank(SCORE_A, c), AX.X, ALU.max,
                                                  negate=True).then_inc(s_max_taken, 1)
                            if not b:
                                continue
                            first = opening and k == 0
                            if 0 < c <= 3 and not first:
                                scale_values(b, tb + (k - 1), 1 - k, c - 1)
                            if c:
                                weigh(b, tb + k, k, c - 1)
                            elif not first:
                                weigh(b, tb + (k - 1), 1 - k, NC - 1)

                def sums(one):
                    dve.wait_ge(s_exped, CHUNKS * (one.n + 1) + NA)
                    dve.wait_ge(s_max_taken, CHUNKS * (one.n + 1))
                    link(one, 1, dve.tensor_reduce(nm[:, :], nmax[:, :, :], AX.X, ALU.min))
                    dve.tensor_tensor(diff[:, :, :], nm[:, :].unsqueeze(2).to_broadcast([128, QT, NC]),
                                      nmax[:, :, :], ALU.subtract).then_inc(s_diff, 1)
                    dve.wait_ge(s_ediff, one.n + 1)
                    link(one, 2, dve.tensor_tensor(ze[:, :, :], zsum[:, :, :], ediff[:, :, :], ALU.mult))
                    dve.tensor_reduce(z[:, :], ze[:, :, :], AX.X, ALU.add).then_inc(s_sum, 1)

                def logs(one):
                    dve.wait_ge(s_log, one.n + 1)
                    link(one, 3, dve.tensor_tensor(bias[:, :], nm[:, :], lnz[:, :], ALU.subtract))
                    link(one, 4, dve.tensor_copy(bparts[:, 0 * QT:1 * QT], bias[:, :]))
                    link(one, 5, dve.tensor_tensor(rest[:, :], bias[:, :], bparts[:, 0 * QT:1 * QT], ALU.subtract))
                    link(one, 6, dve.tensor_copy(bparts[:, 1 * QT:2 * QT], rest[:, :]))
                    dve.tensor_tensor(bparts[:, 2 * QT:3 * QT], rest[:, :], bparts[:, 1 * QT:2 * QT],
                                      ALU.subtract).then_inc(s_bias_parts, 1)

                def flush(two):
                    weigh(two, QT - 1, 1, NC - 1)
                    for step in range(3):
                        scale_values(two, QT - 1, 1, step)
                    dve.wait_ge(s_output, QT * two.n + (QT + 2))
                    dve.wait_ge(s_output_stored, two.n + 1)
                    dve.tensor_copy(osb[:, :, :], ps[:, O_BANK:O_BANK + NO, 0:OS]).then_inc(s_output_taken, 1)

                steps(dve, pair, sums=sums, logs=logs, flush=flush)


def relative_attention(nc, nhb, dh, loads, rel_w, rel_h, v_dram, att_out, sum_out, bias_dram, ind, identb):
    SETS = (("qa", "ka"), ("qa", "kb"), ("qb", "kc"))
    SW = 384
    NSUB = 2
    CB = NSUB * SW
    NCB = L // CB
    NCA = L // SW
    BUFS = 4
    G = 128 // dh
    OW = L // G
    NO = OW // SW
    O_BANK, T_COL = 4, SW
    GZ = 4
    ZW = L // GZ // 2
    TPR = 6
    with Phase(nc, "at3") as ph:
        ops = {n: ph.sb(n, [128, 3, L], BF16) for n in loads}
        rel = ph.sb("rel", [128, 3, 2 * NBX, L], BF16)
        indt = ph.sb("ind", [128, L], BF16)
        v = ph.sb("v", [128, 3, QT, dh])
        idb = ph.sb("idb", [128, 128], BF16)
        w = ph.sb("w", [128, 2, L])
        acc = ph.sb("acc", [128, L])
        ones = ph.sb("ones", [128, 32])
        vs = ph.sb("vs", [128, 2, dh])
        nmax = ph.sb("nmax", [128, QT, NCA])
        nm = ph.sb("nm", [128, QT])
        rest = ph.sb("rest", [128, QT])
        bparts = ph.sb("bparts", [128, 128], BF16)
        bturned = ph.sb("bturned", [128, 128], BF16)
        osb = ph.sb("osb", [128, NO, SW])
        zsb = ph.sb("zsb", [128, 2, ZW])
        ps = ph.psum("ps", [128, 8, 512])
        psb = ps[:, :, :].bitcast(BF16)
        (s_scored, s_max_taken, s_link, s_bias_parts, s_turn, s_turned, s_bias_out, s_bias_row, s_keys_scored, s_keys_exped, s_acc, s_values, s_output, s_output_taken,
         s_zprod, s_zsb, s_stored, s_zstored, s_output_stored, s_zfree, s_bias_stored, s_id, s_begun, s_zero, s_moving) = (
             ph.sem(n) for n in (
                 "scoresA maxed link bparts turn turned biasout brow scoresB expB summed vcopied outprod osb "
                 "sumprod zsb stored zstored ofree zfree bfree id begun zero moving").split())
        s_ops = [ph.sem(f"ops{r}") for r in range(3)]
        n_loads = sum(len(x) for x in loads.values()) + 1 + 4 * NBX
        E0, O0 = 2 * QT * NCB, 3 * QT
        tps = psb[:, O_BANK, 2 * T_COL:2 * T_COL + 128]

        def st(buf):
            return ps[:, NSUB * buf:NSUB * buf + NSUB, 0:SW]

        with nc.Block() as block:

            @block.sync
            def _(sp):
                sp.sem_inc(s_output_stored, 1)
                sp.sem_inc(s_zfree, 1)
                sp.sem_inc(s_bias_stored, 1)
                sp.dma_start(idb[:, :], identb).then_inc(s_id, 16)
                sp.dma_start(indt[0:ind.shape[0], :], ind).then_inc(s_id, 16)

                def load(s, r):
                    for name, parts in loads.items():
                        for dram, part, n, at in parts:
                            src = dram[part].rearrange("(h r) n -> h r n", r=n)[s]
                            sp.dma_start(ops[name][at:at + n, r, :], src).then_inc(s_ops[r], 16)
                    for bx in range(NBX):
                        for half in range(2):
                            sp.dma_start(rel[0:REL_W, r, 2 * bx + half, :], rel_w[s, bx]).then_inc(s_ops[r], 16)
                            sp.dma_start(rel[REL_W:REL, r, 2 * bx + half, :], rel_h[s, half]).then_inc(s_ops[r], 16)
                    sp.dma_start(v[:, r, :, :], v_dram[s]).then_inc(s_ops[r], 16)

                def bias_row(h):
                    sp.wait_ge(s_turned, h.n + 1)
                    sp.dma_start(bias_dram, bturned[0:3 * QT, :]).then_inc(s_bias_out, 16)
                    sp.wait_ge(s_bias_out, 16 * h.n + 16)
                    sp.sem_inc(s_bias_stored, 1)
                    for g in range(2 * NBX):
                        sp.dma_start(rel[REL:REL + 3, h.buf, g, :], bias_dram.rearrange("(a t) w -> a (t w)", a=3))\
                          .then_inc(s_bias_row, 16)
                    sp.wait_ge(s_bias_row, 32 * NBX * h.n + 32 * NBX)

                def store(h):
                    sp.wait_ge(s_output_taken, h.n + 2)
                    dst = att_out.rearrange("(h d) (g n) -> h g d n", d=dh, g=G)[h.n]
                    for g in range(G):
                        sp.dma_start(dst[g], osb[g * dh:(g + 1) * dh, :, :].rearrange("p a b -> p (a b)"))\
                          .then_inc(s_stored, 16)
                    sp.wait_ge(s_stored, 16 * G * h.n + 16 * G)
                    sp.sem_inc(s_output_stored, 1)
                    sp.wait_ge(s_zsb, h.n + 3)
                    dst = sum_out.rearrange("h (g n) -> h g n", g=GZ)[h.n]
                    for g in range(GZ):
                        sp.dma_start(dst[g:g + 1], zsb[32 * g:32 * g + 1, :, :].rearrange("p a b -> p (a b)"))\
                          .then_inc(s_zstored, 16)
                    sp.wait_ge(s_zstored, 16 * GZ * h.n + 16 * GZ)
                    sp.sem_inc(s_zfree, 1)

                def first(h):
                    for r in range(3):
                        load(r, r)
                    bias_row(h)

                def step(h, before, rolled):
                    store(before)
                    bias_row(h)
                    if rolled:
                        load(before.n + 3, before.buf)

                in_heads(sp, nhb, first, step, store)

            @block.gpsimd
            def _(pool):
                pool.memset(ones[:, :], 1.0).then_inc(s_zero, 1)

                def values(h):
                    pool.wait_ge(s_ops[h.buf], 16 * n_loads * h.turn + 16 * n_loads)
                    pool.sem_inc(s_moving, 1)
                    with pool.Fori(0, NBX) as i:
                        for m in range(TPR):
                            pool.wait_ge(s_output, QT * h.n + TPR * i + (m - 1 + O0))
                            pool.tensor_copy(vs[:, m % 2, :], v[:, h.buf, NBX * m:NBX * (m + 1), :][:, i, :])\
                                .then_inc(s_values, 1)

                in_heads(pool, nhb, lambda h: None, lambda h, before, rolled: values(before), values)

            @block.tensor
            def _(pe):
                pe.sem_inc(s_output, O0)
                pe.sem_inc(s_zprod, 1)
                pe.wait_ge(s_id, 32)
                pe.wait_ge(s_zero, 2)

                def score(h):
                    pe.wait_ge(s_ops[h.buf], 16 * n_loads * h.turn + 16 * n_loads)
                    pe.wait_ge(s_keys_exped, NCB * QT * h.n + NCB * QT)
                    pe.wait_ge(s_zsb, h.n + 1)
                    pe.sem_inc(s_begun, 1)
                    with pe.Fori(0, QT // 2) as i:
                        for k in range(2):
                            def tile(ap):
                                return cols(ap, 128)[:, 2 * i + k, :]
                            for c in range(NCA):
                                m = NCA * k + c
                                out = ps[:, m % BUFS, 0:SW]
                                keys = slice(c * SW, (c + 1) * SW)
                                pe.wait_ge(s_max_taken, QT * NCA * h.n + 2 * NCA * i + (m + 1))
                                pe.matmul(out, tile(ops["qa"][:, h.buf, :]), ops["ka"][:, h.buf, keys], start=True,
                                          stop=False, skip_group_check=True)
                                pe.matmul(out, tile(ops["qa"][0:dh, h.buf, :]), ops["kb"][0:dh, h.buf, keys],
                                          start=False, stop=False, skip_group_check=True)
                                for bx in range(NBX):
                                    at = c * SW + bx * 128
                                    last = pe.matmul(out[:, bx * 128:(bx + 1) * 128],
                                                     tile(rel[0:REL, h.buf, 2 * bx + c // HALF, :]),
                                                     indt[0:REL, at:at + 128], start=False, stop=bx == NBX - 1,
                                                     skip_group_check=True)
                                last.then_inc(s_scored, 1)

                def keys(h, i, m):
                    def tile(ap):
                        return cols(ap, 128)[:, NBX * m:NBX * (m + 1), :][:, i, :]
                    half = m // HALF
                    for c in range(NCB):
                        b = NCB * m + c
                        pe.wait_ge(s_keys_exped, QT * NCB * h.n + TPR * NCB * i + (b + E0 - 1))
                        for sub in range(NSUB):
                            out = ps[:, NSUB * (b % 2) + sub, 0:SW]
                            at = c * CB + sub * SW
                            for n, (q, kk) in enumerate(SETS):
                                pe.matmul(out, tile(ops[kk][:, h.buf, :]), ops[q][:, h.buf, at:at + SW],
                                          start=n == 0, stop=False, skip_group_check=True)
                            last = pe.matmul(out, tile(indt[0:REL + 3, :]),
                                             rel[0:REL + 3, h.buf, half:2 * NBX:2, at:at + SW][:, i, :],
                                             start=False, stop=True, skip_group_check=True)
                        last.then_inc(s_keys_scored, 1)

                def values(n_t, k, start, stop):
                    pe.wait_ge(s_values, n_t + 1)
                    pe.wait_ge(s_keys_exped, NCB * n_t + (NCB + E0))
                    for o in range(NO):
                        for g in range(G):
                            last = pe.matmul(ps[g * dh:(g + 1) * dh, O_BANK + o, 0:SW], vs[:, k, :],
                                             w[:, k, g * OW + o * SW:g * OW + (o + 1) * SW],
                                             start=start, stop=stop, skip_group_check=True)
                    last.then_inc(s_output, 1)

                def attend(h, scored):
                    pe.wait_ge(s_max_taken, QT * NCA * scored + BUFS)
                    pe.wait_ge(s_bias_row, 32 * NBX * h.n + 32 * NBX)
                    t0 = QT * h.n
                    for m in range(TPR):
                        keys(h, 0, m)
                        if m == 1:
                            pe.wait_ge(s_output_taken, h.n + 1)
                        if m:
                            values(t0 + (m - 1), (m - 1) % 2, m == 1, False)
                    with pe.Fori(1, NBX) as i:
                        for m in range(TPR):
                            keys(h, i, m)
                            values(t0 + TPR * i + (m - 1), (m - 1) % 2, False, False)
                    values(t0 + (QT - 1), 1, False, True)
                    pe.wait_ge(s_acc, t0 + (QT + 2))
                    for o in range(2):
                        for g in range(GZ):
                            last = pe.matmul(ps[32 * g:32 * g + 32, o, 0:ZW], ones[:, :],
                                             acc[:, (2 * g + o) * ZW:(2 * g + o + 1) * ZW],
                                             start=True, stop=True, skip_group_check=True)
                    last.then_inc(s_zprod, 1)

                def turn_bias(h):
                    pe.wait_ge(s_bias_parts, h.n + 1)
                    pe.wait_ge(s_output_taken, h.n + 1)
                    pe.transpose(tps, bparts[:, :], idb[:, :]).then_inc(s_turn, 1)

                def first(h):
                    score(h)
                    turn_bias(h)

                def step(h, before, rolled):
                    score(h)
                    attend(before, h.n + 1)
                    turn_bias(h)

                in_heads(pe, nhb, first, step, lambda h: attend(h, nhb))

            @block.scalar
            def _(act):
                act.sem_inc(s_keys_exped, E0)
                act.sem_inc(s_zsb, 2)

                def attend(h):
                    with act.Fori(0, QT // 2) as i:
                        for k in range(2):
                            n_t = QT * h.n + 2 * i + k
                            act.wait_ge(s_output, n_t + (O0 - 1))
                            act.wait_ge(s_acc, n_t + 1)
                            for c in range(NCB):
                                m = NCB * k + c
                                act.wait_ge(s_keys_scored, QT * NCB * h.n + 2 * NCB * i + (m + 1))
                                act.activation(w[:, k, c * CB:(c + 1) * CB].rearrange("p (a b) -> p a b", b=SW),
                                               st(m % 2), ACT.Exp).then_inc(s_keys_exped, 1)
                    act.wait_ge(s_zprod, h.n + 2)
                    act.wait_ge(s_zfree, h.n + 1)
                    act.activation(zsb[:, :, :], ps[:, 0:2, 0:ZW], ACT.Copy).then_inc(s_zsb, 1)

                in_heads(act, nhb, lambda h: None, lambda h, before, rolled: attend(before), attend)

            @block.vector
            def _(dve):
                dve.sem_inc(s_max_taken, BUFS)
                dve.sem_inc(s_output_taken, 1)
                dve.sem_inc(s_acc, 2)
                dve.memset(bparts[:, :], 0.0).then_inc(s_zero, 1)
                dve.wait_ge(s_zero, 2)
                N_LINK = 4

                def score(h):
                    with dve.Fori(0, QT // 2) as i:
                        for k in range(2):
                            for c in range(NCA):
                                m = NCA * k + c
                                dve.wait_ge(s_scored, QT * NCA * h.n + 2 * NCA * i + (m + 1))
                                dve.tensor_reduce(nmax[:, 2 * i + k, c:c + 1], ps[:, m % BUFS, 0:SW], AX.X, ALU.max,
                                                  negate=True).then_inc(s_max_taken, 1)

                    def link(n, ins):
                        ins.then_inc(s_link, 1)
                        dve.wait_ge(s_link, N_LINK * h.n + n)

                    dve.wait_ge(s_max_taken, QT * NCA * h.n + (QT * NCA + BUFS))
                    link(1, dve.tensor_reduce(nm[:, :], nmax[:, :, :], AX.X, ALU.min))
                    link(2, dve.tensor_copy(bparts[:, 0 * QT:1 * QT], nm[:, :]))
                    link(3, dve.tensor_tensor(rest[:, :], nm[:, :], bparts[:, 0 * QT:1 * QT], ALU.subtract))
                    link(4, dve.tensor_copy(bparts[:, 1 * QT:2 * QT], rest[:, :]))
                    dve.tensor_tensor(bparts[:, 2 * QT:3 * QT], rest[:, :], bparts[:, 1 * QT:2 * QT],
                                      ALU.subtract).then_inc(s_bias_parts, 1)

                def attend(h):
                    t0 = QT * h.n

                    def add(n_t, k, opening):
                        dve.wait_ge(s_keys_exped, NCB * n_t + (NCB + E0))
                        if opening:
                            dve.wait_ge(s_zprod, h.n + 1)
                            dve.tensor_copy(acc[:, :], w[:, k, :]).then_inc(s_acc, 1)
                        else:
                            dve.wait_ge(s_acc, n_t + 2)
                            dve.tensor_tensor(acc[:, :], acc[:, :], w[:, k, :], ALU.add).then_inc(s_acc, 1)

                    add(t0, 0, True)
                    add(t0 + 1, 1, False)
                    with dve.Fori(1, QT // 2) as i:
                        for k in range(2):
                            add(t0 + 2 * i + k, k, False)
                    dve.wait_ge(s_output, QT * h.n + (QT + O0))
                    dve.wait_ge(s_output_stored, h.n + 1)
                    dve.tensor_copy(osb[:, :, :], ps[:, O_BANK:O_BANK + NO, 0:SW]).then_inc(s_output_taken, 1)

                def turned(h):
                    dve.wait_ge(s_turn, h.n + 1)
                    dve.wait_ge(s_bias_stored, h.n + 1)
                    dve.tensor_copy(bturned[:, :], tps).then_inc(s_turned, 1)

                def first(h):
                    score(h)
                    turned(h)

                def step(h, before, rolled):
                    score(h)
                    attend(before)
                    turned(h)

                in_heads(dve, nhb, first, step, attend)


def network(nc, a, out):
    def dram(name, shape, dt=F32):
        return nc.dram_tensor(name, shape, dt).ap()

    def pieces(src, order, n):
        return [(src, p, n, n * i) for i, p in enumerate(order)]

    x0, x1, x2, x3, x4, xn = (dram(n, [C, T]) for n in "x0 x1 x2 x3 x4 xn".split())
    split = dram("split", [3, 2 * B * C, L], BF16)
    q, k = split[:, 0:B * C, :], split[:, B * C:, :]
    plain = dram("plain", [2 * B * C, L])
    attended = dram("attended", [B * C, L])
    to_channels(nc, a["x"], x0, a["ident"])

    u, y = dram("u", [K * KINDS, 128, L]), dram("y", [K * KINDS, 128, L])
    group_norm(nc, "0", x0, xn, a["group_mean"])
    conv_inputs(nc, xn, a["w_in"], a["params0"], a["ident"], u)
    selective_scan(nc, u, a["w_x"], a["w_dt"], a["params"], a["one_hot"], a["ident"], y)
    norm_project(nc, y, a["norm_w"], a["norm_b"], a["w_out"], x0, x1)

    v1 = dram("v1", [B * NH1, 128, QT, D1])
    g = dram("g", [3, B * NH1 * GP, L], BF16)
    turned1 = dram("turned1", [3 * QT, 128], BF16)
    group_norm(nc, "1", x1, xn, a["group_mean"])
    project_split(nc, "1", xn, a["w_qkv1"], a["scale1"], a["bias1"], split, plain)
    values(nc, "1", xn, a["w_qkv1"], a["zeros"], v1, NH1, D1)
    group_weights(nc, plain[0:B * C, :], a["gaussians"], a["t_param"], g, a["ident"])
    gated_attention(nc, B * NH1, D1,
                    dict(qa=pieces(q, (0, 1, 2), D1), qb=pieces(q, (0, 1, 0), D1),
                         ka=pieces(k, (0, 0, 0), D1), kb=pieces(k, (1, 1, 2), D1),
                         gi=pieces(g, (0, 1, 2, 0, 1, 0), GP), gj=pieces(g, (0, 0, 0, 1, 1, 2), GP)),
                    [("qa", "ka", 3 * D1), ("qb", "kb", 3 * D1)], ("gi", "gj", 6 * GP), v1, attended, turned1,
                    a["ident_b"])
    project_out(nc, "1", attended, a["w_proj1"], a["zeros"], x1, x2)

    group_norm(nc, "2", x2, xn, a["group_mean"])
    box_similarity(nc, x2, xn, x3, a["band"], a["window"])

    v3 = dram("v3", [B * NH3, 128, QT, D3])
    rel_w, rel_h = dram("rel_w", [B * NH3, NBX, REL_W, L], BF16), dram("rel_h", [B * NH3, 2, REL_H, L], BF16)
    sums, inverse = dram("sums", [B * NH3, L]), dram("inverse", [B * NH3, L])
    turned3 = dram("turned3", [3 * QT, 128], BF16)
    group_norm(nc, "3", x3, xn, a["group_mean"], blocks=True)
    project_split(nc, "3", xn, a["w_qkv3"], a["scale3"], a["bias3"], split, plain)
    values(nc, "3", xn, a["w_qkv3"], a["bias_v3"], v3, NH3, D3)
    relative(nc, plain[0:B * C, :], a["rel_table"], rel_w, rel_h)
    relative_attention(nc, B * NH3, D3,
                       dict(qa=pieces(q, (0, 1), D3), qb=pieces(q, (2, 0), D3), ka=pieces(k, (0, 0), D3),
                            kb=pieces(k, (1, 1), D3), kc=pieces(k, (0, 2), D3)),
                       rel_w, rel_h, v3, attended, sums, turned3, a["indicator"], a["ident_b"])
    project_out(nc, "3", attended, a["w_proj3"], a["bias_proj3"], x3, x4, sums, inverse)

    to_tokens(nc, x4, out, a["ident"])


def layouts(inputs):
    import numpy as np
    bfloat16 = mybir.dt.np(BF16)
    f = np.float32
    i = {n: np.asarray(z) for n, z in inputs.items()}
    a = dict(x=i["x"].reshape(T, C))

    group = np.arange(C) // GN_GROUP
    a["group_mean"] = (group[:, None] == group[None]).astype(f) / GN_GROUP
    a["ident"] = np.eye(128, dtype=f)
    a["ident_b"] = a["ident"].astype(bfloat16)
    a["zeros"] = np.zeros(C, f)
    chan = np.arange(C)
    lo = WIN_C // 2
    a["band"] = ((chan[:, None] >= chan[None] - lo) & (chan[:, None] < chan[None] - lo + WIN_C)).astype(f)
    count = np.array([sum(0 <= w + s < W for s in range(-(WIN_W // 2), WIN_W // 2 + 1)) for w in range(W)], f)
    a["window"] = np.tile(count, 8)

    a["w_in"] = i["L0_conv_in_proj_w"].reshape(K, D_IN, CT, 128).transpose(3, 0, 2, 1)
    par = np.concatenate([i["L0_conv_conv_w"].reshape(CI, 9), i["L0_conv_conv_b"][:, None], i["L0_conv_Ds"][:, None],
                          i["L0_conv_dt_projs_bias"].reshape(CI, 1), i["L0_conv_A_logs"]], 1).reshape(K, D_IN, NPAR)
    a["params"] = np.stack([par[:, :128], np.concatenate([par[:, 128:], par[:, 128:]], 1)], 2)
    a["params0"] = a["params"].transpose(1, 0, 2, 3)
    kinds = [[(0, slice(0, 128), slice(0, 128))], [(1, slice(0, 128), slice(0, 128))],
             [(0, slice(0, LEFT), slice(128, D_IN)), (1, slice(LEFT, 128), slice(128, D_IN))]]
    w_x = np.zeros((K, 128, KINDS, 96), f)
    w_dt = np.zeros((K, B * R, KINDS, 128), f)
    one_hot = np.zeros((3, B, NS, KINDS, NS, 128), f)
    xw, dw = i["L0_conv_x_proj_weight"].transpose(0, 2, 1), i["L0_conv_dt_projs_weight"].transpose(0, 2, 1)
    for t, parts in enumerate(kinds):
        for b, to, of in parts:
            w_x[:, to, t, NS * b:NS * (b + 1)] = xw[:, of, R:R + NS]
            w_x[:, to, t, NS * (B + b):NS * (B + b + 1)] = xw[:, of, R + NS:]
            w_x[:, to, t, 2 * B * NS + R * b:2 * B * NS + R * (b + 1)] = xw[:, of, :R]
            w_dt[:, R * b:R * (b + 1), t, to] = dw[:, :, of]
            for s in range(NS):
                one_hot[:, b, s, t, s, to] = 1
    a["w_x"], a["w_dt"] = w_x, w_dt
    a["one_hot"] = one_hot.reshape(3 * B * NS, KINDS * NS, 128).astype(bfloat16)

    def by_tiles(z):
        z = z.reshape(K, D_IN, -1)
        return np.stack([z[k, :128] for k in range(K)] + [np.concatenate([z[k, 128:], z[k + 1, 128:]])
                                                          for k in range(0, K, 2)], 1)

    a["norm_w"] = by_tiles(i["L0_conv_out_norm_w"])[:, :, 0]
    a["norm_b"] = by_tiles(i["L0_conv_out_norm_b"])[:, :, 0]
    a["w_out"] = by_tiles(i["L0_conv_out_proj_w"].T)

    def affine(scale):
        s = np.ones((128, 2 * CT), f)
        s[:, CT:] = scale
        return s

    a["w_qkv1"], a["w_proj1"], a["t_param"] = i["L1_conv_W_qkv"], i["L1_conv_W_proj"], i["L1_conv_t_param"]
    a["scale1"], a["bias1"] = affine(D1 ** -0.5), np.zeros((128, 2 * CT), f)
    gp = i["L1_conv_gp_w"].reshape(NH1, GP, D1)
    a["gaussians"] = np.zeros((128, CT, 4 * GP), f)
    for h in range(NH1):
        r = h % 4
        a["gaussians"][D1 * r:D1 * (r + 1), h // 4, GP * r:GP * (r + 1)] = gp[h].T

    a["w_qkv3"], a["w_proj3"], a["bias_proj3"] = i["L3_conv_qkv_w"], i["L3_conv_proj_w"], i["L3_conv_proj_b"]
    a["scale3"] = affine(D3 ** -0.5)
    a["bias3"] = i["L3_conv_qkv_b"][:2 * C].reshape(2 * CT, 128).T
    a["bias_v3"] = i["L3_conv_qkv_b"][2 * C:]
    rows = np.minimum(2 * H - 2 - np.arange(2 * H - 1), i["L3_conv_rel_pos_h"].shape[0] - 1)
    a["rel_table"] = np.stack([i["L3_conv_rel_pos_h"][rows].T, i["L3_conv_rel_pos_w"][rows].T], 1)
    indicator = np.ones((REL + 3, L), f)
    token = np.arange(L)
    row, column = token // BROW * BY + token % 128 // BX, token % BX
    n = HALF * BY
    for part in range(3):
        indicator[BX * part:BX * (part + 1)] = column == np.arange(BX)[:, None]
        indicator[REL_W + n * part:REL_W + n * (part + 1)] = row % n == np.arange(n)[:, None]
    a["indicator"] = indicator.astype(bfloat16)
    return {n: np.ascontiguousarray(z) for n, z in a.items()}


def kernel(**inputs):
    import numpy as np
    import concourse.bacc as bacc
    from concourse.bass_utils import run_bass_kernel_spmd

    nc = bacc.Bacc("TRN2", target_bir_lowering=False, num_devices=1)
    arrays = {f"in_{n}": z for n, z in layouts(inputs).items()}
    args = {n[3:]: nc.dram_tensor(n, z.shape, mybir.dt.from_np(z.dtype), kind="ExternalInput").ap()
            for n, z in arrays.items()}
    out = nc.dram_tensor("out", (T, C), F32, kind="ExternalOutput").ap()
    network(nc, args, out)
    r = run_bass_kernel_spmd(nc, [arrays], core_ids=[0])
    return r.results[0]["out"].reshape(B, H, W, C)
```
